# Optimizing a Trainium2 kernel written in Bass

```python
import numpy as np
import jax
import jax.numpy as jnp

def _softmax(x, axis=-1):
    return jax.nn.softmax(x, axis=axis)

def _gelu(x):
    return jax.nn.gelu(x, approximate=True)

def _silu(x):
    return jax.nn.silu(x)

def _sigmoid(x):
    return jax.nn.sigmoid(x)

def _layernorm(x, axis=-1, eps=1e-05):
    m = jnp.mean(x, axis=axis, keepdims=True)
    v = jnp.var(x, axis=axis, keepdims=True)
    return (x - m) / jnp.sqrt(v + eps)

def _scatter_add(tgt, idx, src, axis=0):
    return tgt.at[idx].add(src)

def _segment_sum(src, seg, n):
    return jax.ops.segment_sum(src, seg, n)
kernel_name = 'mk_gnn_resnorm_d2_gnn_r8_830ef0'

def setup_inputs(seed: int=0):
    np.random.seed(seed)
    _w = jnp.asarray

    def _rec_inputs():
        import jax
        import jax.numpy as jnp
        _gk = jax.random.key(seed)
        x = -0.0005121 + 1.001 * jax.random.normal(jax.random.fold_in(_gk, 1), (6250, 64), jnp.float32)
        src = jax.random.randint(jax.random.fold_in(_gk, 2), (200000,), 0, 6250, jnp.int32)
        dst = jax.random.randint(jax.random.fold_in(_gk, 3), (200000,), 0, 6250, jnp.int32)
        _o = jnp.argsort(dst, stable=True)
        src = src[_o]
        dst = dst[_o]
        edge_type_5 = jax.random.randint(jax.random.fold_in(_gk, 13), (200000,), 0, 5, jnp.int32)
        edge_weight = jax.random.uniform(jax.random.fold_in(_gk, 14), (200000,), jnp.float32, 0.0, 1)
        edge_weight_n2 = jax.random.uniform(jax.random.fold_in(_gk, 15), (200000,), jnp.float32, 0.0, 1)
        return (x, src, dst, edge_type_5, edge_weight, edge_weight_n2)
    x, src, dst, edge_type_5, edge_weight, edge_weight_n2 = _rec_inputs()

    def _L0_gnn_setup():
        import jax, jax.numpy as jnp
        import numpy as np
        N_NODES = 6250
        N_EDGES = 100000
        IN_DIM = 64
        HEADS = 8
        HID = IN_DIM // HEADS
        OUT_DIM = 64
        N_ETYPES = 5
        NEG_SLOPE = 0.2

        def typed_linear(x, W, etype):
            out = jnp.zeros((x.shape[0], W.shape[2]), dtype=x.dtype)
            for t in range(W.shape[0]):
                out = out + jnp.where((etype == t)[:, None], x @ W[t], 0.0)
            return out

        def hetsann_conv(feat, src, dst, etype, edge_weight, W, Al, Ar, heads, out_dim, n_nodes, Wres=None, bres=None, use_elu=False):
            h = typed_linear(feat[src], W, etype)
            h3 = h.reshape(-1, heads, out_dim)
            h_l = typed_linear(h, Al, etype).reshape(-1, heads, out_dim).sum(-1)
            h_r = typed_linear(h, Ar, etype).reshape(-1, heads, out_dim).sum(-1)
            att = jax.nn.sigmoid(jax.nn.leaky_relu(h_l + h_r, NEG_SLOPE))
            att = att * edge_weight[:, None]
            msg = h3.transpose(0, 2, 1) * att[:, None, :]
            agg = jax.ops.segment_sum(msg, dst, num_segments=n_nodes)
            out = agg.reshape(n_nodes, out_dim * heads)
            if Wres is not None:
                out = out + feat @ Wres + bres
            if use_elu:
                out = jax.nn.elu(out)
            return out
        key = jax.random.key(seed)
        ks = jax.random.split(key, 12)
        s = 1.0 / np.sqrt(IN_DIM)
        inp = {'feat': jax.random.normal(ks[0], (N_NODES, IN_DIM), dtype=jnp.float32), 'edge_weight': jax.random.uniform(ks[1], (N_EDGES,), dtype=jnp.float32), 'src': jax.random.randint(ks[2], (N_EDGES,), 0, N_NODES), 'dst': jax.random.randint(ks[3], (N_EDGES,), 0, N_NODES), 'etype': jax.random.randint(ks[4], (N_EDGES,), 0, N_ETYPES), 'W0': jax.random.normal(ks[5], (N_ETYPES, IN_DIM, HEADS * HID), dtype=jnp.float32) * s, 'Al0': jax.random.normal(ks[6], (N_ETYPES, HEADS * HID, HEADS * HID), dtype=jnp.float32) * s, 'Ar0': jax.random.normal(ks[7], (N_ETYPES, HEADS * HID, HEADS * HID), dtype=jnp.float32) * s, 'W1': jax.random.normal(ks[8], (N_ETYPES, HEADS * HID, OUT_DIM), dtype=jnp.float32) * s, 'Al1': jax.random.normal(ks[9], (N_ETYPES, OUT_DIM, OUT_DIM), dtype=jnp.float32) * s, 'Ar1': jax.random.normal(ks[10], (N_ETYPES, OUT_DIM, OUT_DIM), dtype=jnp.float32) * s, 'Wres': jax.random.normal(ks[11], (HEADS * HID, OUT_DIM), dtype=jnp.float32) * s, 'bres': jnp.zeros((OUT_DIM,), dtype=jnp.float32)}
        return inp
    _L0_gnn_all = _L0_gnn_setup()
    _L0_gnn_in = {k: v for k, v in _L0_gnn_all.items() if k in ('W0', 'Al0', 'Ar0', 'W1', 'Al1', 'Ar1', 'Wres', 'bres')}
    del _L0_gnn_all

    def _L1_gnn_setup():
        import jax, jax.numpy as jnp
        import numpy as np
        N, E, D_IN, D_OUT = (8192, 131072, 64, 64)
        EPS = 1e-08
        key = jax.random.key(seed)
        ks = jax.random.split(key, 8)
        h = jax.random.normal(ks[0], (N, D_IN), dtype=jnp.float32)
        edge_index = jax.random.randint(ks[1], (2, E), 0, N, dtype=jnp.int64 if jax.config.jax_enable_x64 else jnp.int32)
        adj_v = jax.random.uniform(ks[2], (E,), dtype=jnp.float32)
        deg_v = jax.random.uniform(ks[3], (E,), dtype=jnp.float32)
        W = jax.random.normal(ks[4], (D_IN, D_OUT), dtype=jnp.float32) / np.sqrt(D_IN)
        b = jax.random.normal(ks[5], (D_OUT,), dtype=jnp.float32) * 0.01
        deg_coeff = jnp.array([0.5, 0.0], dtype=jnp.float32)
        coeff_param = jnp.zeros((3,), dtype=jnp.float32)
        scale_param = 2.0 * jnp.ones((1,), dtype=jnp.float32)
        return {'h': h, 'edge_index': edge_index, 'adj_v': adj_v, 'deg_v': deg_v, 'W': W, 'b': b, 'deg_coeff': deg_coeff, 'coeff_param': coeff_param, 'scale_param': scale_param}
    _L1_gnn_all = _L1_gnn_setup()
    _L1_gnn_in = {k: v for k, v in _L1_gnn_all.items() if k in ('W', 'b', 'deg_coeff', 'coeff_param', 'scale_param')}
    del _L1_gnn_all
    return {'x': x, 'src': src, 'dst': dst, 'edge_type_5': edge_type_5, 'edge_weight': edge_weight, 'edge_weight_n2': edge_weight_n2, 'L0_gnn_W0': _L0_gnn_in['W0'], 'L0_gnn_Al0': _L0_gnn_in['Al0'], 'L0_gnn_Ar0': _L0_gnn_in['Ar0'], 'L0_gnn_W1': _L0_gnn_in['W1'], 'L0_gnn_Al1': _L0_gnn_in['Al1'], 'L0_gnn_Ar1': _L0_gnn_in['Ar1'], 'L0_gnn_Wres': _L0_gnn_in['Wres'], 'L0_gnn_bres': _L0_gnn_in['bres'], 'L1_gnn_W': _L1_gnn_in['W'], 'L1_gnn_b': _L1_gnn_in['b'], 'L1_gnn_deg_coeff': _L1_gnn_in['deg_coeff'], 'L1_gnn_coeff_param': _L1_gnn_in['coeff_param'], 'L1_gnn_scale_param': _L1_gnn_in['scale_param']}

def reference(x, src, dst, edge_type_5, edge_weight, edge_weight_n2, L0_gnn_W0, L0_gnn_Al0, L0_gnn_Ar0, L0_gnn_W1, L0_gnn_Al1, L0_gnn_Ar1, L0_gnn_Wres, L0_gnn_bres, L1_gnn_W, L1_gnn_b, L1_gnn_deg_coeff, L1_gnn_coeff_param, L1_gnn_scale_param):
    import jax
    import jax.numpy as jnp

    def _L0_gnn_ref(feat, edge_weight, src, dst, etype, W0, Al0, Ar0, W1, Al1, Ar1, Wres, bres):
        import jax, jax.numpy as jnp
        import numpy as np
        N_NODES = 6250
        N_EDGES = 100000
        IN_DIM = 64
        HEADS = 8
        HID = IN_DIM // HEADS
        OUT_DIM = 64
        N_ETYPES = 5
        NEG_SLOPE = 0.2

        def typed_linear(x, W, etype):
            out = jnp.zeros((x.shape[0], W.shape[2]), dtype=x.dtype)
            for t in range(W.shape[0]):
                out = out + jnp.where((etype == t)[:, None], x @ W[t], 0.0)
            return out

        def hetsann_conv(feat, src, dst, etype, edge_weight, W, Al, Ar, heads, out_dim, n_nodes, Wres=None, bres=None, use_elu=False):
            h = typed_linear(feat[src], W, etype)
            h3 = h.reshape(-1, heads, out_dim)
            h_l = typed_linear(h, Al, etype).reshape(-1, heads, out_dim).sum(-1)
            h_r = typed_linear(h, Ar, etype).reshape(-1, heads, out_dim).sum(-1)
            att = jax.nn.sigmoid(jax.nn.leaky_relu(h_l + h_r, NEG_SLOPE))
            att = att * edge_weight[:, None]
            msg = h3.transpose(0, 2, 1) * att[:, None, :]
            agg = jax.ops.segment_sum(msg, dst, num_segments=n_nodes)
            out = agg.reshape(n_nodes, out_dim * heads)
            if Wres is not None:
                out = out + feat @ Wres + bres
            if use_elu:
                out = jax.nn.elu(out)
            return out
        h = hetsann_conv(feat, src, dst, etype, edge_weight, W0, Al0, Ar0, heads=HEADS, out_dim=HID, n_nodes=N_NODES, use_elu=True)
        out = hetsann_conv(h, src, dst, etype, edge_weight, W1, Al1, Ar1, heads=1, out_dim=OUT_DIM, n_nodes=N_NODES, Wres=Wres, bres=bres, use_elu=False)
        return out

    def _L1_gnn_ref(h, edge_index, adj_v, deg_v, W, b, deg_coeff, coeff_param, scale_param):
        import jax, jax.numpy as jnp
        import numpy as np
        N, E, D_IN, D_OUT = (8192, 131072, 64, 64)
        EPS = 1e-08
        n_nodes = h.shape[0]
        Wh = h @ W + b
        row, col = (edge_index[0], edge_index[1])
        sc = jax.nn.softplus(deg_coeff[0] * deg_v + deg_coeff[1])
        Wr = Wh[row]
        Wc = Wh[col]
        dot = jnp.sum(Wr * Wc, axis=-1)
        nr = jnp.sqrt(jnp.sum(Wr * Wr, axis=-1))
        nc = jnp.sqrt(jnp.sum(Wc * Wc, axis=-1))
        sim = dot / jnp.maximum(nr * nc, EPS)
        sim_pos = jax.nn.relu(sim)
        sim_neg = -jax.nn.relu(-sim)
        no_diag = (row != col).astype(Wh.dtype)
        base = adj_v * sc * no_diag
        prop_pos = jax.ops.segment_sum((base * sim_pos)[:, None] * Wc, row, num_segments=n_nodes)
        prop_neg = jax.ops.segment_sum((base * sim_neg)[:, None] * Wc, row, num_segments=n_nodes)
        coeff = jax.nn.softmax(coeff_param)
        scale = jax.nn.softplus(scale_param)
        return scale * (coeff[0] * prop_pos + coeff[1] * prop_neg + coeff[2] * Wh)
    edge_index = jnp.stack([src, dst])
    x = _layernorm(x + _L0_gnn_ref(x, edge_weight, src, dst, edge_type_5, L0_gnn_W0, L0_gnn_Al0, L0_gnn_Ar0, L0_gnn_W1, L0_gnn_Al1, L0_gnn_Ar1, L0_gnn_Wres, L0_gnn_bres), axis=-1)
    x = _layernorm(x + _L1_gnn_ref(x, edge_index, edge_weight, edge_weight_n2, L1_gnn_W, L1_gnn_b, L1_gnn_deg_coeff, L1_gnn_coeff_param, L1_gnn_scale_param), axis=-1)
    return x

_drawn_inputs = setup_inputs


def setup_inputs(seed=0):
    import zlib

    import numpy as np

    out = dict(_drawn_inputs(seed))
    spreads = {'L0_gnn_bres': (0.0, 0.1), 'L1_gnn_coeff_param': (0.0, 0.286)}
    factors = {'edge_weight_n2': 3.015, 'L1_gnn_b': 3.774}
    for name, (base, spread) in spreads.items():
        noise = np.random.default_rng([zlib.crc32(name.encode()), seed]).standard_normal(out[name].shape)
        drawn = base * np.exp(spread * noise) if base else spread * noise
        out[name] = jnp.asarray(drawn.astype(out[name].dtype))
    for name, factor in factors.items():
        out[name] = (out[name] * factor).astype(out[name].dtype)
    return out
```

```python
from contextlib import ExitStack

import concourse.bass as bass
from concourse import mybir

F32 = mybir.dt.float32
I32 = mybir.dt.int32
ALU = mybir.AluOpType
ACT = mybir.ActivationFunctionType
AX = mybir.AxisListType

P = 128
F = 64
T = 5
HEADS = 8
HID = F // HEADS
SLOPE = 0.2
EPS_LN = 1e-5
EPS_SIM = 1e-8

NODES = 6250
NT = -(-NODES // P)
NPAD = NT * P
LAST = NODES - (NT - 1) * P
EDGES = 200000
ROWS, ROWLEN = 98, 2048
ET = ROWS * ROWLEN // P
FULLROWS = EDGES // ROWLEN
TAIL = EDGES - FULLROWS * ROWLEN
JT = ROWLEN // P
PAD_SRC = NPAD - 1
PAD_DST = NODES - 1

BT = 8
NB = ET // BT
TAB = NPAD + P
CH = 7
NCH = NT // CH
A_IDX, A_W, A_DST, A_SRC, A_BASE = range(5)
NA = 5


def take(eng, sem, n=1):
    eng.wait_ge(sem, n).then_inc(sem, -n)


def build(nc, A, out):
    ctx = ExitStack()
    with ctx:
        names = iter(range(10000))

        def sem(name):
            return ctx.enter_context(nc.semaphore(name))

        def sb(name, shape, dt=F32, c=ctx):
            return c.enter_context(nc.sbuf_tensor(name, shape, dt))

        def psum(name, shape, c=ctx):
            return c.enter_context(nc.psum_tensor(name, shape, F32))

        ident = sb("ident", [P, P])
        lower = sb("lower", [P, P])
        iota_p = sb("iota_p", [P, 1])
        edge = sb("edge", [P, NA, ET])
        x_sb = sb("x_sb", [P, NT, F])
        skip = sb("skip", [P, NT, F])
        acc = sb("acc", [P, NT, F])
        w0 = sb("w0", [F, T * F + T * HEADS])
        w1 = sb("w1", [F, T * F + T + F])
        w2 = sb("w2", [F, F])
        bres = sb("bres", [P, F])
        b2 = sb("b2", [P, F])
        deg = sb("deg", [P, 2])
        coeff = sb("coeff", [P, 4])
        mom = sb("mom", [P, 4, NT])
        nbuf = [sb(f"nbuf{i}", [P, NT, F]) for i in range(2)]

        tab_l = [nc.dram_tensor(f"messages{l}", [NPAD * T, F], F32) for l in range(2)]
        tab_g = nc.dram_tensor("wh_norm", [NPAD, F + 1], F32)
        sums = [[nc.dram_tensor(f"sums{l}_{k}", [TAB, F], F32) for k in range(BT)] for l in range(3)]

        with ExitStack() as s1, nc.Block() as block:
            raw_i = [sb(f"raw_i{k}", [P, ROWLEN], I32, s1) for k in range(2)]
            raw_t = sb("raw_t", [P, ROWLEN], I32, s1)
            row = sb("row", [P, NA, ROWLEN], F32, s1)
            turn = sb("turn", [P, 2, NA, P], F32, s1)
            wload = sb("wload", [F, T, F], F32, s1)
            al = [sb(f"al{l}", [F, T, F], F32, s1) for l in range(2)]
            ar = [sb(f"ar{l}", [F, T, F], F32, s1) for l in range(2)]
            asum = [sb("asum0", [F, T, HEADS], F32, s1), sb("asum1", [F, T], F32, s1)]
            wt = [sb(f"wt{l}", [F, T, F], F32, s1) for l in range(2)]
            cin = sb("cin", [P, 4], F32, s1)
            csm = sb("csm", [P, 8], F32, s1)
            zeros = sb("zeros", [P, TAB // P * F], F32, s1)
            ps_turn = [psum(f"ps_turn{k}", [P, 512], s1) for k in range(2)]
            ps_w = [psum(f"ps_w{k}", [P, 512], s1) for k in range(4)]
            s_pad, s_x, s_rows, s_wts, s_small = sem("s_pad"), sem("s_x"), sem("s_rows"), sem("s_wts"), sem("s_small")
            s_zero, s_zeroed = sem("s_zero"), sem("s_zeroed")
            s_id, s_idm = sem("s_id"), sem("s_idm")
            v, a = sem("v_chain"), sem("a_chain")
            s_z, s_sp, s_rowready = sem("s_z"), sem("s_sp"), sem("s_rowready")
            s_turn_in = [sem(f"s_turn_in{k}") for k in range(2)]
            s_turn_free = [sem(f"s_turn_free{k}") for k in range(2)]
            s_turned = [sem(f"s_turned{k}") for k in range(2)]
            s_turned_free = [sem(f"s_turned_free{k}") for k in range(2)]
            s_wt, s_wtc, s_asum, s_wa, s_csm = sem("s_wt"), sem("s_wtc"), sem("s_asum"), sem("s_wa"), sem("s_csm")

            @block.sync
            def _(sp):
                sp.wait_ge(s_pad, 6)
                for dst, src in ((raw_i[0], A["src"]), (raw_i[1], A["dst"]), (raw_t, A["edge_type_5"]),
                                 (row[:, A_W, :], A["edge_weight"]), (row[:, A_BASE, :], A["edge_weight_n2"])):
                    sp.dma_start(dst[0:FULLROWS, :], src[0:FULLROWS * ROWLEN].rearrange("(p n) -> p n", n=ROWLEN)).then_inc(s_rows, 16)
                    sp.dma_start(dst[FULLROWS:ROWS, 0:TAIL], src[FULLROWS * ROWLEN:EDGES].rearrange("(p n) -> p n", p=1)).then_inc(s_rows, 16)
                sp.dma_start(x_sb[:, 0:NT - 1, :], A["x"][0:(NT - 1) * P, :].rearrange("(i p) f -> p i f", p=P)).then_inc(s_x, 16)
                sp.dma_start(x_sb[0:LAST, NT - 1, :], A["x"][(NT - 1) * P:NODES, :]).then_inc(s_x, 16)
                sp.wait_ge(s_zero, 1)
                for layer in sums:
                    for t in layer:
                        sp.dma_start(t.ap().rearrange("(p n) f -> p (n f)", p=P), zeros[:, :]).then_inc(s_zeroed, 16)
                sp.wait_ge(s_zeroed, 16 * 3 * BT)
                sp.wait_ge(s_x, 32)

            @block.gpsimd
            def _(pool):
                pool.memset(ident[:, :], 0.0).then_inc(s_idm, 1)
                pool.memset(lower[:, :], 1.0).then_inc(s_idm, 1)
                pool.wait_ge(s_idm, 2)
                pool.affine_select(out=ident[:, :], in_=ident[:, :], compare_op=ALU.not_equal, fill=1.0, base=0,
                                   pattern=[[-1, P]], channel_multiplier=1).then_inc(s_id, 1)
                pool.affine_select(out=lower[:, :], in_=lower[:, :], compare_op=ALU.is_gt, fill=0.0, base=0,
                                   pattern=[[-1, P]], channel_multiplier=1).then_inc(s_id, 1)
                pool.iota(iota_p[:, :], [[0, 1]], base=NPAD, channel_multiplier=1,
                          allow_small_or_imprecise_dtypes=True).then_inc(s_id, 1)

            @block.scalar
            def _(act):
                act.dma_start(wload[:, :, :], A["L0_gnn_W0"].rearrange("t k n -> k t n")).then_inc(s_wts, 16)
                act.dma_start(w0[:, 0:T * F].rearrange("k (t n) -> k t n", t=T), A["L0_gnn_W0"].rearrange("t k n -> k t n")).then_inc(s_wts, 16)
                act.dma_start(w1[:, 0:T * F].rearrange("k (t n) -> k t n", t=T), A["L0_gnn_W1"].rearrange("t k n -> k t n")).then_inc(s_wts, 16)
                act.dma_start(w1[:, T * F + T:], A["L0_gnn_Wres"]).then_inc(s_wts, 16)
                act.dma_start(w2[:, :], A["L1_gnn_W"]).then_inc(s_wts, 16)
                for l in range(2):
                    act.dma_start(al[l][:, :, :], A[f"L0_gnn_Al{l}"].rearrange("t k n -> k t n")).then_inc(s_wts, 16)
                    act.dma_start(ar[l][:, :, :], A[f"L0_gnn_Ar{l}"].rearrange("t k n -> k t n")).then_inc(s_wts, 16)
                act.dma_start(bres[:, :], A["L0_gnn_bres"].partition_broadcast(P)).then_inc(s_small, 16)
                act.dma_start(b2[:, :], A["L1_gnn_b"].partition_broadcast(P)).then_inc(s_small, 16)
                act.dma_start(deg[:, :], A["L1_gnn_deg_coeff"].partition_broadcast(P)).then_inc(s_small, 16)
                act.dma_start(cin[:, 0:3], A["L1_gnn_coeff_param"].partition_broadcast(P)).then_inc(s_small, 16)
                act.dma_start(cin[:, 3:4], A["L1_gnn_scale_param"].partition_broadcast(P)).then_inc(s_small, 16)
                for l in range(2):
                    act.wait_ge(s_wt, l + 1)
                    act.activation(wt[l][:, :, :], ps_w[l][0:F, 0:T * F].rearrange("k (t n) -> k t n", t=T), ACT.Copy).then_inc(s_wtc, 1)
                act.wait_ge(s_csm, 1)
                act.activation(csm[:, 0:3], csm[:, 0:3], ACT.Exp, accum_out=csm[:, 3:4]).then_inc(a, 1)
                act.activation(csm[:, 5:6], csm[:, 4:5], ACT.Exp, scale=-1.0).then_inc(a, 1)
                act.wait_ge(a, 2)
                act.activation(csm[:, 6:7], csm[:, 5:6], ACT.Ln, bias=1.0).then_inc(a, 1)
                act.wait_ge(s_z, 1)
                act.activation(raw_i[0].ap()[0:ROWS, :].bitcast(F32), raw_i[0].ap()[0:ROWS, :].bitcast(F32), ACT.Exp, scale=-1.0).then_inc(a, 1)
                act.wait_ge(a, 4)
                act.activation(raw_i[0].ap()[0:ROWS, :].bitcast(F32), raw_i[0].ap()[0:ROWS, :].bitcast(F32), ACT.Ln, bias=1.0).then_inc(s_sp, 1)
                act.wait_ge(s_rowready, 1)
                with act.Fori(0, JT // 2) as i:
                    for q in range(2):
                        take(act, s_turn_free[q])
                        act.activation(turn[0:ROWS, q, :, :], row[0:ROWS, :, bass.ds(i * (2 * P) + q * P, P)], ACT.Copy).then_inc(s_turn_in[q], 1)
                for q in range(2):
                    take(act, s_turn_free[q])

            @block.vector
            def _(dve):
                nv = [0]

                def link(ins):
                    nv[0] += 1
                    ins.then_inc(v, 1)
                    dve.wait_ge(v, nv[0])

                lo = 96
                dve.memset(x_sb[:, NT - 1, :], 0.0).then_inc(s_pad, 1)
                dve.memset(raw_i[0][lo:ROWS, :], PAD_SRC).then_inc(s_pad, 1)
                dve.memset(raw_i[1][lo:ROWS, :], PAD_DST).then_inc(s_pad, 1)
                dve.memset(raw_t[lo:ROWS, :], 0).then_inc(s_pad, 1)
                dve.memset(row[lo:ROWS, A_W, :], 0.0).then_inc(s_pad, 1)
                dve.memset(row[lo:ROWS, A_BASE, :], 0.0).then_inc(s_pad, 1)
                dve.memset(zeros[:, :], 0.0).then_inc(s_zero, 1)
                dve.wait_ge(s_wts, 16 * 9)
                for l in range(2):
                    link(dve.tensor_tensor(al[l][:, :, :], al[l][:, :, :], ar[l][:, :, :], ALU.add))
                link(dve.tensor_reduce(asum[0][:, :, :], al[0].ap().rearrange("k t (h d) -> k t h d", h=HEADS), AX.X, ALU.add))
                dve.tensor_reduce(asum[1][:, :], al[1][:, :, :], AX.X, ALU.add).then_inc(s_asum, 1)
                dve.wait_ge(s_small, 16 * 5)
                link(dve.tensor_reduce(csm[:, 7:8], cin[:, 0:3], AX.X, ALU.max))
                link(dve.tensor_scalar(csm[:, 0:3], cin[:, 0:3], csm[:, 7:8], None, ALU.subtract))
                dve.scalar_tensor_tensor(csm[:, 4:5], cin[:, 3:4], -1.0, cin[:, 3:4], ALU.mult, ALU.max).then_inc(s_csm, 1)
                dve.wait_ge(a, 3)
                link(dve.reciprocal(csm[:, 7:8], csm[:, 3:4]))
                link(dve.tensor_scalar(coeff[:, 0:3], csm[:, 0:3], csm[:, 7:8], None, ALU.mult))
                link(dve.scalar_tensor_tensor(coeff[:, 3:4], cin[:, 3:4], 0.0, csm[:, 6:7], ALU.max, ALU.add))
                dve.wait_ge(s_rows, 160)
                src_f, dst_f = row[0:ROWS, A_SRC, :], row[0:ROWS, A_DST, :]
                link(dve.tensor_copy(src_f, raw_i[0][0:ROWS, :]))
                link(dve.tensor_copy(dst_f, raw_i[1][0:ROWS, :]))
                link(dve.scalar_tensor_tensor(row[0:ROWS, A_IDX, :], src_f, float(T), raw_t[0:ROWS, :], ALU.mult, ALU.add))
                z = raw_i[1].ap()[0:ROWS, :].bitcast(F32)
                lg = raw_i[0].ap()[0:ROWS, :].bitcast(F32)
                base = row[0:ROWS, A_BASE, :]
                link(dve.tensor_scalar(z, base, deg[0:ROWS, 0:1], deg[0:ROWS, 1:2], ALU.mult, ALU.add))
                dve.scalar_tensor_tensor(lg, z, -1.0, z, ALU.mult, ALU.max).then_inc(s_z, 1)
                link(dve.tensor_tensor(base, src_f, dst_f, ALU.not_equal))
                link(dve.tensor_tensor(base, base, row[0:ROWS, A_W, :], ALU.mult))
                dve.wait_ge(s_sp, 1)
                link(dve.scalar_tensor_tensor(z, z, 0.0, lg, ALU.max, ALU.add))
                dve.tensor_tensor(base, base, z, ALU.mult).then_inc(s_rowready, 1)
                for l in range(2):
                    dve.wait_ge(s_wa, l + 1)
                    n = T * HEADS if l == 0 else T
                    dve.tensor_copy((w0, w1)[l][:, T * F:T * F + n], ps_w[2 + l][0:F, 0:n]).then_inc(v, 1)
                    nv[0] += 1
                with dve.Fori(0, JT // 2) as i:
                    for q in range(2):
                        take(dve, s_turned[q])
                        dve.sem_inc(s_turn_free[q], 1)
                        dve.tensor_copy(edge.ap().rearrange("p a (r j) -> p a r j", j=JT)[:, :, :, bass.ds(2 * i + q, 1)].rearrange("p a r j -> p a (r j)"),
                                        ps_turn[q][:, 0:NA * ROWS].rearrange("p (a r) -> p a r", a=NA)).then_inc(s_turned_free[q], 1)
                for q in range(2):
                    dve.wait_ge(s_turned_free[q], 1)

            @block.tensor
            def _(pe):
                pe.wait_ge(s_id, 3)
                pe.wait_ge(s_wts, 16 * 9)
                for l, w in enumerate((w0, w1)):
                    for t in range(T):
                        last = pe.transpose(ps_w[l][0:F, t * F:(t + 1) * F], w[:, t * F:(t + 1) * F], ident[0:F, 0:F])
                    last.then_inc(s_wt, 1)
                pe.wait_ge(s_asum, 1)
                for l in range(2):
                    pe.wait_ge(s_wtc, l + 1)
                    n = HEADS if l == 0 else 1
                    for t in range(T):
                        rhs = asum[0][:, t, :] if l == 0 else asum[1][:, t:t + 1]
                        last = pe.matmul(ps_w[2 + l][0:F, t * n:(t + 1) * n], wt[l][:, t, :], rhs, start=True, stop=True)
                    last.then_inc(s_wa, 1)
                for q in range(2):
                    pe.sem_inc(s_turn_free[q], 1)
                    pe.sem_inc(s_turned_free[q], 1)
                with pe.Fori(0, JT // 2) as i:
                    for q in range(2):
                        take(pe, s_turn_in[q])
                        take(pe, s_turned_free[q])
                        for k in range(NA):
                            last = pe.transpose(ps_turn[q][:, k * ROWS:(k + 1) * ROWS], turn[0:ROWS, q, k, :], ident[0:ROWS, 0:ROWS])
                        last.then_inc(s_turned[q], 1)

        def table_phase(layer):
            w, heads = ((w0, HEADS), (w1, 1))[layer]
            natt = T * heads
            ncol = T * F + natt + (F if layer else 0)
            node_in = x_sb if layer == 0 else acc
            with ExitStack() as s2, nc.Block() as block:
                stage = sb(f"stage{layer}", [P, CH * F], F32, s2)
                xt = sb(f"xt{layer}", [F, CH * P], F32, s2)
                prod = sb(f"prod{layer}", [P, CH, T * F + natt], F32, s2)
                lk = sb(f"lk{layer}", [P, CH, natt], F32, s2)
                msg = sb(f"msg{layer}", [P, NT, T * F], F32, s2)
                ps_t = psum(f"ps_t{layer}", [F, 2, 512], s2)
                ps_h = [psum(f"ps_h{layer}{k}", [P, 512], s2) for k in range(4)]
                s_stage, s_xt, s_xt_copied, s_h = (sem(f"{n}{layer}") for n in ("s_stage", "s_xt", "s_xt_copied", "s_h"))
                s_h_free, s_prod, s_lk, s_att, s_msg, s_out = (sem(f"{n}{layer}") for n in ("s_h_free", "s_prod", "s_lk", "s_att", "s_msg", "s_out"))
                s_next, v = sem(f"s_next{layer}"), sem(f"v_table{layer}")

                @block.vector
                def _(dve):
                    with dve.Fori(0, NCH) as i:
                        dve.tensor_copy(stage[:, :].rearrange("p (c f) -> p c f", f=F), node_in[:, bass.ds(i * CH, CH), :]).then_inc(s_stage, 1)
                        take(dve, s_prod)
                        dve.sem_inc(s_h_free, 1)
                        att = prod[:, :, T * F:T * F + natt]
                        dve.scalar_tensor_tensor(lk[:, :, :], att, SLOPE, att, ALU.mult, ALU.max).then_inc(s_lk, 1)
                        take(dve, s_att)
                        for c in range(CH):
                            o = msg[:, bass.ds(i * CH + c, 1), :]
                            if layer == 0:
                                h = prod[:, c, 0:T * F].rearrange("p (t h d) -> p t d h", t=T, h=HEADS)
                                o = o.rearrange("p c (t d h) -> p (c t) d h", t=T, h=HEADS)
                                g = lk[:, c, :].rearrange("p (t o h) -> p t o h", t=T, o=1).to_broadcast([P, T, HID, HEADS])
                            else:
                                h = prod[:, c, 0:T * F].rearrange("p (t f) -> p t f", t=T)
                                o = o.rearrange("p c (t f) -> p (c t) f", t=T)
                                g = lk[:, c, :].rearrange("p (t o) -> p t o", t=T).to_broadcast([P, T, F])
                            last = dve.tensor_tensor(o, h, g, ALU.mult)
                        last.then_inc(s_msg, 1)

                @block.sync
                def _(sp):
                    rows = tab_l[layer].ap().rearrange("(i p t) f -> p i (t f)", p=P, t=T)
                    with sp.Fori(0, NCH) as i:
                        take(sp, s_msg)
                        sp.sem_inc(s_next, 1)
                        sp.dma_start(rows[:, bass.ds(i * CH, CH), :], msg[:, bass.ds(i * CH, CH), :]).then_inc(s_out, 16)
                    sp.wait_ge(s_out, 16 * NCH)

                @block.tensor
                def _(pe):
                    with pe.Fori(0, NCH) as i:
                        take(pe, s_stage)
                        for c in range(CH):
                            last = pe.transpose(ps_t[:, c // 4, c % 4 * P:(c % 4 + 1) * P], stage[:, c * F:(c + 1) * F], ident[:, :])
                        last.then_inc(s_xt, 1)
                        take(pe, s_xt_copied)
                        for c in range(CH):
                            take(pe, s_h_free)
                            pe.matmul(ps_h[c % 4][:, 0:ncol], xt[:, c * P:(c + 1) * P], w[:, 0:ncol], start=True, stop=True).then_inc(s_h, 1)

                @block.scalar
                def _(act):
                    act.sem_inc(s_h_free, 4)
                    act.sem_inc(s_next, 1)
                    with act.Fori(0, NCH) as i:
                        take(act, s_xt)
                        for k, n in ((0, 4), (1, CH - 4)):
                            last = act.activation(xt[:, k * 4 * P:(k * 4 + n) * P], ps_t[:, k, 0:n * P], ACT.Copy)
                        last.then_inc(s_xt_copied, 1)
                        take(act, s_next)
                        for c in range(CH):
                            take(act, s_h)
                            if layer:
                                act.activation(skip[:, bass.ds(i * CH + c, 1), :].rearrange("p c f -> p (c f)"), ps_h[c % 4][:, T * F + natt:ncol], ACT.Copy)
                            act.activation(prod[:, c, :], ps_h[c % 4][:, 0:T * F + natt], ACT.Copy).then_inc(s_prod if c == CH - 1 else s_h_free, 1)
                        take(act, s_lk)
                        act.activation(lk[:, :, :], lk[:, :, :], ACT.Sigmoid).then_inc(s_att, 1)

        def edge_phase(n, tabs, width, key, tables):
            ng = len(tabs)
            with ExitStack() as s3, nc.Block() as block:
                idx = sb(f"idx{n}", [P, 2, ng, BT], I32, s3)
                keyf = sb(f"keyf{n}", [P, 2, BT], F32, s3)
                rows = sb(f"rows{n}", [P, 2, ng, BT, width], F32, s3)
                same = sb(f"same{n}", [P, BT, P], F32, s3)
                before = sb(f"before{n}", [P, BT, P], F32, s3)
                dup = sb(f"dup{n}", [P, 3, BT], F32, s3)
                sidx = sb(f"sidx{n}", [P, 2, BT], I32, s3)
                wmsg = sb(f"wmsg{n}", [P, BT, F], F32, s3)
                outm = sb(f"outm{n}", [P, 2, BT, F], F32, s3)
                sc = sb(f"sc{n}", [P, 6, BT], F32, s3)
                ps_key = psum(f"ps_key{n}", [P, BT * P], s3)
                ps_sum = psum(f"ps_sum{n}", [P, BT * F], s3)
                s_idx = [sem(f"s_idx{n}{q}") for q in range(2)]
                s_idx_free = [sem(f"s_idx_free{n}{q}") for q in range(2)]
                s_got = [sem(f"s_got{n}{q}") for q in range(2)]
                s_rows_free = [sem(f"s_rows_free{n}{q}") for q in range(2)]
                s_key, s_wm, s_sum = sem(f"s_key{n}"), sem(f"s_wm{n}"), sem(f"s_sum{n}")
                s_keyf, s_key_free = sem(f"s_keyf{n}"), sem(f"s_key_free{n}")
                s_out = sem(f"s_outm{n}")
                s_out_free = [sem(f"s_out_free{n}{q}") for q in range(2)]
                s_add = [sem(f"s_add{n}{k}") for k in range(BT)]
                v = sem(f"v_edge{n}")

                @block.gpsimd
                def _(pool):
                    def gather(q, first=False):
                        take(pool, s_idx[q])
                        if not first:
                            take(pool, s_rows_free[q])
                        for g in range(ng):
                            for k in range(BT):
                                pool.indirect_dma_start(rows[:, q, g, k, :], None, tabs[g][0].ap(),
                                                        bass.IndirectOffsetOnAxis(ap=idx[:, q, g, k:k + 1], axis=0)).then_inc(s_got[q], 16)

                    def scatter(q, done=None):
                        take(pool, s_out)
                        for k in range(BT):
                            if done is not None:
                                pool.wait_ge(s_add[k], done).then_inc(s_out_free[1 - q], 1)
                            pool.indirect_dma_start(tables[k].ap(), bass.IndirectOffsetOnAxis(ap=sidx[:, q, k:k + 1], axis=0),
                                                    outm[:, q, k, :], None, compute_op=ALU.add).then_inc(s_add[k], 16)

                    gather(0, True)
                    gather(1, True)
                    scatter(0)
                    with pool.Fori(0, NB // 2 - 1) as i:
                        gather(0)
                        scatter(1, i * 32 + 16)
                        gather(1)
                        scatter(0, i * 32 + 32)
                    scatter(1, 16 * (NB - 1))
                    for k in range(BT):
                        pool.wait_ge(s_add[k], 16 * NB)

                @block.scalar
                def _(act):
                    for q in range(2):
                        act.sem_inc(s_idx_free[q], 1)
                    with act.Fori(0, NB // 2) as i:
                        for q in range(2):
                            take(act, s_idx_free[q])
                            for g in range(ng):
                                last = act.activation(idx[:, q, g, :], edge[:, tabs[g][1], bass.ds(i * (2 * BT) + q * BT, BT)], ACT.Copy)
                            last.then_inc(s_idx[q], 1)
                            act.activation(keyf[:, q, :], edge[:, key, bass.ds(i * (2 * BT) + q * BT, BT)], ACT.Copy).then_inc(s_keyf, 1)

                @block.tensor
                def _(pe):
                    pe.sem_inc(s_key_free, 1)
                    with pe.Fori(0, NB // 2) as i:
                        for q in range(2):
                            take(pe, s_keyf)
                            take(pe, s_key_free)
                            for k in range(BT):
                                last = pe.matmul(ps_key[:, k * P:(k + 1) * P], keyf[:, q, k:k + 1].to_broadcast([P, P]), ident[:, :],
                                                 start=True, stop=True)
                            last.then_inc(s_key, 1)
                            take(pe, s_wm)
                            for k in range(BT):
                                last = pe.matmul(ps_sum[:, k * F:(k + 1) * F], same[:, k, :], wmsg[:, k, :], start=True, stop=True)
                            last.then_inc(s_sum, 1)

                @block.vector
                def _(dve):
                    def link(ins):
                        ins.then_inc(v, 1)
                        take(dve, v)

                    for q in range(2):
                        dve.sem_inc(s_out_free[q], BT)
                    with dve.Fori(0, NB // 2) as i:
                        for q in range(2):
                            at = i * (2 * BT) + q * BT
                            take(dve, s_key)
                            kq = keyf[:, q, :].rearrange("p (k o) -> p k o", o=1).to_broadcast([P, BT, P])
                            link(dve.tensor_tensor(same[:, :, :], ps_key[:, :].rearrange("p (k c) -> p k c", k=BT), kq, ALU.is_equal))
                            dve.sem_inc(s_key_free, 1)
                            low = lower[:, :].rearrange("p (o c) -> p o c", o=1).to_broadcast([P, BT, P])
                            link(dve.tensor_tensor(before[:, :, :], same[:, :, :], low, ALU.mult))
                            link(dve.tensor_reduce(dup[:, 0, :], before[:, :, :], AX.X, ALU.max))
                            spare = iota_p[:, 0:1].to_broadcast([P, BT])
                            link(dve.tensor_tensor(dup[:, 1, :], spare, keyf[:, q, :], ALU.subtract))
                            link(dve.tensor_tensor(dup[:, 2, :], dup[:, 1, :], dup[:, 0, :], ALU.mult))
                            take(dve, s_out_free[q], BT)
                            link(dve.tensor_tensor(sidx[:, q, :], dup[:, 2, :], keyf[:, q, :], ALU.add))
                            dve.wait_ge(s_got[q], i * (16 * BT * ng) + 16 * BT * ng).then_inc(s_idx_free[q], 1)
                            if n < 2:
                                wq = edge[:, A_W, bass.ds(at, BT)].rearrange("p (k o) -> p k o", o=1).to_broadcast([P, BT, F])
                                dve.tensor_tensor(wmsg[:, :, :], rows[:, q, 0, :, :], wq, ALU.mult).then_inc(s_wm, 1)
                            else:
                                link(dve.tensor_tensor(wmsg[:, :, :], rows[:, q, 0, :, 0:F], rows[:, q, 1, :, 0:F], ALU.mult))
                                link(dve.tensor_reduce(sc[:, 0, :], wmsg[:, :, :], AX.X, ALU.add))
                                link(dve.tensor_tensor(sc[:, 1, :], rows[:, q, 0, :, F], rows[:, q, 1, :, F], ALU.mult))
                                link(dve.tensor_scalar(sc[:, 1, :], sc[:, 1, :], EPS_SIM, None, ALU.max))
                                link(dve.reciprocal(sc[:, 2, :], sc[:, 1, :]))
                                link(dve.tensor_tensor(sc[:, 0, :], sc[:, 0, :], sc[:, 2, :], ALU.mult))
                                link(dve.tensor_scalar(sc[:, 3, :], sc[:, 0, :], 0.0, coeff[:, 0:1], ALU.max, ALU.mult))
                                link(dve.tensor_scalar(sc[:, 4, :], sc[:, 0, :], 0.0, coeff[:, 1:2], ALU.min, ALU.mult))
                                link(dve.tensor_tensor(sc[:, 3, :], sc[:, 3, :], sc[:, 4, :], ALU.add))
                                link(dve.tensor_tensor(sc[:, 5, :], sc[:, 3, :], edge[:, A_BASE, bass.ds(at, BT)], ALU.mult))
                                cq = sc[:, 5, :].rearrange("p (k o) -> p k o", o=1).to_broadcast([P, BT, F])
                                dve.tensor_tensor(wmsg[:, :, :], rows[:, q, 1, :, 0:F], cq, ALU.mult).then_inc(s_wm, 1)
                            take(dve, s_sum)
                            dve.sem_inc(s_rows_free[q], 1)
                            dve.tensor_copy(outm[:, q, :, :], ps_sum[:, :].rearrange("p (k f) -> p k f", k=BT)).then_inc(s_out, 1)

        def add_tables(dve, n, s_load, s_used, link):
            for k in range(BT):
                dve.wait_ge(s_load[k % 2], 16 * (k // 2 + 1))
                if k == 0:
                    ins = dve.tensor_copy(acc[:, :, :], nbuf[0][:, :, :])
                else:
                    ins = dve.tensor_tensor(acc[:, :, :], acc[:, :, :], nbuf[k % 2][:, :, :], ALU.add)
                link(ins)
                dve.sem_inc(s_used, 1)

        def load_tables(sp, n, s_load, s_used):
            for k in range(BT):
                if k >= 2:
                    sp.wait_ge(s_used, k - 1)
                sp.dma_start(nbuf[k % 2][:, :, :], sums[n][k].ap()[0:NPAD, :].rearrange("(i p) f -> p i f", p=P)).then_inc(s_load[k % 2], 16)

        def bc_n(ap):
            return ap.rearrange("p (i o) -> p i o", o=1).to_broadcast([P, NT, F])

        def bc_f(ap):
            return ap.rearrange("p (o f) -> p o f", o=1).to_broadcast([P, NT, F])

        def layer_norm(dve, link, s_var, s_std, out_ap, src, tmp):
            link(dve.tensor_reduce(mom[:, 0, :], src[:, :, :], AX.X, ALU.add))
            link(dve.tensor_scalar(mom[:, 0, :], mom[:, 0, :], 1.0 / F, None, ALU.mult))
            link(dve.tensor_tensor(src[:, :, :], src[:, :, :], bc_n(mom[:, 0, :]), ALU.subtract))
            link(dve.tensor_tensor(tmp[:, :, :], src[:, :, :], src[:, :, :], ALU.mult))
            link(dve.tensor_reduce(mom[:, 1, :], tmp[:, :, :], AX.X, ALU.add))
            dve.tensor_scalar(mom[:, 1, :], mom[:, 1, :], 1.0 / F, EPS_LN, ALU.mult, ALU.add).then_inc(s_var, 1)
            dve.wait_ge(s_std, 1)
            link(dve.reciprocal(mom[:, 3, :], mom[:, 2, :]))
            return dve.tensor_tensor(out_ap, src[:, :, :], bc_n(mom[:, 3, :]), ALU.mult)

        table_phase(0)
        edge_phase(0, [(tab_l[0], A_IDX)], F, A_DST, sums[0])

        with nc.Block() as block:
            s_load, s_used, v, s_low, s_exp = [sem("s_load0a"), sem("s_load0b")], sem("s_used0"), sem("v_elu"), sem("s_low"), sem("s_exp")

            @block.sync
            def _(sp):
                load_tables(sp, 0, s_load, s_used)

            @block.scalar
            def _(act):
                act.wait_ge(s_low, 1)
                act.activation(nbuf[0][:, :, :], nbuf[0][:, :, :], ACT.Exp).then_inc(s_exp, 1)

            @block.vector
            def _(dve):
                def link(ins):
                    ins.then_inc(v, 1)
                    take(dve, v)
                add_tables(dve, 0, s_load, s_used, link)
                dve.tensor_scalar(nbuf[0][:, :, :], acc[:, :, :], 0.0, None, ALU.min).then_inc(s_low, 1)
                dve.tensor_scalar(nbuf[1][:, :, :], acc[:, :, :], 0.0, -1.0, ALU.max, ALU.add).then_inc(v, 1)
                take(dve, v)
                dve.wait_ge(s_exp, 1)
                link(dve.tensor_tensor(acc[:, :, :], nbuf[0][:, :, :], nbuf[1][:, :, :], ALU.add))

        table_phase(1)
        edge_phase(1, [(tab_l[1], A_IDX)], F, A_DST, sums[1])

        with ExitStack() as s4, nc.Block() as block:
            s_load, s_used, v, s_var, s_std = [sem("s_load1a"), sem("s_load1b")], sem("s_used1"), sem("v_n1"), sem("s_var1"), sem("s_std1")
            s_stage, s_xt, s_xtc, s_wh, s_whc, s_sq, s_nrm, s_tab = (sem(k) for k in ("s_stage2", "s_xt2", "s_xtc2", "s_wh", "s_whc", "s_sq", "s_nrm", "s_tab"))
            stage = sb("stage2", [P, CH * F], F32, s4)
            xt = sb("xt2", [F, CH * P], F32, s4)
            wide = sb("wide", [P, NT, F + 1], F32, s4)
            ps_t = psum("ps_t2", [F, 2, 512], s4)
            ps_h = psum("ps_h2", [P, 512], s4)

            @block.sync
            def _(sp):
                load_tables(sp, 1, s_load, s_used)
                sp.wait_ge(s_nrm, 1)
                sp.dma_start(tab_g.ap().rearrange("(i p) f -> p i f", p=P), wide[:, :, :]).then_inc(s_tab, 16)
                sp.wait_ge(s_tab, 16)

            @block.scalar
            def _(act):
                act.wait_ge(s_var, 1)
                act.activation(mom[:, 2, :], mom[:, 1, :], ACT.Sqrt).then_inc(s_std, 1)
                with act.Fori(0, NCH) as i:
                    take(act, s_xt)
                    for k, m in ((0, 4), (1, CH - 4)):
                        last = act.activation(xt[:, k * 4 * P:(k * 4 + m) * P], ps_t[:, k, 0:m * P], ACT.Copy)
                    last.then_inc(s_xtc, 1)
                act.wait_ge(s_sq, 1)
                act.activation(wide[:, :, F], mom[:, 0, :], ACT.Sqrt).then_inc(s_nrm, 1)

            @block.tensor
            def _(pe):
                with pe.Fori(0, NCH) as i:
                    take(pe, s_stage)
                    for c in range(CH):
                        last = pe.transpose(ps_t[:, c // 4, c % 4 * P:(c % 4 + 1) * P], stage[:, c * F:(c + 1) * F], ident[:, :])
                    last.then_inc(s_xt, 1)
                    take(pe, s_xtc)
                    for c in range(CH):
                        last = pe.matmul(ps_h[:, c * F:(c + 1) * F], xt[:, c * P:(c + 1) * P], w2[:, :], start=True, stop=True)
                    last.then_inc(s_wh, 1)

            @block.vector
            def _(dve):
                def link(ins):
                    ins.then_inc(v, 1)
                    take(dve, v)
                add_tables(dve, 1, s_load, s_used, link)
                link(dve.tensor_tensor(acc[:, :, :], acc[:, :, :], skip[:, :, :], ALU.add))
                link(dve.tensor_tensor(acc[:, :, :], acc[:, :, :], bc_f(bres[:, :]), ALU.add))
                link(dve.tensor_tensor(acc[:, :, :], acc[:, :, :], x_sb[:, :, :], ALU.add))
                link(layer_norm(dve, link, s_var, s_std, x_sb[:, :, :], acc, nbuf[0]))
                with dve.Fori(0, NCH) as i:
                    dve.tensor_copy(stage[:, :].rearrange("p (c f) -> p c f", f=F), x_sb[:, bass.ds(i * CH, CH), :]).then_inc(s_stage, 1)
                    take(dve, s_wh)
                    b7 = b2[:, :].rearrange("p (o f) -> p o f", o=1).to_broadcast([P, CH, F])
                    link(dve.tensor_tensor(skip[:, bass.ds(i * CH, CH), :], ps_h[:, 0:CH * F].rearrange("p (c f) -> p c f", f=F), b7, ALU.add))
                link(dve.tensor_copy(wide[:, :, 0:F], skip[:, :, :]))
                link(dve.tensor_tensor(nbuf[0][:, :, :], skip[:, :, :], skip[:, :, :], ALU.mult))
                dve.tensor_reduce(mom[:, 0, :], nbuf[0][:, :, :], AX.X, ALU.add).then_inc(s_sq, 1)

        edge_phase(2, [(tab_g, A_SRC), (tab_g, A_DST)], F + 1, A_SRC, sums[2])

        with nc.Block() as block:
            s_load, s_used, v, s_var, s_std = [sem("s_load2a"), sem("s_load2b")], sem("s_used2"), sem("v_n2"), sem("s_var2"), sem("s_std2")
            s_fin, s_out = sem("s_fin"), sem("s_out")

            @block.sync
            def _(sp):
                load_tables(sp, 2, s_load, s_used)
                sp.wait_ge(s_fin, 1)
                sp.dma_start(out[0:(NT - 1) * P, :].rearrange("(i p) f -> p i f", p=P), nbuf[1][:, 0:NT - 1, :]).then_inc(s_out, 16)
                sp.dma_start(out[(NT - 1) * P:NODES, :], nbuf[1][0:LAST, NT - 1, :]).then_inc(s_out, 16)
                sp.wait_ge(s_out, 32)

            @block.scalar
            def _(act):
                act.wait_ge(s_var, 1)
                act.activation(mom[:, 2, :], mom[:, 1, :], ACT.Sqrt).then_inc(s_std, 1)

            @block.vector
            def _(dve):
                def link(ins):
                    ins.then_inc(v, 1)
                    take(dve, v)
                add_tables(dve, 2, s_load, s_used, link)
                link(dve.scalar_tensor_tensor(acc[:, :, :], skip[:, :, :], coeff[:, 2:3], acc[:, :, :], ALU.mult, ALU.add))
                link(dve.scalar_tensor_tensor(acc[:, :, :], acc[:, :, :], coeff[:, 3:4], x_sb[:, :, :], ALU.mult, ALU.add))
                layer_norm(dve, link, s_var, s_std, nbuf[1][:, :, :], acc, nbuf[0]).then_inc(s_fin, 1)


_INS = ["x", "src", "dst", "edge_type_5", "edge_weight", "edge_weight_n2", "L0_gnn_W0", "L0_gnn_Al0", "L0_gnn_Ar0",
        "L0_gnn_W1", "L0_gnn_Al1", "L0_gnn_Ar1", "L0_gnn_Wres", "L0_gnn_bres", "L1_gnn_W", "L1_gnn_b",
        "L1_gnn_deg_coeff", "L1_gnn_coeff_param", "L1_gnn_scale_param"]


def kernel(**inputs):
    import numpy as _np
    import concourse.bacc as _bacc
    from concourse import mybir as _mybir
    from concourse.bass_utils import run_bass_kernel_spmd as _run

    nc = _bacc.Bacc("TRN2", target_bir_lowering=False, num_devices=1)
    arrays, args = {}, {}
    for name in _INS:
        a = _np.ascontiguousarray(inputs[name])
        arrays[f"in_{name}"] = a
        args[name] = nc.dram_tensor(f"in_{name}", a.shape, _mybir.dt.from_np(a.dtype), kind="ExternalInput").ap()
    out = nc.dram_tensor("out", (NODES, F), F32, kind="ExternalOutput").ap()
    build(nc, args, out)
    r = _run(nc, [arrays], core_ids=[0])
    return r.results[0]["out"]
```

```python
from contextlib import ExitStack, contextmanager

import concourse.bass as bass
from concourse import mybir

F32 = mybir.dt.float32
I32 = mybir.dt.int32
ALU = mybir.AluOpType
ACT = mybir.ActivationFunctionType
AX = mybir.AxisListType
DVE, POOL, SP = mybir.EngineType.DVE, mybir.EngineType.Pool, mybir.EngineType.SP

P = 128
F = 64
T = 5
HEADS = 8
HID = F // HEADS
SLOPE = 0.2
EPS_LN = 1e-5
EPS_SIM = 1e-8

NODES = 6250
NT = -(-NODES // P)
NPAD = NT * P
LAST = NODES - (NT - 1) * P
EDGES = 200000
ROWS = 112
JT = 14
ROWLEN = JT * P
ET = ROWS * JT
FULLROWS = EDGES // ROWLEN
TAIL = EDGES - FULLROWS * ROWLEN
PAD_SRC = NPAD - 1
PAD_DST = NODES - 1

WIN = 80
STRIP = P
TWIN = 8
GROUPS = ROWS // 2
NGPAD = NPAD + P
LOOPS = 14
SLOTS = ROWS // LOOPS
RB = 4
HT = JT // 2
SB = 448
NSB = NPAD // SB
PAIRS = GROUPS // 2

BT = 8
NB = ET // BT
TAB = NPAD + P
CH = 7
NCH = NT // CH
A_IDX, A_W, A_BASE, A_REL, A_LO, A_KEY = range(6)
A_DST, A_SRC = A_REL, A_LO
NA = 6
TINY = 1e-30


def take(eng, sem, n=1):
    eng.wait_ge(sem, n).then_inc(sem, -n)


def build(nc, A, out):
    ctx = ExitStack()
    with ctx:
        scopes = []

        def sem(name, keep=False):
            if keep or not scopes:
                return ctx.enter_context(nc.semaphore(name))
            s = nc.alloc_semaphore(name)
            scopes[-1].append(s)
            return s

        @contextmanager
        def scope():
            scopes.append([])
            with ExitStack() as stack:
                yield stack
            sems = sorted(scopes.pop(), key=lambda s: s.num)
            run = 0
            for k in range(1, len(sems) + 1):
                if k == len(sems) or sems[k].num != sems[k - 1].num + 1:
                    nc.gpsimd.sem_clear(range(sems[run].num, sems[k - 1].num + 1))
                    run = k
            nc.all_engine_barrier()
            for s in sems:
                nc.release_semaphore(s)

        def sb(name, shape, dt=F32, c=ctx):
            return c.enter_context(nc.sbuf_tensor(name, shape, dt))

        def psum(name, shape, c=ctx):
            return c.enter_context(nc.psum_tensor(name, shape, F32))

        ident = sb("ident", [P, P])
        lower = sb("lower", [P, P])
        iota_p = sb("iota_p", [P, 1])
        iota_f = sb("iota_f", [P, NT * TWIN])
        edge = sb("edge", [P, NA, ET + RB * JT])
        x_sb = sb("x_sb", [P, NT, F])
        skip = sb("skip", [P, NT, F])
        acc = sb("acc", [P, NT, F])
        w0 = sb("w0", [F, T * F + T * HEADS])
        w1 = sb("w1", [F, T * F + T + F])
        w2 = sb("w2", [F, F])
        bres = sb("bres", [P, F])
        b2 = sb("b2", [P, F])
        deg = sb("deg", [P, 2])
        coeff = sb("coeff", [P, 8])
        mom = sb("mom", [P, 4, NT])
        offs = sb("offs", [1, 2 * ROWS * 8], I32)
        firsts = sb("firsts", [1, 2 * ROWS], I32)
        flags = sb("flags", [1, 2], I32)
        ones = sb("ones", [P, 1])
        eye2 = sb("eye2", [P, F])

        tab_l = [nc.dram_tensor(f"messages{l}", [NPAD * T, F], F32) for l in range(2)]
        tab_g = nc.dram_tensor("wh_norm", [NPAD, F + 1], F32)
        offs_d = nc.dram_tensor("offs_d", [ROWS, 16], I32)
        firsts_d = nc.dram_tensor("firsts_d", [ROWS, 2], I32)
        adj = nc.dram_tensor("adj", [2, GROUPS // 2 + 1, P, NPAD], F32)
        wh_rows = nc.dram_tensor("wh_rows", [NGPAD, F], F32)
        sums = [[nc.dram_tensor(f"sums{l}_{k}", [TAB, F], F32) for k in range(BT)] for l in range(3)]

        with scope() as s1, nc.Block() as block:
            raw_s, raw_d, raw_t = (sb(n, [P, ROWLEN], I32, s1) for n in ("raw_s", "raw_d", "raw_t"))
            row = sb("row", [P, NA, ROWLEN], F32, s1)
            hi, z, lg = (sb(n, [P, ROWLEN], d, s1) for n, d in (("hi", I32), ("z", F32), ("lg", F32)))
            first = sb("first", [P, 2], I32, s1)
            first_f = sb("first_f", [P, 2], F32, s1)
            off_f = sb("off_f", [P, 2, JT], F32, s1)
            off_i = sb("off_i", [P, 16], I32, s1)
            bad = sb("bad", [P, 8], F32, s1)
            turn = sb("turn", [P, 2, NA, P], F32, s1)
            al = [sb(f"al{l}", [F, T, F], F32, s1) for l in range(2)]
            ar = [sb(f"ar{l}", [F, T, F], F32, s1) for l in range(2)]
            asum = [sb("asum0", [F, T, HEADS], F32, s1), sb("asum1", [F, T], F32, s1)]
            wt = [sb(f"wt{l}", [F, T, F], F32, s1) for l in range(2)]
            cin = sb("cin", [P, 4], F32, s1)
            csm = sb("csm", [P, 8], F32, s1)
            ps_turn = [psum(f"ps_turn{k}", [P, 1024], s1) for k in range(2)]
            ps_w = [psum(f"ps_w{k}", [P, 512], s1) for k in range(4)]
            s_pad, s_x, s_rows, s_first, s_wts, s_small = (sem(n) for n in ("s_pad", "s_x", "s_rows", "s_first", "s_wts", "s_small"))
            s_id, s_idm, s_off, s_offd, s_offl = (sem(n) for n in ("s_id", "s_idm", "s_off", "s_offd", "s_offl"))
            v, a = sem("v_chain"), sem("a_chain")
            s_z, s_sp, s_rowready, s_bad, s_badsum = (sem(n) for n in ("s_z", "s_sp", "s_rowready", "s_bad", "s_badsum"))
            s_turn_in = [sem(f"s_turn_in{k}") for k in range(2)]
            s_turn_free = [sem(f"s_turn_free{k}") for k in range(2)]
            s_turned = [sem(f"s_turned{k}") for k in range(2)]
            s_turned_free = [sem(f"s_turned_free{k}") for k in range(2)]
            s_wt, s_wtc, s_asum, s_wa, s_csm = sem("s_wt"), sem("s_wtc"), sem("s_asum"), sem("s_wa"), sem("s_csm")

            @block.sync
            def _(sp):
                sp.wait_ge(s_pad, 6)
                for dst, src in ((raw_s, A["src"]), (raw_d, A["dst"]), (raw_t, A["edge_type_5"]),
                                 (row[:, A_W, :], A["edge_weight"]), (row[:, A_BASE, :], A["edge_weight_n2"])):
                    sp.dma_start(dst[0:FULLROWS, :], src[0:FULLROWS * ROWLEN].rearrange("(p n) -> p n", n=ROWLEN)).then_inc(s_rows, 16)
                    sp.dma_start(dst[FULLROWS:ROWS, 0:TAIL], src[FULLROWS * ROWLEN:EDGES].rearrange("(p n) -> p n", p=1)).then_inc(s_rows, 16)
                full = (GROUPS - 1) * 2 * ROWLEN
                sp.dma_start(first[0:ROWS - 2, 1:2], A["dst"][0:full].rearrange("(g n) -> g n", n=2 * ROWLEN)[:, 0:1]
                             .rearrange("g (a o) -> g a o", a=1).to_broadcast([GROUPS - 1, 2, 1])).then_inc(s_first, 16)
                sp.dma_start(first[ROWS - 2:ROWS, 1:2], A["dst"][full:full + 1].partition_broadcast(2)).then_inc(s_first, 16)
                sp.dma_start(x_sb[:, 0:NT - 1, :], A["x"][0:(NT - 1) * P, :].rearrange("(i p) f -> p i f", p=P)).then_inc(s_x, 16)
                sp.dma_start(x_sb[0:LAST, NT - 1, :], A["x"][(NT - 1) * P:NODES, :]).then_inc(s_x, 16)
                sp.wait_ge(s_off, 1)
                sp.dma_start(offs_d.ap(), off_i[0:ROWS, :]).then_inc(s_offd, 16)
                sp.dma_start(firsts_d.ap(), first[0:ROWS, :]).then_inc(s_offd, 16)
                sp.wait_ge(s_offd, 32)
                sp.dma_start(offs[:, :], offs_d.ap().rearrange("(o r) k -> o (r k)", o=1)).then_inc(s_offl, 16)
                sp.dma_start(firsts[:, :], firsts_d.ap().rearrange("(o r) k -> o (r k)", o=1)).then_inc(s_offl, 16)
                sp.wait_ge(s_offl, 32)
                sp.wait_ge(s_x, 32)

            @block.gpsimd
            def _(pool):
                pool.memset(ident[:, :], 0.0).then_inc(s_idm, 1)
                pool.memset(lower[:, :], 1.0).then_inc(s_idm, 1)
                pool.memset(ones[:, :], 1.0).then_inc(s_idm, 1)
                pool.memset(edge[:, :, ET:ET + RB * JT], 0.0).then_inc(s_idm, 1)
                pool.memset(eye2[:, :], 0.0).then_inc(s_idm, 1)
                pool.wait_ge(s_idm, 5)
                for h in range(2):
                    pool.affine_select(out=eye2[:, :], in_=eye2[:, :], compare_op=ALU.not_equal, fill=1.0, base=-h * F,
                                       pattern=[[-1, F]], channel_multiplier=1).then_inc(s_idm, 1)
                    pool.wait_ge(s_idm, 6 + h)
                pool.affine_select(out=ident[:, :], in_=ident[:, :], compare_op=ALU.not_equal, fill=1.0, base=0,
                                   pattern=[[-1, P]], channel_multiplier=1).then_inc(s_id, 1)
                pool.affine_select(out=lower[:, :], in_=lower[:, :], compare_op=ALU.is_gt, fill=0.0, base=0,
                                   pattern=[[-1, P]], channel_multiplier=1).then_inc(s_id, 1)
                pool.iota(iota_p[:, :], [[0, 1]], base=NPAD, channel_multiplier=1,
                          allow_small_or_imprecise_dtypes=True).then_inc(s_id, 1)
                pool.iota(iota_f[:, :], [[1, NT * TWIN]], base=0, channel_multiplier=0,
                          allow_small_or_imprecise_dtypes=True).then_inc(s_id, 1)

            @block.scalar
            def _(act):
                for l, w in enumerate((w0, w1)):
                    act.dma_start(w[:, 0:T * F].rearrange("k (t n) -> k t n", t=T), A[f"L0_gnn_W{l}"].rearrange("t k n -> k t n")).then_inc(s_wts, 16)
                act.dma_start(w1[:, T * F + T:], A["L0_gnn_Wres"]).then_inc(s_wts, 16)
                act.dma_start(w2[:, :], A["L1_gnn_W"]).then_inc(s_wts, 16)
                for l in range(2):
                    act.dma_start(al[l][:, :, :], A[f"L0_gnn_Al{l}"].rearrange("t k n -> k t n")).then_inc(s_wts, 16)
                    act.dma_start(ar[l][:, :, :], A[f"L0_gnn_Ar{l}"].rearrange("t k n -> k t n")).then_inc(s_wts, 16)
                act.dma_start(bres[:, :], A["L0_gnn_bres"].partition_broadcast(P)).then_inc(s_small, 16)
                act.dma_start(b2[:, :], A["L1_gnn_b"].partition_broadcast(P)).then_inc(s_small, 16)
                act.dma_start(deg[:, :], A["L1_gnn_deg_coeff"].partition_broadcast(P)).then_inc(s_small, 16)
                act.dma_start(cin[:, 0:3], A["L1_gnn_coeff_param"].partition_broadcast(P)).then_inc(s_small, 16)
                act.dma_start(cin[:, 3:4], A["L1_gnn_scale_param"].partition_broadcast(P)).then_inc(s_small, 16)
                for l in range(2):
                    act.wait_ge(s_wt, l + 1)
                    act.activation(wt[l][:, :, :], ps_w[l][0:F, 0:T * F].rearrange("k (t n) -> k t n", t=T), ACT.Copy).then_inc(s_wtc, 1)
                act.wait_ge(s_csm, 1)
                act.activation(csm[:, 0:3], csm[:, 0:3], ACT.Exp, accum_out=csm[:, 3:4]).then_inc(a, 1)
                act.activation(csm[:, 5:6], csm[:, 4:5], ACT.Exp, scale=-1.0).then_inc(a, 1)
                act.wait_ge(a, 2)
                act.activation(csm[:, 6:7], csm[:, 5:6], ACT.Ln, bias=1.0).then_inc(a, 1)
                act.wait_ge(s_z, 1)
                act.activation(lg[0:ROWS, :], lg[0:ROWS, :], ACT.Exp, scale=-1.0).then_inc(a, 1)
                act.wait_ge(a, 4)
                act.activation(lg[0:ROWS, :], lg[0:ROWS, :], ACT.Ln, bias=1.0).then_inc(s_sp, 1)
                act.wait_ge(s_rowready, 1)
                for q in range(2):
                    act.sem_inc(s_turn_free[q], 1)
                with act.Fori(0, JT // 2) as i:
                    for q in range(2):
                        take(act, s_turn_free[q])
                        act.activation(turn[0:ROWS, q, :, :], row[0:ROWS, :, bass.ds(i * (2 * P) + q * P, P)], ACT.Copy).then_inc(s_turn_in[q], 1)

            @block.vector
            def _(dve):
                nv = [0]

                def link(ins):
                    nv[0] += 1
                    ins.then_inc(v, 1)
                    dve.wait_ge(v, nv[0])

                lo96 = 96
                dve.memset(x_sb[:, NT - 1, :], 0.0).then_inc(s_pad, 1)
                dve.memset(raw_s[lo96:ROWS, :], PAD_SRC).then_inc(s_pad, 1)
                dve.memset(raw_d[lo96:ROWS, :], PAD_DST).then_inc(s_pad, 1)
                dve.memset(raw_t[lo96:ROWS, :], 0).then_inc(s_pad, 1)
                dve.memset(row[lo96:ROWS, A_W, :], 0.0).then_inc(s_pad, 1)
                dve.memset(row[lo96:ROWS, A_BASE, :], 0.0).then_inc(s_pad, 1)
                dve.wait_ge(s_wts, 16 * 8)
                for l in range(2):
                    link(dve.tensor_tensor(al[l][:, :, :], al[l][:, :, :], ar[l][:, :, :], ALU.add))
                link(dve.tensor_reduce(asum[0][:, :, :], al[0].ap().rearrange("k t (h d) -> k t h d", h=HEADS), AX.X, ALU.add))
                dve.tensor_reduce(asum[1][:, :], al[1][:, :, :], AX.X, ALU.add).then_inc(s_asum, 1)
                dve.wait_ge(s_small, 16 * 5)
                link(dve.tensor_reduce(csm[:, 7:8], cin[:, 0:3], AX.X, ALU.max))
                link(dve.tensor_scalar(csm[:, 0:3], cin[:, 0:3], csm[:, 7:8], None, ALU.subtract))
                dve.scalar_tensor_tensor(csm[:, 4:5], cin[:, 3:4], -1.0, cin[:, 3:4], ALU.mult, ALU.max).then_inc(s_csm, 1)
                dve.wait_ge(a, 3)
                link(dve.reciprocal(csm[:, 7:8], csm[:, 3:4]))
                link(dve.tensor_scalar(coeff[:, 0:3], csm[:, 0:3], csm[:, 7:8], None, ALU.mult))
                link(dve.scalar_tensor_tensor(coeff[:, 3:4], cin[:, 3:4], 0.0, csm[:, 6:7], ALU.max, ALU.add))
                link(dve.tensor_tensor(coeff[:, 4:5], coeff[:, 0:1], coeff[:, 1:2], ALU.subtract))
                link(dve.tensor_tensor(coeff[:, 5:6], coeff[:, 0:1], coeff[:, 1:2], ALU.min))
                link(dve.tensor_scalar(coeff[:, 6:7], coeff[:, 4:5], 0.0, 2.0, ALU.is_ge, ALU.mult))
                link(dve.tensor_scalar(coeff[:, 6:7], coeff[:, 6:7], -1.0, None, ALU.add))
                link(dve.tensor_tensor(coeff[:, 5:6], coeff[:, 5:6], coeff[:, 6:7], ALU.mult))
                dve.wait_ge(s_rows, 160)
                dve.wait_ge(s_first, 32)
                R = slice(0, ROWS)
                base, rel, lo, key = (row[R, k, :] for k in (A_BASE, A_REL, A_LO, A_KEY))
                link(dve.tensor_scalar(z[R, :], base, deg[R, 0:1], deg[R, 1:2], ALU.mult, ALU.add))
                dve.scalar_tensor_tensor(lg[R, :], z[R, :], -1.0, z[R, :], ALU.mult, ALU.max).then_inc(s_z, 1)
                link(dve.tensor_copy(first[R, 0:1], raw_d[R, 0:1]))
                link(dve.tensor_copy(first_f[R, :], first[R, :]))
                link(dve.tensor_scalar(off_f[R, 0, :], raw_d[R, :].rearrange("p (j q) -> p j q", q=P)[:, :, 0], first_f[R, 1:2], float(STRIP - TWIN), ALU.subtract, ALU.min))
                link(dve.tensor_scalar(off_f[R, 1, :], off_f[R, 0, :], first_f[R, 1:2], None, ALU.add))
                link(dve.memset(off_i[:, :], 0))
                dve.tensor_copy(off_i[R, :].rearrange("p (b k) -> p b k", b=2)[:, :, 0:HT], off_f[R, 0, :].rearrange("p (b k) -> p b k", b=2)).then_inc(s_off, 1)
                dve.scalar_tensor_tensor(row[R, A_IDX, :], raw_s[R, :], float(T), raw_t[R, :], ALU.mult, ALU.add)
                dve.tensor_scalar(rel, raw_d[R, :], first_f[R, 0:1], None, ALU.subtract)
                dve.tensor_scalar(hi[R, :], raw_s[R, :], 7, None, ALU.arith_shift_right)
                link(dve.tensor_tensor(key.rearrange("p (j q) -> p j q", q=P), raw_d[R, :].rearrange("p (j q) -> p j q", q=P),
                                       off_f[R, 1, :].rearrange("p (j o) -> p j o", o=1).to_broadcast([ROWS, JT, P]), ALU.subtract))
                dve.tensor_reduce(bad[R, 0:1], rel, AX.X, ALU.max)
                dve.tensor_reduce(bad[R, 1:2], key, AX.X, ALU.max)
                dve.tensor_reduce(bad[R, 2:3], rel, AX.X, ALU.min)
                dve.tensor_reduce(bad[R, 3:4], key, AX.X, ALU.min)
                link(dve.tensor_reduce(bad[R, 4:5], off_f[R, 0, :], AX.X, ALU.min))
                dve.tensor_scalar(bad[R, 0:1], bad[R, 0:1], float(WIN - 1), None, ALU.is_gt)
                dve.tensor_scalar(bad[R, 1:2], bad[R, 1:2], float(TWIN - 1), None, ALU.is_gt)
                link(dve.tensor_scalar(bad[R, 2:5], bad[R, 2:5], 0.0, None, ALU.is_lt))
                dve.tensor_reduce(bad[R, 5:6], bad[R, 0:5], AX.X, ALU.add).then_inc(s_bad, 1)
                dve.scalar_tensor_tensor(lo, hi[R, :], float(-P), raw_s[R, :], ALU.mult, ALU.add)
                link(dve.scalar_tensor_tensor(key, hi[R, :], float(TWIN), key, ALU.mult, ALU.add))
                link(dve.tensor_tensor(base, raw_s[R, :], raw_d[R, :], ALU.not_equal))
                link(dve.tensor_tensor(base, base, row[R, A_W, :], ALU.mult))
                dve.wait_ge(s_sp, 1)
                link(dve.scalar_tensor_tensor(z[R, :], z[R, :], 0.0, lg[R, :], ALU.max, ALU.add))
                dve.tensor_tensor(base, base, z[R, :], ALU.mult).then_inc(s_rowready, 1)
                for l in range(2):
                    dve.wait_ge(s_wa, l + 1)
                    n = T * HEADS if l == 0 else T
                    link(dve.tensor_copy((w0, w1)[l][:, T * F:T * F + n], ps_w[2 + l][0:F, 0:n]))
                dve.wait_ge(s_badsum, 1)
                link(dve.tensor_copy(flags[0:1, 0:1], ps_w[0][0:1, 0:1]))
                for q in range(2):
                    dve.sem_inc(s_turned_free[q], 1)
                with dve.Fori(0, JT // 2) as i:
                    for q in range(2):
                        take(dve, s_turned[q])
                        dve.sem_inc(s_turn_free[q], 1)
                        for h in range(2):
                            last = dve.tensor_copy(edge.ap().rearrange("p a (r j) -> p a r j", j=JT)[:, 3 * h:3 * h + 3, 0:ROWS, bass.ds(2 * i + q, 1)].rearrange("p a r j -> p a (r j)"),
                                                   ps_turn[q][:, h * 512:h * 512 + 3 * ROWS].rearrange("p (a r) -> p a r", a=3))
                        last.then_inc(s_turned_free[q], 1)

            @block.tensor
            def _(pe):
                pe.wait_ge(s_id, 4)
                pe.wait_ge(s_wts, 16 * 8)
                for l, w in enumerate((w0, w1)):
                    for t in range(T):
                        last = pe.transpose(ps_w[l][0:F, t * F:(t + 1) * F], w[:, t * F:(t + 1) * F], ident[0:F, 0:F])
                    last.then_inc(s_wt, 1)
                pe.wait_ge(s_asum, 1)
                for l in range(2):
                    pe.wait_ge(s_wtc, l + 1)
                    n = HEADS if l == 0 else 1
                    for t in range(T):
                        rhs = asum[0][:, t, :] if l == 0 else asum[1][:, t:t + 1]
                        last = pe.matmul(ps_w[2 + l][0:F, t * n:(t + 1) * n], wt[l][:, t, :], rhs, start=True, stop=True)
                    last.then_inc(s_wa, 1)
                pe.wait_ge(s_bad, 1)
                pe.matmul(ps_w[0][0:1, 0:1], bad[0:ROWS, 5:6], ones[0:ROWS, :], start=True, stop=True).then_inc(s_badsum, 1)
                with pe.Fori(0, JT // 2) as i:
                    for q in range(2):
                        take(pe, s_turn_in[q])
                        take(pe, s_turned_free[q])
                        for k in range(NA):
                            at = k // 3 * 512 + k % 3 * ROWS
                            last = pe.transpose(ps_turn[q][:, at:at + ROWS], turn[0:ROWS, q, k, :], ident[0:ROWS, 0:ROWS])
                        last.then_inc(s_turned[q], 1)

        def table_phase(layer):
            w, heads = ((w0, HEADS), (w1, 1))[layer]
            natt = T * heads
            ncol = T * F + natt + (F if layer else 0)
            node_in = x_sb if layer == 0 else acc
            with scope() as s2, nc.Block() as block:
                stage = sb(f"stage{layer}", [P, CH * F], F32, s2)
                xt = sb(f"xt{layer}", [F, CH * P], F32, s2)
                prod = sb(f"prod{layer}", [P, CH, T * F + natt], F32, s2)
                lk = sb(f"lk{layer}", [P, CH, natt], F32, s2)
                msg = sb(f"msg{layer}", [P, NT, T * F], F32, s2)
                ps_t = psum(f"ps_t{layer}", [F, 2, 512], s2)
                ps_h = [psum(f"ps_h{layer}{k}", [P, 512], s2) for k in range(4)]
                s_stage, s_xt, s_xt_copied, s_h = (sem(f"{n}{layer}") for n in ("s_stage", "s_xt", "s_xt_copied", "s_h"))
                s_h_free, s_prod, s_lk, s_att, s_msg, s_out = (sem(f"{n}{layer}") for n in ("s_h_free", "s_prod", "s_lk", "s_att", "s_msg", "s_out"))
                s_next, s_skip = sem(f"s_next{layer}"), sem(f"s_skip{layer}")

                @block.vector
                def _(dve):
                    with dve.Fori(0, NCH) as i:
                        dve.tensor_copy(stage[:, :].rearrange("p (c f) -> p c f", f=F), node_in[:, bass.ds(i * CH, CH), :]).then_inc(s_stage, 1)
                        take(dve, s_prod)
                        dve.sem_inc(s_h_free, 1)
                        att = prod[:, :, T * F:T * F + natt]
                        dve.scalar_tensor_tensor(lk[:, :, :], att, SLOPE, att, ALU.mult, ALU.max).then_inc(s_lk, 1)
                        take(dve, s_att)
                        for c in range(CH):
                            o = msg[:, bass.ds(i * CH + c, 1), :]
                            if layer == 0:
                                h = prod[:, c, 0:T * F].rearrange("p (t h d) -> p t d h", t=T, h=HEADS)
                                o = o.rearrange("p c (t d h) -> p (c t) d h", t=T, h=HEADS)
                                g = lk[:, c, :].rearrange("p (t o h) -> p t o h", t=T, o=1).to_broadcast([P, T, HID, HEADS])
                            else:
                                h = prod[:, c, 0:T * F].rearrange("p (t f) -> p t f", t=T)
                                o = o.rearrange("p c (t f) -> p (c t) f", t=T)
                                g = lk[:, c, :].rearrange("p (t o) -> p t o", t=T).to_broadcast([P, T, F])
                            last = dve.tensor_tensor(o, h, g, ALU.mult)
                        last.then_inc(s_msg, 1)

                @block.sync
                def _(sp):
                    rows = tab_l[layer].ap().rearrange("(i p t) f -> p i (t f)", p=P, t=T)
                    with sp.Fori(0, NCH) as i:
                        take(sp, s_msg)
                        sp.sem_inc(s_next, 1)
                        sp.dma_start(rows[:, bass.ds(i * CH, CH), :], msg[:, bass.ds(i * CH, CH), :]).then_inc(s_out, 16)
                    sp.wait_ge(s_out, 16 * NCH)

                @block.tensor
                def _(pe):
                    with pe.Fori(0, NCH) as i:
                        take(pe, s_stage)
                        for c in range(CH):
                            last = pe.transpose(ps_t[:, c // 4, c % 4 * P:(c % 4 + 1) * P], stage[:, c * F:(c + 1) * F], ident[:, :])
                        last.then_inc(s_xt, 1)
                        take(pe, s_xt_copied)
                        for c in range(CH):
                            take(pe, s_h_free)
                            pe.matmul(ps_h[c % 4][:, 0:ncol], xt[:, c * P:(c + 1) * P], w[:, 0:ncol], start=True, stop=True).then_inc(s_h, 1)

                @block.scalar
                def _(act):
                    act.sem_inc(s_h_free, 4)
                    act.sem_inc(s_next, 1)
                    with act.Fori(0, NCH) as i:
                        take(act, s_xt)
                        for k, n in ((0, 4), (1, CH - 4)):
                            last = act.activation(xt[:, k * 4 * P:(k * 4 + n) * P], ps_t[:, k, 0:n * P], ACT.Copy)
                        last.then_inc(s_xt_copied, 1)
                        take(act, s_next)
                        for c in range(CH):
                            take(act, s_h)
                            if layer:
                                act.activation(skip[:, bass.ds(i * CH + c, 1), :].rearrange("p c f -> p (c f)"), ps_h[c % 4][:, T * F + natt:ncol], ACT.Copy)
                            act.activation(prod[:, c, :], ps_h[c % 4][:, 0:T * F + natt], ACT.Copy).then_inc(s_prod if c == CH - 1 else s_h_free, 1)
                        take(act, s_lk)
                        act.activation(lk[:, :, :], lk[:, :, :], ACT.Sigmoid).then_inc(s_att, 1)

        def general_edges(n):
            with scope() as s5, nc.Block() as block:
                raw = [sb(f"graw{n}{k}", [P, ROWLEN], I32, s5) for k in range(2)]
                rowf = sb(f"growf{n}", [P, 2, ROWLEN], F32, s5)
                zeros = sb(f"gzeros{n}", [P, TAB // P * F], F32, s5)
                turn = sb(f"gturn{n}", [P, 2, P], F32, s5)
                ps = psum(f"gps{n}", [P, 512], s5)
                s_pad, s_rows, s_f, s_z, s_zd = (sem(f"g_{k}{n}") for k in ("pad", "rows", "f", "z", "zd"))
                s_in, s_out, s_back = (sem(f"g_{k}{n}") for k in ("in", "out", "back"))

                @block.vector
                def _(dve):
                    dve.memset(raw[0][96:ROWS, :], PAD_SRC).then_inc(s_pad, 1)
                    dve.memset(raw[1][96:ROWS, :], PAD_DST).then_inc(s_pad, 1)
                    dve.memset(zeros[:, :], 0.0).then_inc(s_z, 1)
                    dve.wait_ge(s_rows, 64)
                    dve.tensor_copy(rowf[0:ROWS, 0, :], raw[0][0:ROWS, :])
                    dve.tensor_copy(rowf[0:ROWS, 1, :], raw[1][0:ROWS, :]).then_inc(s_f, 1)
                    with dve.Fori(0, JT) as i:
                        take(dve, s_out)
                        for k, arr in enumerate((A_SRC, A_DST)):
                            last = dve.tensor_copy(edge.ap().rearrange("p a (r j) -> p a r j", j=JT)[:, arr, 0:ROWS, bass.ds(i, 1)].rearrange("p r j -> p (r j)"),
                                                   ps[:, k * ROWS:(k + 1) * ROWS])
                        last.then_inc(s_back, 1)

                @block.scalar
                def _(act):
                    act.wait_ge(s_f, 1)
                    act.sem_inc(s_back, 1)
                    with act.Fori(0, JT) as i:
                        take(act, s_back)
                        act.activation(turn[0:ROWS, :, :], rowf[0:ROWS, :, bass.ds(i * P, P)], ACT.Copy).then_inc(s_in, 1)

                @block.tensor
                def _(pe):
                    with pe.Fori(0, JT) as i:
                        take(pe, s_in)
                        for k in range(2):
                            last = pe.transpose(ps[:, k * ROWS:(k + 1) * ROWS], turn[0:ROWS, k, :], ident[0:ROWS, 0:ROWS])
                        last.then_inc(s_out, 1)

                @block.gpsimd
                def _(pool):
                    pool.wait_ge(s_z, 1)

                @block.sync
                def _(sp):
                    sp.wait_ge(s_pad, 2)
                    for k, name in enumerate(("src", "dst")):
                        sp.dma_start(raw[k][0:FULLROWS, :], A[name][0:FULLROWS * ROWLEN].rearrange("(p n) -> p n", n=ROWLEN)).then_inc(s_rows, 16)
                        sp.dma_start(raw[k][FULLROWS:ROWS, 0:TAIL], A[name][FULLROWS * ROWLEN:EDGES].rearrange("(p n) -> p n", p=1)).then_inc(s_rows, 16)
                    sp.wait_ge(s_z, 1)
                    for t in sums[n]:
                        sp.dma_start(t.ap().rearrange("(p n) f -> p (n f)", p=P), zeros[:, :]).then_inc(s_zd, 16)
                    sp.wait_ge(s_zd, 16 * BT)

        def edge_phase(n, tabs, width, key, tables):
            ng = len(tabs)
            with scope() as s3, nc.Block() as block:
                idx = sb(f"idx{n}", [P, 2, ng, BT], I32, s3)
                keyf = sb(f"keyf{n}", [P, 2, BT], F32, s3)
                rows = sb(f"rows{n}", [P, 2, ng, BT, width], F32, s3)
                same = sb(f"same{n}", [P, BT, P], F32, s3)
                before = sb(f"before{n}", [P, BT, P], F32, s3)
                dup = sb(f"dup{n}", [P, 3, BT], F32, s3)
                sidx = sb(f"sidx{n}", [P, 2, BT], I32, s3)
                wmsg = sb(f"wmsg{n}", [P, BT, F], F32, s3)
                outm = sb(f"outm{n}", [P, 2, BT, F], F32, s3)
                sc = sb(f"sc{n}", [P, 6, BT], F32, s3)
                ps_key = psum(f"ps_key{n}", [P, BT * P], s3)
                ps_sum = psum(f"ps_sum{n}", [P, BT * F], s3)
                s_idx = [sem(f"s_idx{n}{q}") for q in range(2)]
                s_idx_free = [sem(f"s_idx_free{n}{q}") for q in range(2)]
                s_got = [sem(f"s_got{n}{q}", True) for q in range(2)]
                s_rows_free = [sem(f"s_rows_free{n}{q}") for q in range(2)]
                s_key, s_wm, s_sum = sem(f"s_key{n}"), sem(f"s_wm{n}"), sem(f"s_sum{n}")
                s_keyf, s_key_free = sem(f"s_keyf{n}"), sem(f"s_key_free{n}")
                s_out = sem(f"s_outm{n}")
                s_out_free = [sem(f"s_out_free{n}{q}") for q in range(2)]
                s_add = [sem(f"s_add{n}{k}", True) for k in range(BT)]
                v = sem(f"v_edge{n}")

                @block.gpsimd
                def _(pool):
                    def gather(q, first=False):
                        take(pool, s_idx[q])
                        if not first:
                            take(pool, s_rows_free[q])
                        for g in range(ng):
                            for k in range(BT):
                                pool.indirect_dma_start(rows[:, q, g, k, :], None, tabs[g][0].ap(),
                                                        bass.IndirectOffsetOnAxis(ap=idx[:, q, g, k:k + 1], axis=0)).then_inc(s_got[q], 16)

                    def scatter(q, done=None):
                        take(pool, s_out)
                        for k in range(BT):
                            if done is not None:
                                pool.wait_ge(s_add[k], done).then_inc(s_out_free[1 - q], 1)
                            pool.indirect_dma_start(tables[k].ap(), bass.IndirectOffsetOnAxis(ap=sidx[:, q, k:k + 1], axis=0),
                                                    outm[:, q, k, :], None, compute_op=ALU.add).then_inc(s_add[k], 16)

                    gather(0, True)
                    gather(1, True)
                    scatter(0)
                    with pool.Fori(0, NB // 2 - 1) as i:
                        gather(0)
                        scatter(1, i * 32 + 16)
                        gather(1)
                        scatter(0, i * 32 + 32)
                    scatter(1, 16 * (NB - 1))
                    for k in range(BT):
                        pool.wait_ge(s_add[k], 16 * NB)

                @block.sync
                def _(sp):
                    sp.wait_ge(s_add[0], 16 * NB)

                @block.scalar
                def _(act):
                    for q in range(2):
                        act.sem_inc(s_idx_free[q], 1)
                    with act.Fori(0, NB // 2) as i:
                        for q in range(2):
                            take(act, s_idx_free[q])
                            for g in range(ng):
                                last = act.activation(idx[:, q, g, :], edge[:, tabs[g][1], bass.ds(i * (2 * BT) + q * BT, BT)], ACT.Copy)
                            last.then_inc(s_idx[q], 1)
                            act.activation(keyf[:, q, :], edge[:, key, bass.ds(i * (2 * BT) + q * BT, BT)], ACT.Copy).then_inc(s_keyf, 1)

                @block.tensor
                def _(pe):
                    pe.sem_inc(s_key_free, 1)
                    with pe.Fori(0, NB // 2) as i:
                        for q in range(2):
                            take(pe, s_keyf)
                            take(pe, s_key_free)
                            for k in range(BT):
                                last = pe.matmul(ps_key[:, k * P:(k + 1) * P], keyf[:, q, k:k + 1].to_broadcast([P, P]), ident[:, :],
                                                 start=True, stop=True)
                            last.then_inc(s_key, 1)
                            take(pe, s_wm)
                            for k in range(BT):
                                last = pe.matmul(ps_sum[:, k * F:(k + 1) * F], same[:, k, :], wmsg[:, k, :], start=True, stop=True)
                            last.then_inc(s_sum, 1)

                @block.vector
                def _(dve):
                    def link(ins):
                        ins.then_inc(v, 1)
                        take(dve, v)

                    for q in range(2):
                        dve.sem_inc(s_out_free[q], BT)
                    with dve.Fori(0, NB // 2) as i:
                        for q in range(2):
                            at = i * (2 * BT) + q * BT
                            take(dve, s_key)
                            kq = keyf[:, q, :].rearrange("p (k o) -> p k o", o=1).to_broadcast([P, BT, P])
                            link(dve.tensor_tensor(same[:, :, :], ps_key[:, :].rearrange("p (k c) -> p k c", k=BT), kq, ALU.is_equal))
                            dve.sem_inc(s_key_free, 1)
                            low = lower[:, :].rearrange("p (o c) -> p o c", o=1).to_broadcast([P, BT, P])
                            link(dve.tensor_tensor(before[:, :, :], same[:, :, :], low, ALU.mult))
                            link(dve.tensor_reduce(dup[:, 0, :], before[:, :, :], AX.X, ALU.max))
                            spare = iota_p[:, 0:1].to_broadcast([P, BT])
                            link(dve.tensor_tensor(dup[:, 1, :], spare, keyf[:, q, :], ALU.subtract))
                            link(dve.tensor_tensor(dup[:, 2, :], dup[:, 1, :], dup[:, 0, :], ALU.mult))
                            take(dve, s_out_free[q], BT)
                            link(dve.tensor_tensor(sidx[:, q, :], dup[:, 2, :], keyf[:, q, :], ALU.add))
                            dve.wait_ge(s_got[q], i * (16 * BT * ng) + 16 * BT * ng).then_inc(s_idx_free[q], 1)
                            if n < 2:
                                wq = edge[:, A_W, bass.ds(at, BT)].rearrange("p (k o) -> p k o", o=1).to_broadcast([P, BT, F])
                                dve.tensor_tensor(wmsg[:, :, :], rows[:, q, 0, :, :], wq, ALU.mult).then_inc(s_wm, 1)
                            else:
                                link(dve.tensor_tensor(wmsg[:, :, :], rows[:, q, 0, :, 0:F], rows[:, q, 1, :, 0:F], ALU.mult))
                                link(dve.tensor_reduce(sc[:, 0, :], wmsg[:, :, :], AX.X, ALU.add))
                                link(dve.tensor_tensor(sc[:, 1, :], rows[:, q, 0, :, F], rows[:, q, 1, :, F], ALU.mult))
                                link(dve.tensor_scalar(sc[:, 1, :], sc[:, 1, :], EPS_SIM, None, ALU.max))
                                link(dve.reciprocal(sc[:, 2, :], sc[:, 1, :]))
                                link(dve.tensor_tensor(sc[:, 0, :], sc[:, 0, :], sc[:, 2, :], ALU.mult))
                                link(dve.tensor_scalar(sc[:, 3, :], sc[:, 0, :], 0.0, coeff[:, 0:1], ALU.max, ALU.mult))
                                link(dve.tensor_scalar(sc[:, 4, :], sc[:, 0, :], 0.0, coeff[:, 1:2], ALU.min, ALU.mult))
                                link(dve.tensor_tensor(sc[:, 3, :], sc[:, 3, :], sc[:, 4, :], ALU.add))
                                link(dve.tensor_tensor(sc[:, 5, :], sc[:, 3, :], edge[:, A_BASE, bass.ds(at, BT)], ALU.mult))
                                cq = sc[:, 5, :].rearrange("p (k o) -> p k o", o=1).to_broadcast([P, BT, F])
                                dve.tensor_tensor(wmsg[:, :, :], rows[:, q, 1, :, 0:F], cq, ALU.mult).then_inc(s_wm, 1)
                            take(dve, s_sum)
                            dve.sem_inc(s_rows_free[q], 1)
                            dve.tensor_copy(outm[:, q, :, :], ps_sum[:, :].rearrange("p (k f) -> p k f", k=BT)).then_inc(s_out, 1)

        def general_sums(n):
            with scope() as s6, nc.Block() as block:
                buf = [sb(f"gbuf{n}{k}", [P, NT, F], F32, s6) for k in range(2)]
                s_load, s_used, v = [sem(f"s_load{n}{k}") for k in range(2)], sem(f"s_used{n}"), sem(f"v_sums{n}")

                @block.sync
                def _(sp):
                    for k in range(BT):
                        if k >= 2:
                            sp.wait_ge(s_used, k - 1)
                        sp.dma_start(buf[k % 2][:, :, :], sums[n][k].ap()[0:NPAD, :].rearrange("(i p) f -> p i f", p=P)).then_inc(s_load[k % 2], 16)

                @block.vector
                def _(dve):
                    for k in range(BT):
                        dve.wait_ge(s_load[k % 2], 16 * (k // 2 + 1))
                        if k:
                            dve.wait_ge(s_used, k)
                            dve.tensor_tensor(acc[:, :, :], acc[:, :, :], buf[k % 2][:, :, :], ALU.add).then_inc(s_used, 1)
                        else:
                            dve.tensor_copy(acc[:, :, :], buf[0][:, :, :]).then_inc(s_used, 1)

                for other in (block.scalar, block.tensor, block.gpsimd):
                    other(lambda eng: eng.sem_inc(v, 1))

        def general_path(n):
            general_edges(n)
            tabs = [(tab_l[n], A_IDX)] if n < 2 else [(tab_g, A_SRC), (tab_g, A_DST)]
            edge_phase(n, tabs, F if n < 2 else F + 1, A_DST if n < 2 else A_SRC, sums[n])
            general_sums(n)

        def fast_path(l):
            with ExitStack() as s7:
                sums_t = sb(f"sums_t{l}", [F, NPAD + WIN], F32, s7)
                with scope() as s8, nc.Block() as block:
                    KB = 4
                    AHEAD = KB - 1
                    strip = [sb(f"strip{l}{k}", [P, NT, STRIP], F32, s8) for k in range(2)]
                    turned = [sb(f"turned{l}{k}", [P, 4 * P], F32, s8) for k in range(2)]
                    idx = sb(f"fidx{l}", [P, RB, JT], I32, s8)
                    rows = sb(f"frows{l}", [P, RB, JT, F], F32, s8)
                    hot = sb(f"hot{l}", [P, 2, JT, WIN], F32, s8)
                    hot_lo = sb(f"hot_lo{l}", [P, 2, HT, P], F32, s8)
                    hot_key = sb(f"hot_key{l}", [P, KB, NT * TWIN], F32, s8)
                    zcol = sb(f"zcol{l}", [P, 1], F32, s8)
                    ps_sum = [psum(f"fps_sum{l}{k}", [P, 512], s8) for k in range(2)]
                    ps_b = [psum(f"fps_b{l}{k}", [P, 512], s8) for k in range(KB)]
                    ps_t = [psum(f"fps_t{l}{k}", [P, 512], s8) for k in range(2)]

                    def fs(name):
                        return sem(f"f{l}_{name}")
                    s_idx, s_idx_free, s_rows_free = ([fs(f"{n}{q}") for q in range(RB)] for n in ("idx", "idx_free", "rows_free"))
                    s_got = [sem(f"f{l}_got{q}", True) for q in range(RB)]
                    s_wm, s_agg, s_key, s_b = (fs(n) for n in ("wm", "agg", "key", "b"))
                    s_full, s_zeroed, s_stored = ([fs(f"{n}{k}") for k in range(2)] for n in ("full", "zeroed", "stored"))
                    s_t, s_t_free, s_piece = (fs(n) for n in ("t", "t_free", "piece"))
                    v, v_agg, s_zc = fs("v"), fs("v_agg"), fs("zc")
                    PIECES = [list(range(k, min(k + 4, NT))) for k in range(0, NT, 4)]
                    PER = [PIECES[0:4], PIECES[4:8], PIECES[8:12], PIECES[12:13]]

                    def side(k, piece):
                        return (piece[0] // 4 + (1 - k) * len(PIECES)) % 2

                    @block.gpsimd
                    def _(pool):
                        for q in range(RB):
                            pool.sem_inc(s_rows_free[q], 1)
                        with pool.Fori(0, LOOPS) as i:
                            for u in range(SLOTS):
                                q = u % RB
                                take(pool, s_idx[q])
                                take(pool, s_rows_free[q])
                                for k in range(JT):
                                    pool.indirect_dma_start(rows[:, q, k, :], None, tab_l[l].ap(),
                                                            bass.IndirectOffsetOnAxis(ap=idx[:, q, k:k + 1], axis=0)).then_inc(s_got[q], 16)

                    @block.scalar
                    def _(act):
                        def zero(part, n):
                            return act.activation(part, zcol[:, 0:1].rearrange("p (a b) -> p a b", a=1).to_broadcast([P, n, STRIP]), ACT.Copy)

                        def pieces(k, u):
                            for piece in PER[u]:
                                a, b = piece[0], piece[-1] + 1
                                j = side(k, piece)
                                take(act, s_t)
                                take(act, s_stored[j], 16)
                                act.activation(turned[j][:, 0:(b - a) * P], ps_t[j][:, 0:(b - a) * P], ACT.Copy).then_inc(s_t_free, 1)
                                zero(strip[k][:, a:b, :], b - a).then_inc(s_piece, 1)

                        def indices(u, row):
                            act.activation(idx[:, u % RB, :], edge[:, A_IDX, bass.ds(row * JT, JT)], ACT.Copy).then_inc(s_idx[u % RB], 1)

                        for u in range(RB):
                            indices(u, u)
                        for j in range(2):
                            act.sem_inc(s_stored[j], 16)
                        act.wait_ge(s_zc, 1)
                        zero(strip[0][:, :, :], NT).then_inc(s_zeroed[0], 1)
                        zero(strip[1][:, :, :], NT).then_inc(s_full[1], 1)
                        with act.Fori(0, LOOPS) as i:
                            for u in range(SLOTS):
                                pieces(1 - u // 4, u % 4)
                                take(act, s_idx_free[u % RB])
                                indices(u, i * SLOTS + (u + RB))
                        for u in range(4):
                            pieces(1, u)
                        for j in range(2):
                            take(act, s_stored[j], 16)

                    @block.sync
                    def _(sp):
                        def store(slot, k):
                            for n, piece in enumerate(PIECES):
                                take(sp, s_piece)
                                if n == len(PIECES) - 1:
                                    sp.sem_inc(s_zeroed[k], 1)
                                a, b = piece[0], piece[-1] + 1
                                j = side(k, piece)
                                sp.dma_start(adj.ap()[l, bass.ds(slot, 1), :, a * P:b * P].rearrange("o w n -> (o w) n"), turned[j][:, 0:(b - a) * P]).then_inc(s_stored[j], 16)

                        with sp.Fori(0, LOOPS) as i:
                            store(i * 2, 1)
                            store(i * 2 + 1, 0)
                        store(LOOPS * 2, 1)

                    @block.tensor
                    def _(pe):
                        def turn(k, piece):
                            if piece[0] == 0:
                                take(pe, s_full[k])
                            take(pe, s_t_free)
                            for n, hi in enumerate(piece):
                                last = pe.matmul(ps_t[side(k, piece)][:, n * P:(n + 1) * P], strip[k][:, hi, :], ident[:, :], start=True, stop=True)
                            last.then_inc(s_t, 1)

                        def sum_row(u):
                            take(pe, s_wm)
                            for k in range(JT):
                                last = pe.matmul(ps_sum[u % 2][0:F, 0:WIN], rows[:, u % RB, k, :], hot[:, u % 2, k, :], start=(k == 0), stop=(k == JT - 1))
                            last.then_inc(s_agg, 1)

                        pe.sem_inc(s_t_free, 2)
                        with pe.Fori(0, LOOPS) as i:
                            for u in range(SLOTS):
                                todo = list(PER[u % 4])
                                for k in range(HT):
                                    take(pe, s_key)
                                    pe.matmul(ps_b[(u * HT + k) % KB][:, 0:NT * TWIN], hot_lo[:, u % 2, k, :], hot_key[:, (u * HT + k) % KB, :], start=True, stop=True).then_inc(s_b, 1)
                                    if k == 0 and u > 0:
                                        sum_row(u - 1)
                                    if todo and (k % 2 == 1 or k == HT - 1):
                                        turn(1 - u // 4, todo.pop(0))
                            sum_row(SLOTS - 1)
                        for u in range(4):
                            for piece in PER[u]:
                                turn(1, piece)

                    @block.vector
                    def _(dve):
                        dve.memset(zcol[:, :], 0.0).then_inc(s_zc, 1)
                        dve.memset(sums_t[:, :], 0.0).then_inc(v_agg, 1)
                        dve.sem_inc(v, 1)
                        windows = {}

                        def per_edge(array, at, n, width):
                            return edge[:, array, bass.ds(at, n)].rearrange("p (k o) -> p k o", o=1).to_broadcast([P, n, width])

                        def one_hot(out_ap, array, at, n, width):
                            return dve.tensor_tensor(out_ap, iota_f[:, 0:width].rearrange("p (o c) -> p o c", o=1).to_broadcast([P, n, width]),
                                                     per_edge(array, at, n, width), ALU.is_equal)

                        def key(i, n):
                            at = i * (SLOTS * HT) + (n + l * (ET // 2))
                            dve.tensor_scalar(hot_key[:, n % KB, :], iota_f[:, :], edge[:, A_KEY, bass.ds(at, 1)], edge[:, A_BASE, bass.ds(at, 1)],
                                              ALU.is_equal, ALU.mult).then_inc(s_key, 1)

                        def add_sums(u):
                            take(dve, s_agg)
                            dve.sem_inc(s_rows_free[u % RB], 1)
                            take(dve, v_agg)
                            part = sums_t[:, bass.ds(windows[u], WIN)]
                            dve.tensor_tensor(part, part, ps_sum[u % 2][0:F, 0:WIN], ALU.add).then_inc(v_agg, 1)

                        one_hot(hot_lo[:, 0, :, :], A_LO, l * (ET // 2), HT, P)
                        for n in range(AHEAD):
                            key(0, n)
                        with dve.Fori(0, LOOPS) as i:
                            for u in range(SLOTS):
                                row = i * SLOTS + u
                                _, (windows[u],) = nc.values_load_multi_w_load_instructions(firsts[0:1, bass.ds(2 * row, 1)], engines=[DVE], min_val=0, max_val=NODES - 1, skip_runtime_bounds_check_because="the windows were checked")
                                e = i * (SLOTS * 8) + (u * 8 + l * ROWS * 8)
                                _, offv = nc.values_load_multi_w_load_instructions(offs[0:1, bass.ds(e, HT)], engines=[DVE], min_val=0, max_val=STRIP - TWIN, skip_runtime_bounds_check_because="the windows were checked")
                                one_hot(hot_lo[:, (u + 1) % 2, :, :], A_LO, i * (SLOTS * HT) + ((u + 1) * HT + l * (ET // 2)), HT, P)
                                st = u // 4
                                if u % 4 == 0:
                                    take(dve, s_zeroed[st])
                                for k in range(HT):
                                    n = u * HT + k
                                    take(dve, s_b)
                                    take(dve, v)
                                    part = strip[st][:, :, bass.ds(offv[k], TWIN)]
                                    dve.tensor_tensor(part, part, ps_b[n % KB][:, 0:NT * TWIN].rearrange("p (h w) -> p h w", w=TWIN), ALU.add).then_inc(v, 1)
                                    key(i, n + AHEAD)
                                    if k == 2:
                                        one_hot(hot[:, u % 2, :, :], A_REL, row * JT, JT, WIN)
                                    if k == 3 and u > 0:
                                        add_sums(u - 1)
                                if u % 4 == 3:
                                    take(dve, v)
                                    dve.sem_inc(s_full[st], 1)
                                    dve.sem_inc(v, 1)
                                dve.wait_ge(s_got[u % RB], i * (SLOTS // RB * JT * 16) + (u // RB + 1) * JT * 16).then_inc(s_idx_free[u % RB], 1)
                                dve.tensor_tensor(rows[:, u % RB, :, :], rows[:, u % RB, :, :], per_edge(A_W, row * JT, JT, F), ALU.mult).then_inc(s_wm, 1)
                            add_sums(SLOTS - 1)
                        take(dve, v_agg)
                        take(dve, v)

                turn_back(f"l{l}", sums_t, F, ident[0:F, 0:F])

        def turn_back(name, cols, k, eye):
            with scope() as s9, nc.Block() as block:
                stage = sb(f"tb_{name}", [P, CH * P], F32, s9)
                ps = psum(f"tbp_{name}", [P, 512], s9)
                s_in, s_out, s_free, s_sp = (sem(f"tb_{name}_{n}") for n in ("in", "out", "free", "sp"))

                @block.gpsimd
                def _(pool):
                    pool.sem_inc(s_sp, 1)

                @block.sync
                def _(sp):
                    sp.wait_ge(s_sp, 1)

                @block.scalar
                def _(act):
                    with act.Fori(0, NCH) as i:
                        take(act, s_out)
                        act.activation(acc[:, bass.ds(i * CH, CH), :], ps[:, 0:CH * F].rearrange("p (c f) -> p c f", f=F), ACT.Copy).then_inc(s_free, 1)

                @block.vector
                def _(dve):
                    dve.sem_inc(s_free, 1)
                    with dve.Fori(0, NCH) as i:
                        take(dve, s_free)
                        dve.tensor_copy(stage[0:k, :], cols[0:k, bass.ds(i * (CH * P), CH * P)]).then_inc(s_in, 1)

                @block.tensor
                def _(pe):
                    with pe.Fori(0, NCH) as i:
                        take(pe, s_in)
                        for c in range(CH):
                            last = pe.matmul(ps[:, c * F:(c + 1) * F], stage[0:k, c * P:(c + 1) * P], eye, start=True, stop=True)
                        last.then_inc(s_out, 1)

        def flag(n):
            return nc.values_load(flags[0:1, n:n + 1], min_val=0, max_val=1 << 20)

        def aggregate(l):
            with nc.If(flag(0) == 0):
                fast_path(l)
            with nc.Else():
                general_path(l)

        def bc_n(ap):
            return ap.rearrange("p (i o) -> p i o", o=1).to_broadcast([P, NT, F])

        def bc_f(ap):
            return ap.rearrange("p (o f) -> p o f", o=1).to_broadcast([P, NT, F])

        def layer_norm(dve, link, s_var, s_std, out_ap, src, tmp):
            link(dve.tensor_reduce(mom[:, 0, :], src[:, :, :], AX.X, ALU.add))
            link(dve.tensor_scalar(mom[:, 0, :], mom[:, 0, :], 1.0 / F, None, ALU.mult))
            link(dve.tensor_tensor(src[:, :, :], src[:, :, :], bc_n(mom[:, 0, :]), ALU.subtract))
            link(dve.tensor_tensor(tmp[:, :, :], src[:, :, :], src[:, :, :], ALU.mult))
            link(dve.tensor_reduce(mom[:, 1, :], tmp[:, :, :], AX.X, ALU.add))
            dve.tensor_scalar(mom[:, 1, :], mom[:, 1, :], 1.0 / F, EPS_LN, ALU.mult, ALU.add).then_inc(s_var, 1)
            dve.wait_ge(s_std, 1)
            link(dve.reciprocal(mom[:, 3, :], mom[:, 2, :]))
            return dve.tensor_tensor(out_ap, src[:, :, :], bc_n(mom[:, 3, :]), ALU.mult)

        table_phase(0)
        aggregate(0)

        with scope() as s10, nc.Block() as block:
            nbuf = [sb(f"elu{k}", [P, NT, F], F32, s10) for k in range(2)]
            v, s_low, s_exp = sem("v_elu"), sem("s_low"), sem("s_exp")

            @block.scalar
            def _(act):
                act.wait_ge(s_low, 1)
                act.activation(nbuf[0][:, :, :], nbuf[0][:, :, :], ACT.Exp).then_inc(s_exp, 1)

            @block.vector
            def _(dve):
                dve.tensor_scalar(nbuf[0][:, :, :], acc[:, :, :], 0.0, None, ALU.min).then_inc(s_low, 1)
                dve.tensor_scalar(nbuf[1][:, :, :], acc[:, :, :], 0.0, -1.0, ALU.max, ALU.add).then_inc(v, 1)
                dve.wait_ge(v, 1)
                dve.wait_ge(s_exp, 1)
                dve.tensor_tensor(acc[:, :, :], nbuf[0][:, :, :], nbuf[1][:, :, :], ALU.add).then_inc(v, 1)
                dve.wait_ge(v, 2)

        table_phase(1)
        aggregate(1)

        with ExitStack() as s4:
          unit_t = sb("unit_t", [P, NGPAD], F32, s4)
          with scope() as s11, nc.Block() as block:
            v, s_var, s_std = sem("v_n1"), sem("s_var1"), sem("s_std1")
            s_stage, s_xt, s_xtc, s_wh, s_sq, s_nrm, s_tab, s_wide, s_pad = (sem(k) for k in ("s_stage2", "s_xt2", "s_xtc2", "s_wh", "s_sq", "s_nrm", "s_tab", "s_wide", "s_pad2"))
            s_min, s_minT, s_u, s_ut, s_utc = (sem(k) for k in ("s_min", "s_minT", "s_u", "s_ut", "s_utc"))
            stage = sb("stage2", [P, CH * F], F32, s11)
            stage2 = sb("stage3", [P, CH, 2, F], F32, s11)
            xt = sb("xt2", [F, CH * P], F32, s11)
            wide = sb("wide", [P, NT, F + 1], F32, s11)
            tmp = sb("tmp2", [P, NT, F], F32, s11)
            nrm = sb("nrm", [P, NT], F32, s11)
            low = sb("low", [P, 2], F32, s11)
            ps_t = psum("ps_t2", [P, 2, 512], s11)
            ps_h = psum("ps_h2", [P, 512], s11)

            @block.gpsimd
            def _(pool):
                pool.memset(nrm[:, :], 1.0).then_inc(s_pad, 1)
                pool.memset(unit_t[:, NPAD:NGPAD], 0.0).then_inc(s_pad, 1)

            @block.sync
            def _(sp):
                sp.wait_ge(s_wide, 1)
                sp.dma_start(wh_rows.ap()[0:NPAD, :].rearrange("(i p) f -> p i f", p=P), skip[:, :, :]).then_inc(s_tab, 16)
                sp.dma_start(wh_rows.ap()[NPAD:NGPAD, :].rearrange("(i p) f -> p i f", p=P), skip[:, 0:1, :]).then_inc(s_tab, 16)
                sp.wait_ge(s_nrm, 1)
                sp.dma_start(tab_g.ap().rearrange("(i p) f -> p i f", p=P), wide[:, :, :]).then_inc(s_tab, 16)
                sp.wait_ge(s_tab, 48)

            @block.scalar
            def _(act):
                act.wait_ge(s_var, 1)
                act.activation(mom[:, 2, :], mom[:, 1, :], ACT.Sqrt).then_inc(s_std, 1)
                with act.Fori(0, NCH) as i:
                    take(act, s_xt)
                    for k, m in ((0, 4), (1, CH - 4)):
                        last = act.activation(xt[:, k * 4 * P:(k * 4 + m) * P], ps_t[0:F, k, 0:m * P], ACT.Copy)
                    last.then_inc(s_xtc, 1)
                act.wait_ge(s_sq, 1)
                act.activation(wide[:, :, F], mom[:, 0, :], ACT.Sqrt).then_inc(s_nrm, 1)
                with act.Fori(0, NCH) as i:
                    take(act, s_ut)
                    for k, m in ((0, 4), (1, CH - 4)):
                        last = act.activation(unit_t[:, bass.ds(i * (CH * P) + k * 4 * P, m * P)], ps_t[:, k, 0:m * P], ACT.Copy)
                    last.then_inc(s_utc, 1)

            @block.tensor
            def _(pe):
                with pe.Fori(0, NCH) as i:
                    take(pe, s_stage)
                    for c in range(CH):
                        last = pe.transpose(ps_t[0:F, c // 4, c % 4 * P:(c % 4 + 1) * P], stage[:, c * F:(c + 1) * F], ident[:, :])
                    last.then_inc(s_xt, 1)
                    take(pe, s_xtc)
                    for c in range(CH):
                        last = pe.matmul(ps_h[:, c * F:(c + 1) * F], xt[:, c * P:(c + 1) * P], w2[:, :], start=True, stop=True)
                    last.then_inc(s_wh, 1)
                pe.wait_ge(s_min, 1)
                pe.matmul(ps_h[0:1, 0:1], low[:, 1:2], ones[:, :], start=True, stop=True).then_inc(s_minT, 1)
                with pe.Fori(0, NCH) as i:
                    take(pe, s_u)
                    for c in range(CH):
                        last = pe.transpose(ps_t[:, c // 4, c % 4 * P:(c % 4 + 1) * P], stage2[:, c, :, :].rearrange("p a f -> p (a f)"), ident[:, :])
                    last.then_inc(s_ut, 1)

            @block.vector
            def _(dve):
                def link(ins):
                    ins.then_inc(v, 1)
                    take(dve, v)
                link(dve.tensor_tensor(acc[:, :, :], acc[:, :, :], skip[:, :, :], ALU.add))
                link(dve.tensor_tensor(acc[:, :, :], acc[:, :, :], bc_f(bres[:, :]), ALU.add))
                link(dve.tensor_tensor(acc[:, :, :], acc[:, :, :], x_sb[:, :, :], ALU.add))
                link(layer_norm(dve, link, s_var, s_std, x_sb[:, :, :], acc, tmp))
                with dve.Fori(0, NCH) as i:
                    dve.tensor_copy(stage[:, :].rearrange("p (c f) -> p c f", f=F), x_sb[:, bass.ds(i * CH, CH), :]).then_inc(s_stage, 1)
                    take(dve, s_wh)
                    b7 = b2[:, :].rearrange("p (o f) -> p o f", o=1).to_broadcast([P, CH, F])
                    link(dve.tensor_tensor(skip[:, bass.ds(i * CH, CH), :], ps_h[:, 0:CH * F].rearrange("p (c f) -> p c f", f=F), b7, ALU.add))
                dve.tensor_copy(wide[:, :, 0:F], skip[:, :, :]).then_inc(s_wide, 1)
                link(dve.tensor_tensor(tmp[:, :, :], skip[:, :, :], skip[:, :, :], ALU.mult))
                dve.tensor_reduce(mom[:, 0, :], tmp[:, :, :], AX.X, ALU.add).then_inc(s_sq, 1)
                dve.wait_ge(s_nrm, 1)
                dve.wait_ge(s_pad, 2)
                dve.tensor_copy(nrm[:, 0:NT - 1], wide[:, 0:NT - 1, F])
                link(dve.tensor_copy(nrm[0:LAST, NT - 1:NT], wide[0:LAST, NT - 1:NT, F]))
                link(dve.tensor_reduce(low[:, 0:1], nrm[:, :], AX.X, ALU.min))
                dve.tensor_scalar(low[:, 1:2], low[:, 0:1], 2.0 * EPS_SIM ** 0.5, None, ALU.is_lt).then_inc(s_min, 1)
                link(dve.tensor_scalar(mom[:, 1, :], wide[:, :, F], TINY, None, ALU.max))
                link(dve.reciprocal(mom[:, 2, :], mom[:, 1, :]))
                link(dve.tensor_tensor(tmp[:, :, :], skip[:, :, :], bc_n(mom[:, 2, :]), ALU.mult))
                dve.wait_ge(s_minT, 1)
                link(dve.scalar_tensor_tensor(flags[0:1, 1:2], ps_h[0:1, 0:1], 1.0, flags[0:1, 0:1], ALU.mult, ALU.add))
                dve.sem_inc(s_utc, 1)
                with dve.Fori(0, NCH) as i:
                    take(dve, s_utc)
                    dve.tensor_copy(stage2[:, :, :, :], tmp[:, bass.ds(i * CH, CH), :].rearrange("p c (o f) -> p c o f", o=1).to_broadcast([P, CH, 2, F])).then_inc(s_u, 1)
                take(dve, s_utc)

          def dense_path():
            with ExitStack() as s12:
                out_t = sb("out_t", [P, NPAD], F32, s12)
                unit_g = sb("unit_g", [P, PAIRS, STRIP], F32, s12)
                wh_g = sb("wh_g", [P, GROUPS, F], F32, s12)
                unit_s = sb("unit_s", [P, 2, SB], F32, s12)
                NBUF = 7
                adj_b = edge.ap().rearrange("p a e -> p (a e)")[:, 0:NBUF * 2 * SB].rearrange("p (k g n) -> p k g n", k=NBUF, g=2)
                LAG = 3
                CB = LAG + 1
                pos = sb("pos", [P, 2, 2, SB], F32, s12)
                con = sb("con", [P, CB, 2, SB], F32, s12)
                with scope() as s13, nc.Block() as block:
                    ps_c = [psum(f"ps_c{k}", [P, 2, 512], s13) for k in range(2)]
                    ps_o = psum("ps_o", [P, 512], s13)
                    s_whg, s_ug, s_us, s_us_free, s_c, s_pos, s_blend, s_con, s_o, s_o_free = (
                        sem(f"d_{n}") for n in ("whg", "ug", "us", "us_free", "c", "pos", "blend", "con", "o", "o_free"))
                    s_us0 = sem("d_us0")
                    s_adj = [sem(f"d_adj{k}") for k in range(NBUF)]
                    s_adj_free = [sem(f"d_adj_free{k}") for k in range(NBUF)]

                    @block.sync
                    def _(sp):
                        with sp.Fori(0, GROUPS) as g:
                            at = nc.values_load(firsts[0:1, bass.ds(4 * g + 1, 1)], engines=[SP], min_val=0, max_val=NODES - 1, skip_runtime_bounds_check_because="dst is below the number of nodes")
                            sp.dma_start(wh_g[:, bass.ds(g, 1), :], wh_rows.ap()[bass.ds(at, STRIP), :].rearrange("p (o f) -> p o f", o=1)).then_inc(s_whg, 16)
                        for k in range(NBUF):
                            sp.sem_inc(s_adj_free[k], 1)
                        half = GROUPS // 2
                        with sp.Fori(0, NSB) as b:
                            for p in range(PAIRS):
                                g = 2 * p
                                take(sp, s_adj_free[p % NBUF])
                                sp.dma_start(adj_b[:, p % NBUF, :, :], adj.ap()[g // half, g % half + 1:g % half + 3, :, bass.ds(b * SB, SB)].rearrange("g w n -> w g n")).then_inc(s_adj[p % NBUF], 16)

                    @block.gpsimd
                    def _(pool):
                        with pool.Fori(0, PAIRS) as p:
                            for h in range(2):
                                at = nc.values_load(firsts[0:1, bass.ds(8 * p + (4 * h + 1), 1)], engines=[POOL], min_val=0, max_val=NODES - 1, skip_runtime_bounds_check_because="dst is below the number of nodes")
                                pool.tensor_copy(unit_g[h * F:(h + 1) * F, bass.ds(p, 1), :].rearrange("p o w -> p (o w)"), unit_t[h * F:(h + 1) * F, bass.ds(at, STRIP)]).then_inc(s_ug, 1)
                        pool.wait_ge(s_ug, GROUPS)
                        with pool.Fori(1, NSB) as b:
                            take(pool, s_us_free)
                            for h in range(2):
                                pool.tensor_copy(unit_s[h * F:(h + 1) * F, h, :], unit_t[h * F:(h + 1) * F, bass.ds(b * SB, SB)]).then_inc(s_us, 1)

                    @block.tensor
                    def _(pe):
                        def cosines(b, p, first):
                            if p == 0:
                                take(pe, s_us, 2)
                            if first:
                                pe.wait_ge(s_ug, 2 * (p + 1))
                            if not first or p >= 2:
                                pe.wait_ge(s_blend, b * PAIRS + (p - 1))
                            for h in range(2):
                                last = pe.matmul(ps_c[p % 2][:, h, 0:SB], unit_g[:, p, :], unit_s[:, h, :], start=True, stop=True)
                            last.then_inc(s_c, 1)

                        def product(p):
                            if p == 0:
                                take(pe, s_o_free)
                            take(pe, s_con)
                            for h in range(2):
                                last = pe.matmul(ps_o[h * F:(h + 1) * F, 0:SB], wh_g[:, 2 * p + h, :], con[:, p % CB, h, :],
                                                 start=(p == 0), stop=(p == PAIRS - 1), skip_group_check=True)
                            last.then_inc(s_adj_free[p % NBUF] if p < PAIRS - 1 else s_o, 1)

                        def block_of_sources(b, first=False):
                            for p in range(PAIRS):
                                cosines(b, p, first)
                                if p >= LAG:
                                    if first and p == LAG:
                                        pe.wait_ge(s_whg, 16 * GROUPS)
                                    product(p - LAG)
                                elif not first:
                                    product(PAIRS + p - LAG)

                        pe.sem_inc(s_o_free, 1)
                        block_of_sources(0, True)
                        with pe.Fori(1, NSB) as b:
                            block_of_sources(b)
                        for p in range(PAIRS - LAG, PAIRS):
                            product(p)

                    @block.scalar
                    def _(act):
                        def keep(b):
                            take(act, s_o)
                            act.sem_inc(s_adj_free[(PAIRS - 1) % NBUF], 1)
                            act.activation(out_t[:, bass.ds(b * SB, SB)], ps_o[:, 0:SB], ACT.Copy).then_inc(s_o_free, 1)

                        def positive(b, first=False):
                            for p in range(PAIRS):
                                take(act, s_c)
                                act.activation(pos[:, p % 2, :, :], ps_c[p % 2][:, :, 0:SB], ACT.Relu, scale=coeff[:, 4:5]).then_inc(s_pos, 1)
                                if p == LAG - 1 and not first:
                                    keep(b - 1)
                            act.sem_inc(s_us_free, 1)

                        for h in range(2):
                            act.wait_ge(s_us0, 1)
                            act.activation(unit_s[h * F:(h + 1) * F, h, :], unit_t[h * F:(h + 1) * F, 0:SB], ACT.Copy).then_inc(s_us, 1)
                        positive(0, True)
                        with act.Fori(1, NSB) as b:
                            positive(b)
                        keep(NSB - 1)
                        take(act, s_o_free)

                    @block.vector
                    def _(dve):
                        def blend(p):
                            take(dve, s_pos)
                            dve.scalar_tensor_tensor(con[:, p % CB, :, :], ps_c[p % 2][:, :, 0:SB], coeff[:, 5:6], pos[:, p % 2, :, :], ALU.mult, ALU.add).then_inc(s_blend, 1)

                        def weigh(p, b):
                            dve.wait_ge(s_blend, b * PAIRS + (p + 1))
                            dve.wait_ge(s_adj[p % NBUF], b * (16 * PAIRS // NBUF) + (p // NBUF + 1) * 16)
                            dve.tensor_tensor(con[:, p % CB, :, :], con[:, p % CB, :, :], adj_b[:, p % NBUF, :, :], ALU.mult).then_inc(s_con, 1)

                        dve.memset(unit_s[:, :, :], 0.0).then_inc(s_us0, 1)
                        with dve.Fori(0, NSB) as b:
                            blend(0)
                            for p in range(PAIRS):
                                if p < PAIRS - 1:
                                    blend(p + 1)
                                weigh(p, b)

                turn_back("dense", out_t, P, eye2[:, :])

          with nc.If(flag(1) == 0):
            dense_path()
          with nc.Else():
            general_path(2)
            with scope() as _, nc.Block() as block:
                s_sg, s_o = sem("s_sg"), sem("s_other")

                @block.vector
                def _(dve):
                    dve.tensor_scalar(acc[:, :, :], acc[:, :, :], coeff[:, 6:7], None, ALU.mult).then_inc(s_sg, 1)
                    dve.wait_ge(s_sg, 1)

                for other in (block.scalar, block.tensor, block.gpsimd, block.sync):
                    other(lambda eng: eng.sem_inc(s_o, 1))

        with scope() as s14, nc.Block() as block:
            nbuf = [sb(f"fin{k}", [P, NT, F], F32, s14) for k in range(2)]
            v, s_var, s_std = sem("v_n2"), sem("s_var2"), sem("s_std2")
            s_fin, s_out = sem("s_fin"), sem("s_out")

            @block.sync
            def _(sp):
                sp.wait_ge(s_fin, 1)
                sp.dma_start(out[0:(NT - 1) * P, :].rearrange("(i p) f -> p i f", p=P), nbuf[1][:, 0:NT - 1, :]).then_inc(s_out, 16)
                sp.dma_start(out[(NT - 1) * P:NODES, :], nbuf[1][0:LAST, NT - 1, :]).then_inc(s_out, 16)
                sp.wait_ge(s_out, 32)

            @block.scalar
            def _(act):
                act.wait_ge(s_var, 1)
                act.activation(mom[:, 2, :], mom[:, 1, :], ACT.Sqrt).then_inc(s_std, 1)

            @block.vector
            def _(dve):
                def link(ins):
                    ins.then_inc(v, 1)
                    take(dve, v)
                link(dve.tensor_scalar(acc[:, :, :], acc[:, :, :], coeff[:, 6:7], None, ALU.mult))
                link(dve.scalar_tensor_tensor(acc[:, :, :], skip[:, :, :], coeff[:, 2:3], acc[:, :, :], ALU.mult, ALU.add))
                link(dve.scalar_tensor_tensor(acc[:, :, :], acc[:, :, :], coeff[:, 3:4], x_sb[:, :, :], ALU.mult, ALU.add))
                layer_norm(dve, link, s_var, s_std, nbuf[1][:, :, :], acc, nbuf[0]).then_inc(s_fin, 1)


_INS = ["x", "src", "dst", "edge_type_5", "edge_weight", "edge_weight_n2", "L0_gnn_W0", "L0_gnn_Al0", "L0_gnn_Ar0",
        "L0_gnn_W1", "L0_gnn_Al1", "L0_gnn_Ar1", "L0_gnn_Wres", "L0_gnn_bres", "L1_gnn_W", "L1_gnn_b",
        "L1_gnn_deg_coeff", "L1_gnn_coeff_param", "L1_gnn_scale_param"]


def kernel(**inputs):
    import numpy as _np
    import concourse.bacc as _bacc
    from concourse import mybir as _mybir
    from concourse.bass_utils import run_bass_kernel_spmd as _run

    nc = _bacc.Bacc("TRN2", target_bir_lowering=False, num_devices=1)
    arrays, args = {}, {}
    for name in _INS:
        a = _np.ascontiguousarray(inputs[name])
        arrays[f"in_{name}"] = a
        args[name] = nc.dram_tensor(f"in_{name}", a.shape, _mybir.dt.from_np(a.dtype), kind="ExternalInput").ap()
    out = nc.dram_tensor("out", (NODES, F), F32, kind="ExternalOutput").ap()
    build(nc, args, out)
    r = _run(nc, [arrays], core_ids=[0])
    return r.results[0]["out"]
```

```python
from contextlib import ExitStack, contextmanager

import concourse.bass as bass
from concourse import mybir

F32 = mybir.dt.float32
I32 = mybir.dt.int32
ALU = mybir.AluOpType
ACT = mybir.ActivationFunctionType
AX = mybir.AxisListType
DVE, POOL, SP = mybir.EngineType.DVE, mybir.EngineType.Pool, mybir.EngineType.SP

P = 128
F = 64
T = 5
HEADS = 8
HID = F // HEADS
SLOPE = 0.2
EPS_LN = 1e-5
EPS_SIM = 1e-8

NODES = 6250
NT = -(-NODES // P)
NPAD = NT * P
LAST = NODES - (NT - 1) * P
EDGES = 200000
ROWS = 112
JT = 14
ROWLEN = JT * P
ET = ROWS * JT
FULLROWS = EDGES // ROWLEN
TAIL = EDGES - FULLROWS * ROWLEN
PAD_SRC = NPAD - 1
PAD_DST = NODES - 1

WIN = 80
STRIP = P
TWIN = 8
GROUPS = ROWS // 2
NGPAD = NPAD + P
LOOPS = 14
SLOTS = ROWS // LOOPS
RB = 4
HT = JT // 2
SB = 448
NSB = NPAD // SB
PAIRS = GROUPS // 2

BT = 8
NB = ET // BT
TAB = NPAD + P
CH = 7
NCH = NT // CH
A_IDX, A_W, A_BASE, A_REL, A_LO, A_KEY = range(6)
A_DST, A_SRC = A_REL, A_LO
NA = 6
TINY = 1e-30


def take(eng, sem, n=1):
    eng.wait_ge(sem, n).then_inc(sem, -n)


def build(nc, A, out):
    ctx = ExitStack()
    with ctx:
        scopes = []

        def sem(name, keep=False):
            if keep or not scopes:
                return ctx.enter_context(nc.semaphore(name))
            s = nc.alloc_semaphore(name)
            scopes[-1].append(s)
            return s

        @contextmanager
        def scope():
            scopes.append([])
            with ExitStack() as stack:
                yield stack
            sems = sorted(scopes.pop(), key=lambda s: s.num)
            run = 0
            for k in range(1, len(sems) + 1):
                if k == len(sems) or sems[k].num != sems[k - 1].num + 1:
                    nc.gpsimd.sem_clear(range(sems[run].num, sems[k - 1].num + 1))
                    run = k
            nc.all_engine_barrier()
            for s in sems:
                nc.release_semaphore(s)

        def sb(name, shape, dt=F32, c=ctx):
            return c.enter_context(nc.sbuf_tensor(name, shape, dt))

        def psum(name, shape, c=ctx):
            return c.enter_context(nc.psum_tensor(name, shape, F32))

        ident = sb("ident", [P, P])
        lower = sb("lower", [P, P])
        iota_p = sb("iota_p", [P, 1])
        iota_f = sb("iota_f", [P, NT * TWIN])
        edge = sb("edge", [P, NA, ET + RB * JT])
        x_sb = sb("x_sb", [P, NT, F])
        sums_t = sb("sums_t", [P, NPAD + WIN])
        feat = sums_t[0:F, :]
        skip = sb("skip", [P, NT, F])
        acc = sb("acc", [P, NT, F])
        w0 = sb("w0", [P, T * F + T * HEADS])
        w1 = sb("w1", [P, T * F + T + F])
        w2 = sb("w2", [P, F])
        bres = sb("bres", [P, F])
        b2 = sb("b2", [P, F])
        deg = sb("deg", [P, 2])
        coeff = sb("coeff", [P, 8])
        mom = sb("mom", [P, 4, NT])
        offs = sb("offs", [1, 2 * ROWS * 8], I32)
        firsts = sb("firsts", [1, 2 * ROWS], I32)
        flags = sb("flags", [1, 2], I32)
        ones = sb("ones", [P, 1])
        eye2 = sb("eye2", [P, F])

        tab_l = [nc.dram_tensor(f"messages{l}", [NPAD * T, F], F32) for l in range(2)]
        tab_g = nc.dram_tensor("wh_norm", [NPAD, F + 1], F32)
        offs_d = nc.dram_tensor("offs_d", [ROWS, 16], I32)
        firsts_d = nc.dram_tensor("firsts_d", [ROWS, 2], I32)
        adj = nc.dram_tensor("adj", [2, GROUPS // 2 + 1, P, NPAD], F32)
        wh_rows = nc.dram_tensor("wh_rows", [NGPAD, F], F32)
        sums = [[nc.dram_tensor(f"sums{l}_{k}", [TAB, F], F32) for k in range(BT)] for l in range(3)]

        def chunks(eng, ahead, work):
            ahead(0, 0)
            with eng.Fori(0, NCH // 2) as i:
                for q in range(2):
                    ahead(2 * i + (q + 1), 1 - q)
                    work(2 * i + q, q)
            work(NCH - 1, 0)

        def nothing(c, q):
            pass

        with scope() as s1, nc.Block() as block:
            raw_s, raw_d, raw_t = (sb(n, [P, ROWLEN], I32, s1) for n in ("raw_s", "raw_d", "raw_t"))
            row = sb("row", [P, NA, ROWLEN], F32, s1)
            hi = sb("hi", [P, ROWLEN], I32, s1)
            z, lg = (buf.ap().rearrange("p i f -> p (i f)")[:, 0:ROWLEN] for buf in (acc, skip))
            first = sb("first", [P, 2], I32, s1)
            first_f = sb("first_f", [P, 2], F32, s1)
            off_f = sb("off_f", [P, 2, JT], F32, s1)
            off_i = sb("off_i", [P, 16], I32, s1)
            bad = sb("bad", [P, 8], F32, s1)
            turn = sb("turn", [P, 2, NA, P], F32, s1)
            al, ar, wt = ([buf.ap().rearrange("p i f -> p (i f)")[0:F, ROWLEN + k * T * F:ROWLEN + (k + 1) * T * F].rearrange("k (t n) -> k t n", t=T) for k in ks]
                          for buf, ks in ((acc, (0, 1)), (acc, (2, 3)), (skip, (0, 1))))
            xs = [sb(f"xs{q}", [P, CH * F], F32, s1) for q in range(2)]
            asum = [sb("asum0", [F, T, HEADS], F32, s1), sb("asum1", [F, T], F32, s1)]
            cin = sb("cin", [P, 4], F32, s1)
            csm = sb("csm", [P, 8], F32, s1)
            ps_turn = [psum(f"ps_turn{k}", [P, 1024], s1) for k in range(2)]
            ps_w = [psum(f"ps_w{k}", [P, 512], s1) for k in range(4)]
            s_pad, s_x, s_rows, s_first, s_wts, s_small = (sem(n) for n in ("s_pad", "s_x", "s_rows", "s_first", "s_wts", "s_small"))
            s_id, s_idm, s_off, s_offd, s_offl = (sem(n) for n in ("s_id", "s_idm", "s_off", "s_offd", "s_offl"))
            v, a = sem("v_chain"), sem("a_chain")
            s_z, s_sp, s_rowready, s_bad, s_badsum = (sem(n) for n in ("s_z", "s_sp", "s_rowready", "s_bad", "s_badsum"))
            s_turn_in = [sem(f"s_turn_in{k}") for k in range(2)]
            s_turn_free = [sem(f"s_turn_free{k}") for k in range(2)]
            s_turned = [sem(f"s_turned{k}") for k in range(2)]
            s_turned_free = [sem(f"s_turned_free{k}") for k in range(2)]
            s_xs, s_xturned, s_xkept = sem("s_xs"), sem("s_xturned"), sem("s_xkept")
            s_wt, s_wtc, s_asum, s_wa, s_csm = sem("s_wt"), sem("s_wtc"), sem("s_asum"), sem("s_wa"), sem("s_csm")

            @block.sync
            def _(sp):
                sp.wait_ge(s_pad, 6)
                sp.dma_start(x_sb[:, 0:NT - 1, :], A["x"][0:(NT - 1) * P, :].rearrange("(i p) f -> p i f", p=P)).then_inc(s_x, 16)
                sp.dma_start(x_sb[0:LAST, NT - 1, :], A["x"][(NT - 1) * P:NODES, :]).then_inc(s_x, 16)
                for dst, src in ((raw_s, A["src"]), (raw_d, A["dst"]), (raw_t, A["edge_type_5"]),
                                 (row[:, A_W, :], A["edge_weight"]), (row[:, A_BASE, :], A["edge_weight_n2"])):
                    sp.dma_start(dst[0:FULLROWS, :], src[0:FULLROWS * ROWLEN].rearrange("(p n) -> p n", n=ROWLEN)).then_inc(s_rows, 16)
                    sp.dma_start(dst[FULLROWS:ROWS, 0:TAIL], src[FULLROWS * ROWLEN:EDGES].rearrange("(p n) -> p n", p=1)).then_inc(s_rows, 16)
                full = (GROUPS - 1) * 2 * ROWLEN
                sp.dma_start(first[0:ROWS - 2, 1:2], A["dst"][0:full].rearrange("(g n) -> g n", n=2 * ROWLEN)[:, 0:1]
                             .rearrange("g (a o) -> g a o", a=1).to_broadcast([GROUPS - 1, 2, 1])).then_inc(s_first, 16)
                sp.dma_start(first[ROWS - 2:ROWS, 1:2], A["dst"][full:full + 1].partition_broadcast(2)).then_inc(s_first, 16)
                sp.wait_ge(s_off, 1)
                sp.dma_start(offs_d.ap(), off_i[0:ROWS, :]).then_inc(s_offd, 16)
                sp.dma_start(firsts_d.ap(), first[0:ROWS, :]).then_inc(s_offd, 16)
                sp.wait_ge(s_offd, 32)
                sp.dma_start(offs[:, :], offs_d.ap().rearrange("(o r) k -> o (r k)", o=1)).then_inc(s_offl, 16)
                sp.dma_start(firsts[:, :], firsts_d.ap().rearrange("(o r) k -> o (r k)", o=1)).then_inc(s_offl, 16)
                sp.wait_ge(s_offl, 32)
                sp.wait_ge(s_x, 32)

            @block.gpsimd
            def _(pool):
                pool.memset(ident[:, :], 0.0).then_inc(s_idm, 1)
                pool.memset(lower[:, :], 1.0).then_inc(s_idm, 1)
                pool.memset(ones[:, :], 1.0).then_inc(s_idm, 1)
                pool.memset(edge[:, :, ET:ET + RB * JT], 0.0).then_inc(s_idm, 1)
                pool.memset(eye2[:, :], 0.0).then_inc(s_idm, 1)
                pool.wait_ge(s_idm, 5)
                for h in range(2):
                    pool.affine_select(out=eye2[:, :], in_=eye2[:, :], compare_op=ALU.not_equal, fill=1.0, base=-h * F,
                                       pattern=[[-1, F]], channel_multiplier=1).then_inc(s_idm, 1)
                    pool.wait_ge(s_idm, 6 + h)
                pool.affine_select(out=ident[:, :], in_=ident[:, :], compare_op=ALU.not_equal, fill=1.0, base=0,
                                   pattern=[[-1, P]], channel_multiplier=1).then_inc(s_id, 1)
                pool.affine_select(out=lower[:, :], in_=lower[:, :], compare_op=ALU.is_gt, fill=0.0, base=0,
                                   pattern=[[-1, P]], channel_multiplier=1).then_inc(s_id, 1)
                pool.iota(iota_p[:, :], [[0, 1]], base=NPAD, channel_multiplier=1,
                          allow_small_or_imprecise_dtypes=True).then_inc(s_id, 1)
                pool.iota(iota_f[:, :], [[1, NT * TWIN]], base=0, channel_multiplier=0,
                          allow_small_or_imprecise_dtypes=True).then_inc(s_id, 1)

            @block.scalar
            def _(act):
                for l, w in enumerate((w0, w1)):
                    act.dma_start(w[0:F, 0:T * F].rearrange("k (t n) -> k t n", t=T), A[f"L0_gnn_W{l}"].rearrange("t k n -> k t n")).then_inc(s_wts, 16)
                act.dma_start(w1[0:F, T * F + T:], A["L0_gnn_Wres"]).then_inc(s_wts, 16)
                act.dma_start(w2[0:F, :], A["L1_gnn_W"]).then_inc(s_wts, 16)
                for l in range(2):
                    act.dma_start(al[l][:, :, :], A[f"L0_gnn_Al{l}"].rearrange("t k n -> k t n")).then_inc(s_wts, 16)
                    act.dma_start(ar[l][:, :, :], A[f"L0_gnn_Ar{l}"].rearrange("t k n -> k t n")).then_inc(s_wts, 16)
                act.dma_start(bres[:, :], A["L0_gnn_bres"].partition_broadcast(P)).then_inc(s_small, 16)
                act.dma_start(b2[:, :], A["L1_gnn_b"].partition_broadcast(P)).then_inc(s_small, 16)
                act.dma_start(deg[:, :], A["L1_gnn_deg_coeff"].partition_broadcast(P)).then_inc(s_small, 16)
                act.dma_start(cin[:, 0:3], A["L1_gnn_coeff_param"].partition_broadcast(P)).then_inc(s_small, 16)
                act.dma_start(cin[:, 3:4], A["L1_gnn_scale_param"].partition_broadcast(P)).then_inc(s_small, 16)
                for l in range(2):
                    act.wait_ge(s_wt, l + 1)
                    act.activation(wt[l][:, :, :], ps_w[l][0:F, 0:T * F].rearrange("k (t n) -> k t n", t=T), ACT.Copy).then_inc(s_wtc, 1)
                act.wait_ge(s_csm, 1)
                act.activation(csm[:, 0:3], csm[:, 0:3], ACT.Exp, accum_out=csm[:, 3:4]).then_inc(a, 1)
                act.activation(csm[:, 5:6], csm[:, 4:5], ACT.Exp, scale=-1.0).then_inc(a, 1)
                act.wait_ge(a, 2)
                act.activation(csm[:, 6:7], csm[:, 5:6], ACT.Ln, bias=1.0).then_inc(a, 1)
                def copy(i, q):
                    act.activation(xs[q][:, :].rearrange("p (c f) -> p c f", f=F), x_sb[:, bass.ds(i * CH, CH), :], ACT.Copy).then_inc(s_xs, 1)

                def keep(i, q):
                    take(act, s_xturned)
                    for k, m in ((0, 4), (1, CH - 4)):
                        last = act.activation(feat[:, bass.ds(i * (CH * P) + k * 4 * P, m * P)], ps_turn[q][0:F, k * 512:k * 512 + m * P], ACT.Copy)
                    last.then_inc(s_xkept, 1)

                act.wait_ge(s_x, 32)
                chunks(act, copy, keep)
                act.wait_ge(s_xkept, NCH)
                act.wait_ge(s_z, 1)
                act.activation(lg[0:ROWS, :], lg[0:ROWS, :], ACT.Exp, scale=-1.0).then_inc(a, 1)
                act.wait_ge(a, 4)
                act.activation(lg[0:ROWS, :], lg[0:ROWS, :], ACT.Ln, bias=1.0).then_inc(s_sp, 1)
                act.wait_ge(s_rowready, 1)
                for q in range(2):
                    act.sem_inc(s_turn_free[q], 1)
                with act.Fori(0, JT // 2) as i:
                    for q in range(2):
                        take(act, s_turn_free[q])
                        act.activation(turn[0:ROWS, q, :, :], row[0:ROWS, :, bass.ds(i * (2 * P) + q * P, P)], ACT.Copy).then_inc(s_turn_in[q], 1)

            @block.vector
            def _(dve):
                nv = [0]

                def link(ins):
                    nv[0] += 1
                    ins.then_inc(v, 1)
                    dve.wait_ge(v, nv[0])

                tail_row = ROWS - 16
                dve.memset(x_sb[:, NT - 1, :], 0.0).then_inc(s_pad, 1)
                dve.memset(raw_s[tail_row:ROWS, :], PAD_SRC).then_inc(s_pad, 1)
                dve.memset(raw_d[tail_row:ROWS, :], PAD_DST).then_inc(s_pad, 1)
                dve.memset(raw_t[tail_row:ROWS, :], 0).then_inc(s_pad, 1)
                dve.memset(row[tail_row:ROWS, A_W, :], 0.0).then_inc(s_pad, 1)
                dve.memset(row[tail_row:ROWS, A_BASE, :], 0.0).then_inc(s_pad, 1)
                for w in (w0, w1, w2):
                    link(dve.memset(w[F:P, :], 0.0))
                dve.wait_ge(s_wts, 16 * 8)
                for l in range(2):
                    link(dve.tensor_tensor(al[l][:, :, :], al[l][:, :, :], ar[l][:, :, :], ALU.add))
                link(dve.tensor_reduce(asum[0][:, :, :], al[0].rearrange("k t (h d) -> k t h d", h=HEADS), AX.X, ALU.add))
                dve.tensor_reduce(asum[1][:, :], al[1][:, :, :], AX.X, ALU.add).then_inc(s_asum, 1)
                dve.wait_ge(s_small, 16 * 5)
                link(dve.tensor_reduce(csm[:, 7:8], cin[:, 0:3], AX.X, ALU.max))
                link(dve.tensor_scalar(csm[:, 0:3], cin[:, 0:3], csm[:, 7:8], None, ALU.subtract))
                dve.scalar_tensor_tensor(csm[:, 4:5], cin[:, 3:4], -1.0, cin[:, 3:4], ALU.mult, ALU.max).then_inc(s_csm, 1)
                dve.wait_ge(a, 3)
                link(dve.reciprocal(csm[:, 7:8], csm[:, 3:4]))
                link(dve.tensor_scalar(coeff[:, 0:3], csm[:, 0:3], csm[:, 7:8], None, ALU.mult))
                link(dve.scalar_tensor_tensor(coeff[:, 3:4], cin[:, 3:4], 0.0, csm[:, 6:7], ALU.max, ALU.add))
                link(dve.tensor_tensor(coeff[:, 4:5], coeff[:, 0:1], coeff[:, 1:2], ALU.subtract))
                link(dve.tensor_tensor(coeff[:, 5:6], coeff[:, 0:1], coeff[:, 1:2], ALU.min))
                link(dve.tensor_scalar(coeff[:, 6:7], coeff[:, 4:5], 0.0, 2.0, ALU.is_ge, ALU.mult))
                link(dve.tensor_scalar(coeff[:, 6:7], coeff[:, 6:7], -1.0, None, ALU.add))
                link(dve.tensor_tensor(coeff[:, 5:6], coeff[:, 5:6], coeff[:, 6:7], ALU.mult))
                link(dve.tensor_tensor(coeff[:, 7:8], coeff[:, 2:3], coeff[:, 3:4], ALU.mult))
                dve.wait_ge(s_rows, 160)
                dve.wait_ge(s_first, 32)
                R = slice(0, ROWS)
                base, rel, lo, key = (row[R, k, :] for k in (A_BASE, A_REL, A_LO, A_KEY))
                link(dve.tensor_scalar(z[R, :], base, deg[R, 0:1], deg[R, 1:2], ALU.mult, ALU.add))
                dve.scalar_tensor_tensor(lg[R, :], z[R, :], -1.0, z[R, :], ALU.mult, ALU.max).then_inc(s_z, 1)
                link(dve.tensor_copy(first[R, 0:1], raw_d[R, 0:1]))
                link(dve.tensor_copy(first_f[R, :], first[R, :]))
                link(dve.tensor_scalar(off_f[R, 0, :], raw_d[R, :].rearrange("p (j q) -> p j q", q=P)[:, :, 0], first_f[R, 1:2], float(STRIP - TWIN), ALU.subtract, ALU.min))
                link(dve.tensor_scalar(off_f[R, 1, :], off_f[R, 0, :], first_f[R, 1:2], None, ALU.add))
                link(dve.memset(off_i[:, :], 0))
                dve.tensor_copy(off_i[R, :].rearrange("p (b k) -> p b k", b=2)[:, :, 0:HT], off_f[R, 0, :].rearrange("p (b k) -> p b k", b=2)).then_inc(s_off, 1)
                dve.scalar_tensor_tensor(row[R, A_IDX, :], raw_s[R, :], float(T), raw_t[R, :], ALU.mult, ALU.add)
                dve.tensor_scalar(rel, raw_d[R, :], first_f[R, 0:1], None, ALU.subtract)
                dve.tensor_scalar(hi[R, :], raw_s[R, :], 7, None, ALU.arith_shift_right)
                link(dve.tensor_tensor(key.rearrange("p (j q) -> p j q", q=P), raw_d[R, :].rearrange("p (j q) -> p j q", q=P),
                                       off_f[R, 1, :].rearrange("p (j o) -> p j o", o=1).to_broadcast([ROWS, JT, P]), ALU.subtract))
                dve.tensor_reduce(bad[R, 0:1], rel, AX.X, ALU.max)
                dve.tensor_reduce(bad[R, 1:2], key, AX.X, ALU.max)
                dve.tensor_reduce(bad[R, 2:3], rel, AX.X, ALU.min)
                dve.tensor_reduce(bad[R, 3:4], key, AX.X, ALU.min)
                link(dve.tensor_reduce(bad[R, 4:5], off_f[R, 0, :], AX.X, ALU.min))
                dve.tensor_scalar(bad[R, 0:1], bad[R, 0:1], float(WIN - 1), None, ALU.is_gt)
                dve.tensor_scalar(bad[R, 1:2], bad[R, 1:2], float(TWIN - 1), None, ALU.is_gt)
                link(dve.tensor_scalar(bad[R, 2:5], bad[R, 2:5], 0.0, None, ALU.is_lt))
                dve.tensor_reduce(bad[R, 5:6], bad[R, 0:5], AX.X, ALU.add).then_inc(s_bad, 1)
                dve.scalar_tensor_tensor(lo, hi[R, :], float(-P), raw_s[R, :], ALU.mult, ALU.add)
                link(dve.scalar_tensor_tensor(key, hi[R, :], float(TWIN), key, ALU.mult, ALU.add))
                link(dve.tensor_tensor(base, raw_s[R, :], raw_d[R, :], ALU.not_equal))
                link(dve.tensor_tensor(base, base, row[R, A_W, :], ALU.mult))
                dve.wait_ge(s_sp, 1)
                link(dve.scalar_tensor_tensor(z[R, :], z[R, :], 0.0, lg[R, :], ALU.max, ALU.add))
                dve.tensor_tensor(base, base, z[R, :], ALU.mult).then_inc(s_rowready, 1)
                for l in range(2):
                    dve.wait_ge(s_wa, l + 1)
                    n = T * HEADS if l == 0 else T
                    link(dve.tensor_copy((w0, w1)[l][0:F, T * F:T * F + n], ps_w[2 + l][0:F, 0:n]))
                dve.wait_ge(s_badsum, 1)
                link(dve.tensor_copy(flags[0:1, 0:1], ps_w[0][0:1, 0:1]))
                for q in range(2):
                    dve.sem_inc(s_turned_free[q], 1)
                with dve.Fori(0, JT // 2) as i:
                    for q in range(2):
                        take(dve, s_turned[q])
                        dve.sem_inc(s_turn_free[q], 1)
                        for h in range(2):
                            last = dve.tensor_copy(edge.ap().rearrange("p a (r j) -> p a r j", j=JT)[:, 3 * h:3 * h + 3, 0:ROWS, bass.ds(2 * i + q, 1)].rearrange("p a r j -> p a (r j)"),
                                                   ps_turn[q][:, h * 512:h * 512 + 3 * ROWS].rearrange("p (a r) -> p a r", a=3))
                        last.then_inc(s_turned_free[q], 1)

            @block.tensor
            def _(pe):
                pe.wait_ge(s_id, 4)
                pe.wait_ge(s_wts, 16 * 8)
                for l, w in enumerate((w0, w1)):
                    for t in range(T):
                        last = pe.transpose(ps_w[l][0:F, t * F:(t + 1) * F], w[0:F, t * F:(t + 1) * F], ident[0:F, 0:F])
                    last.then_inc(s_wt, 1)
                pe.wait_ge(s_asum, 1)
                for l in range(2):
                    pe.wait_ge(s_wtc, l + 1)
                    n = HEADS if l == 0 else 1
                    for t in range(T):
                        rhs = asum[0][:, t, :] if l == 0 else asum[1][:, t:t + 1]
                        last = pe.matmul(ps_w[2 + l][0:F, t * n:(t + 1) * n], wt[l][:, t, :], rhs, start=True, stop=True)
                    last.then_inc(s_wa, 1)
                def turn_x(i, q):
                    take(pe, s_xs)
                    for c in range(CH):
                        at = c // 4 * 512 + c % 4 * P
                        last = pe.matmul(ps_turn[q][0:F, at:at + P], xs[q][:, c * F:(c + 1) * F], ident[:, :], start=True, stop=True)
                    last.then_inc(s_xturned, 1)

                chunks(pe, nothing, turn_x)
                pe.wait_ge(s_bad, 1)
                pe.matmul(ps_w[0][0:1, 0:1], bad[0:ROWS, 5:6], ones[0:ROWS, :], start=True, stop=True).then_inc(s_badsum, 1)
                with pe.Fori(0, JT // 2) as i:
                    for q in range(2):
                        take(pe, s_turn_in[q])
                        take(pe, s_turned_free[q])
                        for k in range(NA):
                            at = k // 3 * 512 + k % 3 * ROWS
                            last = pe.transpose(ps_turn[q][:, at:at + ROWS], turn[0:ROWS, q, k, :], ident[0:ROWS, 0:ROWS])
                        last.then_inc(s_turned[q], 1)

        def table_phase(layer):
            w, heads = ((w0, HEADS), (w1, 1))[layer]
            natt = T * heads
            ncol = T * F + natt + (F if layer else 0)
            with scope() as s2, nc.Block() as block:
                xt = [sb(f"xt{layer}{k}", [P, CH * P], F32, s2) for k in range(2)]
                low, high = ([sb(f"{n}{layer}{k}", [F, CH * P], F32, s2) for k in range(2)] for n in ("low", "high"))
                prod = [sb(f"prod{layer}{k}", [P, CH, T * F + natt], F32, s2) for k in range(2)]
                lk = [sb(f"lk{layer}{k}", [P, CH, natt], F32, s2) for k in range(2)]
                msg = [sb(f"msg{layer}{k}", [P, CH, T * F], F32, s2) for k in range(2)]
                ps_h = [psum(f"ps_h{layer}{c}", [P, 512], s2) for c in range(CH)]
                s_low, s_exp, s_in, v, s_zeros = (sem(f"t{layer}_{n}") for n in ("low", "exp", "in", "v", "zeros"))
                s_h, s_h_free, s_prod, s_prod_free, s_lk, s_att, s_msg = (sem(f"t{layer}_{n}") for n in ("h", "h_free", "prod", "prod_free", "lk", "att", "msg"))
                s_out = [sem(f"t{layer}_out{k}") for k in range(2)]

                @block.gpsimd
                def _(pool):
                    for q in range(2):
                        pool.memset(xt[q][F:P, :], 0.0).then_inc(s_zeros, 1)
                    if layer == 1:
                        pool.wait_ge(s_zeros, 2)
                        pool.tensor_tensor(x_sb[:, :, :], x_sb[:, :, :], bres[:, :].rearrange("p (o f) -> p o f", o=1).to_broadcast([P, NT, F]), ALU.add).then_inc(s_zeros, 1)
                        pool.wait_ge(s_zeros, 3)

                @block.vector
                def _(dve):
                    def inputs(i, q):
                        x = feat[:, bass.ds(i * (CH * P), CH * P)]
                        if layer == 0:
                            dve.tensor_copy(xt[q][0:F, :], x).then_inc(s_in, 1)
                        else:
                            dve.tensor_scalar(low[q][:, :], x, 0.0, None, ALU.min).then_inc(s_low, 1)
                            dve.tensor_scalar(high[q][:, :], x, 0.0, -1.0, ALU.max, ALU.add).then_inc(v, 1)
                            take(dve, v)
                            take(dve, s_exp)
                            dve.tensor_tensor(xt[q][0:F, :], low[q][:, :], high[q][:, :], ALU.add).then_inc(s_in, 1)

                    def messages(i, q):
                        take(dve, s_prod)
                        att = prod[q][:, :, T * F:T * F + natt]
                        dve.scalar_tensor_tensor(lk[q][:, :, :], att, SLOPE, att, ALU.mult, ALU.max).then_inc(s_lk, 1)
                        take(dve, s_att)
                        if layer == 1:
                            dve.tensor_scalar(lk[q][:, :, :], lk[q][:, :, :], 1.0, None, ALU.add).then_inc(v, 1)
                            take(dve, v)
                            dve.reciprocal(lk[q][:, :, :], lk[q][:, :, :]).then_inc(v, 1)
                            take(dve, v)
                        take(dve, s_out[q], 16)
                        for c in range(CH):
                            o = msg[q][:, c, :]
                            if layer == 0:
                                h = prod[q][:, c, 0:T * F].rearrange("p (t h d) -> p t d h", t=T, h=HEADS)
                                o = o.rearrange("p (t d h) -> p t d h", t=T, h=HEADS)
                                g = lk[q][:, c, :].rearrange("p (t o h) -> p t o h", t=T, o=1).to_broadcast([P, T, HID, HEADS])
                            else:
                                h = prod[q][:, c, 0:T * F].rearrange("p (t f) -> p t f", t=T)
                                o = o.rearrange("p (t f) -> p t f", t=T)
                                g = lk[q][:, c, :].rearrange("p (t o) -> p t o", t=T).to_broadcast([P, T, F])
                            last = dve.tensor_tensor(o, h, g, ALU.mult)
                        last.then_inc(s_msg, 1)

                    chunks(dve, inputs, messages)

                @block.sync
                def _(sp):
                    rows = tab_l[layer].ap().rearrange("(i p t) f -> p i (t f)", p=P, t=T)

                    def store(i, q):
                        take(sp, s_msg)
                        sp.sem_inc(s_prod_free, 1)
                        sp.dma_start(rows[:, bass.ds(i * CH, CH), :], msg[q][:, :, :]).then_inc(s_out[q], 16)

                    for q in range(2):
                        sp.sem_inc(s_out[q], 16)
                    chunks(sp, nothing, store)
                    for q in range(2):
                        sp.wait_ge(s_out[q], 16)

                @block.tensor
                def _(pe):
                    def products(i, q):
                        take(pe, s_in)
                        for c in range(CH):
                            take(pe, s_h_free)
                            pe.matmul(ps_h[c][:, 0:ncol], xt[q][:, c * P:(c + 1) * P], w[:, 0:ncol], start=True, stop=True).then_inc(s_h, 1)

                    pe.wait_ge(s_zeros, 2)
                    chunks(pe, nothing, products)

                @block.scalar
                def _(act):
                    def inputs(i, q):
                        if layer == 1:
                            take(act, s_low)
                            act.activation(low[q][:, :], low[q][:, :], ACT.Exp).then_inc(s_exp, 1)

                    def products(i, q):
                        take(act, s_prod_free)
                        for c in range(CH):
                            take(act, s_h)
                            if layer:
                                act.activation(skip[:, bass.ds(i * CH + c, 1), :].rearrange("p c f -> p (c f)"), ps_h[c][:, T * F + natt:ncol], ACT.Copy)
                            act.activation(prod[q][:, c, :], ps_h[c][:, 0:T * F + natt], ACT.Copy).then_inc(s_prod if c == CH - 1 else s_h_free, 1)
                        take(act, s_lk)
                        act.sem_inc(s_h_free, 1)
                        if layer == 0:
                            act.activation(lk[q][:, :, :], lk[q][:, :, :], ACT.Sigmoid).then_inc(s_att, 1)
                        else:
                            act.activation(lk[q][:, :, :], lk[q][:, :, :], ACT.Exp, scale=-1.0).then_inc(s_att, 1)

                    act.sem_inc(s_h_free, CH)
                    act.sem_inc(s_prod_free, 2)
                    chunks(act, inputs, products)

        def general_edges(n):
            with scope() as s5, nc.Block() as block:
                raw = [sb(f"graw{n}{k}", [P, ROWLEN], I32, s5) for k in range(2)]
                rowf = sb(f"growf{n}", [P, 2, ROWLEN], F32, s5)
                zeros = sb(f"gzeros{n}", [P, TAB // P * F], F32, s5)
                turn = sb(f"gturn{n}", [P, 2, P], F32, s5)
                ps = psum(f"gps{n}", [P, 512], s5)
                s_pad, s_rows, s_f, s_z, s_zd = (sem(f"g_{k}{n}") for k in ("pad", "rows", "f", "z", "zd"))
                s_in, s_out, s_back = (sem(f"g_{k}{n}") for k in ("in", "out", "back"))

                @block.vector
                def _(dve):
                    dve.memset(raw[0][96:ROWS, :], PAD_SRC).then_inc(s_pad, 1)
                    dve.memset(raw[1][96:ROWS, :], PAD_DST).then_inc(s_pad, 1)
                    dve.memset(zeros[:, :], 0.0).then_inc(s_z, 1)
                    dve.wait_ge(s_rows, 64)
                    dve.tensor_copy(rowf[0:ROWS, 0, :], raw[0][0:ROWS, :])
                    dve.tensor_copy(rowf[0:ROWS, 1, :], raw[1][0:ROWS, :]).then_inc(s_f, 1)
                    with dve.Fori(0, JT) as i:
                        take(dve, s_out)
                        for k, arr in enumerate((A_SRC, A_DST)):
                            last = dve.tensor_copy(edge.ap().rearrange("p a (r j) -> p a r j", j=JT)[:, arr, 0:ROWS, bass.ds(i, 1)].rearrange("p r j -> p (r j)"),
                                                   ps[:, k * ROWS:(k + 1) * ROWS])
                        last.then_inc(s_back, 1)

                @block.scalar
                def _(act):
                    act.wait_ge(s_f, 1)
                    act.sem_inc(s_back, 1)
                    with act.Fori(0, JT) as i:
                        take(act, s_back)
                        act.activation(turn[0:ROWS, :, :], rowf[0:ROWS, :, bass.ds(i * P, P)], ACT.Copy).then_inc(s_in, 1)

                @block.tensor
                def _(pe):
                    with pe.Fori(0, JT) as i:
                        take(pe, s_in)
                        for k in range(2):
                            last = pe.transpose(ps[:, k * ROWS:(k + 1) * ROWS], turn[0:ROWS, k, :], ident[0:ROWS, 0:ROWS])
                        last.then_inc(s_out, 1)

                @block.gpsimd
                def _(pool):
                    pool.wait_ge(s_z, 1)

                @block.sync
                def _(sp):
                    sp.wait_ge(s_pad, 2)
                    for k, name in enumerate(("src", "dst")):
                        sp.dma_start(raw[k][0:FULLROWS, :], A[name][0:FULLROWS * ROWLEN].rearrange("(p n) -> p n", n=ROWLEN)).then_inc(s_rows, 16)
                        sp.dma_start(raw[k][FULLROWS:ROWS, 0:TAIL], A[name][FULLROWS * ROWLEN:EDGES].rearrange("(p n) -> p n", p=1)).then_inc(s_rows, 16)
                    sp.wait_ge(s_z, 1)
                    for t in sums[n]:
                        sp.dma_start(t.ap().rearrange("(p n) f -> p (n f)", p=P), zeros[:, :]).then_inc(s_zd, 16)
                    sp.wait_ge(s_zd, 16 * BT)

        def edge_phase(n, tabs, width, key, tables):
            ng = len(tabs)
            with scope() as s3, nc.Block() as block:
                idx = sb(f"idx{n}", [P, 2, ng, BT], I32, s3)
                keyf = sb(f"keyf{n}", [P, 2, BT], F32, s3)
                rows = sb(f"rows{n}", [P, 2, ng, BT, width], F32, s3)
                same = sb(f"same{n}", [P, BT, P], F32, s3)
                before = sb(f"before{n}", [P, BT, P], F32, s3)
                dup = sb(f"dup{n}", [P, 3, BT], F32, s3)
                sidx = sb(f"sidx{n}", [P, 2, BT], I32, s3)
                wmsg = sb(f"wmsg{n}", [P, BT, F], F32, s3)
                outm = sb(f"outm{n}", [P, 2, BT, F], F32, s3)
                sc = sb(f"sc{n}", [P, 6, BT], F32, s3)
                ps_key = psum(f"ps_key{n}", [P, BT * P], s3)
                ps_sum = psum(f"ps_sum{n}", [P, BT * F], s3)
                s_idx = [sem(f"s_idx{n}{q}") for q in range(2)]
                s_idx_free = [sem(f"s_idx_free{n}{q}") for q in range(2)]
                s_got = [sem(f"s_got{n}{q}", True) for q in range(2)]
                s_rows_free = [sem(f"s_rows_free{n}{q}") for q in range(2)]
                s_key, s_wm, s_sum = sem(f"s_key{n}"), sem(f"s_wm{n}"), sem(f"s_sum{n}")
                s_keyf, s_key_free = sem(f"s_keyf{n}"), sem(f"s_key_free{n}")
                s_out = sem(f"s_outm{n}")
                s_out_free = [sem(f"s_out_free{n}{q}") for q in range(2)]
                s_add = [sem(f"s_add{n}{k}", True) for k in range(BT)]
                v = sem(f"v_edge{n}")

                @block.gpsimd
                def _(pool):
                    def gather(q, first=False):
                        take(pool, s_idx[q])
                        if not first:
                            take(pool, s_rows_free[q])
                        for g in range(ng):
                            for k in range(BT):
                                pool.indirect_dma_start(rows[:, q, g, k, :], None, tabs[g][0].ap(),
                                                        bass.IndirectOffsetOnAxis(ap=idx[:, q, g, k:k + 1], axis=0)).then_inc(s_got[q], 16)

                    def scatter(q, done=None):
                        take(pool, s_out)
                        for k in range(BT):
                            if done is not None:
                                pool.wait_ge(s_add[k], done).then_inc(s_out_free[1 - q], 1)
                            pool.indirect_dma_start(tables[k].ap(), bass.IndirectOffsetOnAxis(ap=sidx[:, q, k:k + 1], axis=0),
                                                    outm[:, q, k, :], None, compute_op=ALU.add).then_inc(s_add[k], 16)

                    gather(0, True)
                    gather(1, True)
                    scatter(0)
                    with pool.Fori(0, NB // 2 - 1) as i:
                        gather(0)
                        scatter(1, i * 32 + 16)
                        gather(1)
                        scatter(0, i * 32 + 32)
                    scatter(1, 16 * (NB - 1))
                    for k in range(BT):
                        pool.wait_ge(s_add[k], 16 * NB)

                @block.sync
                def _(sp):
                    sp.wait_ge(s_add[0], 16 * NB)

                @block.scalar
                def _(act):
                    for q in range(2):
                        act.sem_inc(s_idx_free[q], 1)
                    with act.Fori(0, NB // 2) as i:
                        for q in range(2):
                            take(act, s_idx_free[q])
                            for g in range(ng):
                                last = act.activation(idx[:, q, g, :], edge[:, tabs[g][1], bass.ds(i * (2 * BT) + q * BT, BT)], ACT.Copy)
                            last.then_inc(s_idx[q], 1)
                            act.activation(keyf[:, q, :], edge[:, key, bass.ds(i * (2 * BT) + q * BT, BT)], ACT.Copy).then_inc(s_keyf, 1)

                @block.tensor
                def _(pe):
                    pe.sem_inc(s_key_free, 1)
                    with pe.Fori(0, NB // 2) as i:
                        for q in range(2):
                            take(pe, s_keyf)
                            take(pe, s_key_free)
                            for k in range(BT):
                                last = pe.matmul(ps_key[:, k * P:(k + 1) * P], keyf[:, q, k:k + 1].to_broadcast([P, P]), ident[:, :],
                                                 start=True, stop=True)
                            last.then_inc(s_key, 1)
                            take(pe, s_wm)
                            for k in range(BT):
                                last = pe.matmul(ps_sum[:, k * F:(k + 1) * F], same[:, k, :], wmsg[:, k, :], start=True, stop=True)
                            last.then_inc(s_sum, 1)

                @block.vector
                def _(dve):
                    def link(ins):
                        ins.then_inc(v, 1)
                        take(dve, v)

                    for q in range(2):
                        dve.sem_inc(s_out_free[q], BT)
                    with dve.Fori(0, NB // 2) as i:
                        for q in range(2):
                            at = i * (2 * BT) + q * BT
                            take(dve, s_key)
                            kq = keyf[:, q, :].rearrange("p (k o) -> p k o", o=1).to_broadcast([P, BT, P])
                            link(dve.tensor_tensor(same[:, :, :], ps_key[:, :].rearrange("p (k c) -> p k c", k=BT), kq, ALU.is_equal))
                            dve.sem_inc(s_key_free, 1)
                            low = lower[:, :].rearrange("p (o c) -> p o c", o=1).to_broadcast([P, BT, P])
                            link(dve.tensor_tensor(before[:, :, :], same[:, :, :], low, ALU.mult))
                            link(dve.tensor_reduce(dup[:, 0, :], before[:, :, :], AX.X, ALU.max))
                            spare = iota_p[:, 0:1].to_broadcast([P, BT])
                            link(dve.tensor_tensor(dup[:, 1, :], spare, keyf[:, q, :], ALU.subtract))
                            link(dve.tensor_tensor(dup[:, 2, :], dup[:, 1, :], dup[:, 0, :], ALU.mult))
                            take(dve, s_out_free[q], BT)
                            link(dve.tensor_tensor(sidx[:, q, :], dup[:, 2, :], keyf[:, q, :], ALU.add))
                            dve.wait_ge(s_got[q], i * (16 * BT * ng) + 16 * BT * ng).then_inc(s_idx_free[q], 1)
                            if n < 2:
                                wq = edge[:, A_W, bass.ds(at, BT)].rearrange("p (k o) -> p k o", o=1).to_broadcast([P, BT, F])
                                dve.tensor_tensor(wmsg[:, :, :], rows[:, q, 0, :, :], wq, ALU.mult).then_inc(s_wm, 1)
                            else:
                                link(dve.tensor_tensor(wmsg[:, :, :], rows[:, q, 0, :, 0:F], rows[:, q, 1, :, 0:F], ALU.mult))
                                link(dve.tensor_reduce(sc[:, 0, :], wmsg[:, :, :], AX.X, ALU.add))
                                link(dve.tensor_tensor(sc[:, 1, :], rows[:, q, 0, :, F], rows[:, q, 1, :, F], ALU.mult))
                                link(dve.tensor_scalar(sc[:, 1, :], sc[:, 1, :], EPS_SIM, None, ALU.max))
                                link(dve.reciprocal(sc[:, 2, :], sc[:, 1, :]))
                                link(dve.tensor_tensor(sc[:, 0, :], sc[:, 0, :], sc[:, 2, :], ALU.mult))
                                link(dve.tensor_scalar(sc[:, 3, :], sc[:, 0, :], 0.0, coeff[:, 0:1], ALU.max, ALU.mult))
                                link(dve.tensor_scalar(sc[:, 4, :], sc[:, 0, :], 0.0, coeff[:, 1:2], ALU.min, ALU.mult))
                                link(dve.tensor_tensor(sc[:, 3, :], sc[:, 3, :], sc[:, 4, :], ALU.add))
                                link(dve.tensor_tensor(sc[:, 5, :], sc[:, 3, :], edge[:, A_BASE, bass.ds(at, BT)], ALU.mult))
                                cq = sc[:, 5, :].rearrange("p (k o) -> p k o", o=1).to_broadcast([P, BT, F])
                                dve.tensor_tensor(wmsg[:, :, :], rows[:, q, 1, :, 0:F], cq, ALU.mult).then_inc(s_wm, 1)
                            take(dve, s_sum)
                            dve.sem_inc(s_rows_free[q], 1)
                            dve.tensor_copy(outm[:, q, :, :], ps_sum[:, :].rearrange("p (k f) -> p k f", k=BT)).then_inc(s_out, 1)

        def general_sums(n):
            with scope() as s6, nc.Block() as block:
                buf = [sb(f"gbuf{n}{k}", [P, NT, F], F32, s6) for k in range(2)]
                s_load, s_used, v = [sem(f"s_load{n}{k}") for k in range(2)], sem(f"s_used{n}"), sem(f"v_sums{n}")

                @block.sync
                def _(sp):
                    for k in range(BT):
                        if k >= 2:
                            sp.wait_ge(s_used, k - 1)
                        sp.dma_start(buf[k % 2][:, :, :], sums[n][k].ap()[0:NPAD, :].rearrange("(i p) f -> p i f", p=P)).then_inc(s_load[k % 2], 16)

                @block.vector
                def _(dve):
                    for k in range(BT):
                        dve.wait_ge(s_load[k % 2], 16 * (k // 2 + 1))
                        if k:
                            dve.wait_ge(s_used, k)
                            dve.tensor_tensor(acc[:, :, :], acc[:, :, :], buf[k % 2][:, :, :], ALU.add).then_inc(s_used, 1)
                        else:
                            dve.tensor_copy(acc[:, :, :], buf[0][:, :, :]).then_inc(s_used, 1)

                for other in (block.scalar, block.tensor, block.gpsimd):
                    other(lambda eng: eng.sem_inc(v, 1))

        def general_path(n):
            general_edges(n)
            tabs = [(tab_l[n], A_IDX)] if n < 2 else [(tab_g, A_SRC), (tab_g, A_DST)]
            edge_phase(n, tabs, F if n < 2 else F + 1, A_DST if n < 2 else A_SRC, sums[n])
            general_sums(n)

        def fast_path(l):
            with scope() as s8, nc.Block() as block:
                KB = 4
                AHEAD = KB - 1
                strip = [sb(f"strip{l}{k}", [P, NT, STRIP], F32, s8) for k in range(2)]
                turned = [sb(f"turned{l}{k}", [P, 4 * P], F32, s8) for k in range(2)]
                idx = sb(f"fidx{l}", [P, RB, JT], I32, s8)
                rows = sb(f"frows{l}", [P, RB, JT, F], F32, s8)
                hot = sb(f"hot{l}", [P, 2, JT, WIN], F32, s8)
                hot_lo = sb(f"hot_lo{l}", [P, 2, HT, P], F32, s8)
                hot_key = sb(f"hot_key{l}", [P, KB, NT * TWIN], F32, s8)
                zcol = sb(f"zcol{l}", [P, 1], F32, s8)
                ps_sum = [psum(f"fps_sum{l}{k}", [P, 512], s8) for k in range(2)]
                ps_b = [psum(f"fps_b{l}{k}", [P, 512], s8) for k in range(KB)]
                ps_t = [psum(f"fps_t{l}{k}", [P, 512], s8) for k in range(2)]

                def fs(name):
                    return sem(f"f{l}_{name}")
                s_idx, s_idx_free, s_rows_free = ([fs(f"{n}{q}") for q in range(RB)] for n in ("idx", "idx_free", "rows_free"))
                s_got = [sem(f"f{l}_got{q}", True) for q in range(RB)]
                s_wm, s_agg, s_key, s_b = (fs(n) for n in ("wm", "agg", "key", "b"))
                s_full, s_zeroed, s_stored = ([fs(f"{n}{k}") for k in range(2)] for n in ("full", "zeroed", "stored"))
                s_t, s_t_free, s_piece = (fs(n) for n in ("t", "t_free", "piece"))
                v, v_agg, s_zc = fs("v"), fs("v_agg"), fs("zc")
                PIECES = [list(range(k, min(k + 4, NT))) for k in range(0, NT, 4)]
                PER = [PIECES[0:4], PIECES[4:8], PIECES[8:12], PIECES[12:13]]

                def side(k, piece):
                    return (piece[0] // 4 + (1 - k) * len(PIECES)) % 2

                @block.gpsimd
                def _(pool):
                    for q in range(RB):
                        pool.sem_inc(s_rows_free[q], 1)
                    with pool.Fori(0, LOOPS) as i:
                        for u in range(SLOTS):
                            q = u % RB
                            take(pool, s_idx[q])
                            take(pool, s_rows_free[q])
                            for k in range(JT):
                                pool.indirect_dma_start(rows[:, q, k, :], None, tab_l[l].ap(),
                                                        bass.IndirectOffsetOnAxis(ap=idx[:, q, k:k + 1], axis=0)).then_inc(s_got[q], 16)

                @block.scalar
                def _(act):
                    def zero(part, n):
                        return act.activation(part, zcol[:, 0:1].rearrange("p (a b) -> p a b", a=1).to_broadcast([P, n, STRIP]), ACT.Copy)

                    def pieces(k, u):
                        for piece in PER[u]:
                            a, b = piece[0], piece[-1] + 1
                            j = side(k, piece)
                            take(act, s_t)
                            take(act, s_stored[j], 16)
                            act.activation(turned[j][:, 0:(b - a) * P], ps_t[j][:, 0:(b - a) * P], ACT.Copy).then_inc(s_t_free, 1)
                            zero(strip[k][:, a:b, :], b - a).then_inc(s_piece, 1)

                    def indices(u, row):
                        act.activation(idx[:, u % RB, :], edge[:, A_IDX, bass.ds(row * JT, JT)], ACT.Copy).then_inc(s_idx[u % RB], 1)

                    for u in range(RB):
                        indices(u, u)
                    for j in range(2):
                        act.sem_inc(s_stored[j], 16)
                    act.wait_ge(s_zc, 1)
                    zero(strip[0][:, :, :], NT).then_inc(s_zeroed[0], 1)
                    zero(strip[1][:, :, :], NT).then_inc(s_full[1], 1)
                    with act.Fori(0, LOOPS) as i:
                        for u in range(SLOTS):
                            pieces(1 - u // 4, u % 4)
                            take(act, s_idx_free[u % RB])
                            indices(u, i * SLOTS + (u + RB))
                    for u in range(4):
                        pieces(1, u)
                    for j in range(2):
                        take(act, s_stored[j], 16)

                @block.sync
                def _(sp):
                    def store(slot, k):
                        for n, piece in enumerate(PIECES):
                            take(sp, s_piece)
                            if n == len(PIECES) - 1:
                                sp.sem_inc(s_zeroed[k], 1)
                            a, b = piece[0], piece[-1] + 1
                            j = side(k, piece)
                            sp.dma_start(adj.ap()[l, bass.ds(slot, 1), :, a * P:b * P].rearrange("o w n -> (o w) n"), turned[j][:, 0:(b - a) * P]).then_inc(s_stored[j], 16)

                    with sp.Fori(0, LOOPS) as i:
                        store(i * 2, 1)
                        store(i * 2 + 1, 0)
                    store(LOOPS * 2, 1)

                @block.tensor
                def _(pe):
                    def turn(k, piece):
                        if piece[0] == 0:
                            take(pe, s_full[k])
                        take(pe, s_t_free)
                        for n, hi in enumerate(piece):
                            last = pe.matmul(ps_t[side(k, piece)][:, n * P:(n + 1) * P], strip[k][:, hi, :], ident[:, :], start=True, stop=True)
                        last.then_inc(s_t, 1)

                    def sum_row(u):
                        take(pe, s_wm)
                        for k in range(JT):
                            last = pe.matmul(ps_sum[u % 2][0:F, 0:WIN], rows[:, u % RB, k, :], hot[:, u % 2, k, :], start=(k == 0), stop=(k == JT - 1))
                        last.then_inc(s_agg, 1)

                    pe.sem_inc(s_t_free, 2)
                    with pe.Fori(0, LOOPS) as i:
                        for u in range(SLOTS):
                            todo = list(PER[u % 4])
                            for k in range(HT):
                                take(pe, s_key)
                                pe.matmul(ps_b[(u * HT + k) % KB][:, 0:NT * TWIN], hot_lo[:, u % 2, k, :], hot_key[:, (u * HT + k) % KB, :], start=True, stop=True).then_inc(s_b, 1)
                                if k == 0 and u > 0:
                                    sum_row(u - 1)
                                if todo and (k % 2 == 1 or k == HT - 1):
                                    turn(1 - u // 4, todo.pop(0))
                        sum_row(SLOTS - 1)
                    for u in range(4):
                        for piece in PER[u]:
                            turn(1, piece)

                @block.vector
                def _(dve):
                    dve.memset(zcol[:, :], 0.0).then_inc(s_zc, 1)
                    dve.memset(feat[:, :], 0.0).then_inc(v_agg, 1)
                    dve.sem_inc(v, 1)
                    windows = {}

                    def per_edge(array, at, n, width):
                        return edge[:, array, bass.ds(at, n)].rearrange("p (k o) -> p k o", o=1).to_broadcast([P, n, width])

                    def one_hot(out_ap, array, at, n, width):
                        return dve.tensor_tensor(out_ap, iota_f[:, 0:width].rearrange("p (o c) -> p o c", o=1).to_broadcast([P, n, width]),
                                                 per_edge(array, at, n, width), ALU.is_equal)

                    def key(i, n):
                        at = i * (SLOTS * HT) + (n + l * (ET // 2))
                        dve.tensor_scalar(hot_key[:, n % KB, :], iota_f[:, :], edge[:, A_KEY, bass.ds(at, 1)], edge[:, A_BASE, bass.ds(at, 1)],
                                          ALU.is_equal, ALU.mult).then_inc(s_key, 1)

                    def add_sums(u):
                        take(dve, s_agg)
                        dve.sem_inc(s_rows_free[u % RB], 1)
                        take(dve, v_agg)
                        part = feat[:, bass.ds(windows[u], WIN)]
                        dve.tensor_tensor(part, part, ps_sum[u % 2][0:F, 0:WIN], ALU.add).then_inc(v_agg, 1)

                    one_hot(hot_lo[:, 0, :, :], A_LO, l * (ET // 2), HT, P)
                    for n in range(AHEAD):
                        key(0, n)
                    with dve.Fori(0, LOOPS) as i:
                        for u in range(SLOTS):
                            row = i * SLOTS + u
                            _, (windows[u],) = nc.values_load_multi_w_load_instructions(firsts[0:1, bass.ds(2 * row, 1)], engines=[DVE], min_val=0, max_val=NODES - 1, skip_runtime_bounds_check_because="the windows were checked")
                            e = i * (SLOTS * 8) + (u * 8 + l * ROWS * 8)
                            _, offv = nc.values_load_multi_w_load_instructions(offs[0:1, bass.ds(e, HT)], engines=[DVE], min_val=0, max_val=STRIP - TWIN, skip_runtime_bounds_check_because="the windows were checked")
                            one_hot(hot_lo[:, (u + 1) % 2, :, :], A_LO, i * (SLOTS * HT) + ((u + 1) * HT + l * (ET // 2)), HT, P)
                            st = u // 4
                            if u % 4 == 0:
                                take(dve, s_zeroed[st])
                            for k in range(HT):
                                n = u * HT + k
                                take(dve, s_b)
                                take(dve, v)
                                part = strip[st][:, :, bass.ds(offv[k], TWIN)]
                                dve.tensor_tensor(part, part, ps_b[n % KB][:, 0:NT * TWIN].rearrange("p (h w) -> p h w", w=TWIN), ALU.add).then_inc(v, 1)
                                key(i, n + AHEAD)
                                if k == 2:
                                    one_hot(hot[:, u % 2, :, :], A_REL, row * JT, JT, WIN)
                                if k == 3 and u > 0:
                                    add_sums(u - 1)
                            if u % 4 == 3:
                                take(dve, v)
                                dve.sem_inc(s_full[st], 1)
                                dve.sem_inc(v, 1)
                            dve.wait_ge(s_got[u % RB], i * (SLOTS // RB * JT * 16) + (u // RB + 1) * JT * 16).then_inc(s_idx_free[u % RB], 1)
                            dve.tensor_tensor(rows[:, u % RB, :, :], rows[:, u % RB, :, :], per_edge(A_W, row * JT, JT, F), ALU.mult).then_inc(s_wm, 1)
                        add_sums(SLOTS - 1)
                    take(dve, v_agg)
                    take(dve, v)

            if l == 1:
                turn_back("l1", feat, F, ident[:, 0:F])

        def turn_back(name, cols, k, eye):
            with scope() as s9, nc.Block() as block:
                stage = [sb(f"tb_{name}{q}", [P, CH * P], F32, s9) for q in range(2)]
                ps = [psum(f"tbp_{name}{q}", [P, 512], s9) for q in range(2)]
                s_in, s_out, s_free, s_sp = (sem(f"tb_{name}_{n}") for n in ("in", "out", "free", "sp"))

                @block.gpsimd
                def _(pool):
                    pool.sem_inc(s_sp, 1)
                    if k < P:
                        for q in range(2):
                            pool.memset(stage[q][k:P, :], 0.0).then_inc(s_sp, 1)

                @block.sync
                def _(sp):
                    sp.wait_ge(s_sp, 1)

                @block.scalar
                def _(act):
                    def keep(i, q):
                        take(act, s_out)
                        act.activation(acc[:, bass.ds(i * CH, CH), :], ps[q][:, 0:CH * F].rearrange("p (c f) -> p c f", f=F), ACT.Copy).then_inc(s_free, 1)
                    chunks(act, nothing, keep)

                @block.vector
                def _(dve):
                    def copy(i, q):
                        take(dve, s_free)
                        dve.tensor_copy(stage[q][0:k, :], cols[0:k, bass.ds(i * (CH * P), CH * P)]).then_inc(s_in, 1)
                    dve.sem_inc(s_free, 2)
                    chunks(dve, nothing, copy)

                @block.tensor
                def _(pe):
                    def turn(i, q):
                        take(pe, s_in)
                        for c in range(CH):
                            last = pe.matmul(ps[q][:, c * F:(c + 1) * F], stage[q][:, c * P:(c + 1) * P], eye, start=True, stop=True)
                        last.then_inc(s_out, 1)
                    if k < P:
                        pe.wait_ge(s_sp, 3)
                    chunks(pe, nothing, turn)

        def turn_in():
            with scope() as s15, nc.Block() as block:
                ti = sb("ti", [P, F], F32, s15)
                ps = psum("ti_ps", [F, P], s15)
                s_in, s_out, s_free, s_sp = (sem(f"ti_{n}") for n in ("in", "out", "free", "sp"))

                @block.gpsimd
                def _(pool):
                    pool.sem_inc(s_sp, 1)

                @block.sync
                def _(sp):
                    sp.wait_ge(s_sp, 1)

                @block.scalar
                def _(act):
                    with act.Fori(0, NT) as i:
                        take(act, s_out)
                        act.activation(feat[:, bass.ds(i * P, P)], ps[:, :], ACT.Copy).then_inc(s_free, 1)

                @block.vector
                def _(dve):
                    dve.sem_inc(s_free, 1)
                    with dve.Fori(0, NT) as i:
                        take(dve, s_free)
                        dve.tensor_copy(ti[:, :], acc[:, bass.ds(i, 1), :].rearrange("p o f -> p (o f)")).then_inc(s_in, 1)
                    take(dve, s_free)

                @block.tensor
                def _(pe):
                    with pe.Fori(0, NT) as i:
                        take(pe, s_in)
                        pe.transpose(ps[:, :], ti[:, :], ident[:, :]).then_inc(s_out, 1)

        def flag(n):
            return nc.values_load(flags[0:1, n:n + 1], min_val=0, max_val=1 << 20)

        def aggregate(l):
            with nc.If(flag(0) == 0):
                fast_path(l)
            with nc.Else():
                general_path(l)
                if l == 0:
                    turn_in()

        def bc_n(ap):
            return ap.rearrange("p (i o) -> p i o", o=1).to_broadcast([P, NT, F])

        def bc_f(ap):
            return ap.rearrange("p (o f) -> p o f", o=1).to_broadcast([P, NT, F])

        def layer_norm(dve, link, s_var, s_std, out_ap, src, tmp):
            link(dve.tensor_reduce(mom[:, 0, :], src[:, :, :], AX.X, ALU.add))
            link(dve.tensor_scalar(mom[:, 0, :], mom[:, 0, :], 1.0 / F, None, ALU.mult))
            link(dve.tensor_tensor(src[:, :, :], src[:, :, :], bc_n(mom[:, 0, :]), ALU.subtract))
            link(dve.tensor_tensor(tmp[:, :, :], src[:, :, :], src[:, :, :], ALU.mult))
            link(dve.tensor_reduce(mom[:, 1, :], tmp[:, :, :], AX.X, ALU.add))
            dve.tensor_scalar(mom[:, 1, :], mom[:, 1, :], 1.0 / F, EPS_LN, ALU.mult, ALU.add).then_inc(s_var, 1)
            dve.wait_ge(s_std, 1)
            link(dve.reciprocal(mom[:, 3, :], mom[:, 2, :]))
            return dve.tensor_tensor(out_ap, src[:, :, :], bc_n(mom[:, 3, :]), ALU.mult)

        table_phase(0)
        aggregate(0)

        table_phase(1)
        aggregate(1)

        with ExitStack() as s4:
          unit_t = sb("unit_t", [P, NGPAD], F32, s4)
          wh_g = sb("wh_g", [P, GROUPS, F], F32, s4)
          s_whg = [sem(f"whg{k}", True) for k in range(2)]
          with scope() as s11, nc.Block() as block:
            v, s_var, s_std = sem("v_n1"), sem("s_var1"), sem("s_std1")
            s_stage, s_turned, s_xt, s_wh, s_skip, s_sq, s_nrm, s_tab, s_pad = (sem(f"n_{k}") for k in ("stage", "turned", "xt", "wh", "skip", "sq", "nrm", "tab", "pad"))
            s_rows = sem("n_rows")
            s_min, s_minT, s_u, s_ut, s_u_free = (sem(f"n_{k}") for k in ("min", "minT", "u", "ut", "u_free"))
            stage = [sb(f"nstage{q}", [P, CH * F], F32, s11) for q in range(2)]
            stage_u = [sb(f"ustage{q}", [P, CH, 2, F], F32, s11) for q in range(2)]
            xt = [sb(f"nxt{q}", [P, CH * P], F32, s11) for q in range(2)]
            tmp = sb("tmp2", [P, NT, F], F32, s11)
            nrm = sb("nrm", [P, NT], F32, s11)
            low = sb("low", [P, 2], F32, s11)
            ps_t = psum("ps_t2", [P, 2, 512], s11)
            ps_h = [psum(f"ps_h2{q}", [P, 512], s11) for q in range(2)]
            ps_u = [psum(f"ps_u{q}", [P, 2, 512], s11) for q in range(2)]
            norm = mom[:, 3, :]

            def load_wh(eng, kind, k):
                with eng.Fori(0, GROUPS // 2) as g:
                    at = nc.values_load(firsts[0:1, bass.ds(8 * g + (4 * k + 1), 1)], engines=[kind], min_val=0, max_val=NODES - 1, skip_runtime_bounds_check_because="dst is below the number of nodes")
                    eng.dma_start(wh_g[:, bass.ds(2 * g + k, 1), :], wh_rows.ap()[bass.ds(at, STRIP), :].rearrange("p (o f) -> p o f", o=1)).then_inc(s_whg[k], 16)

            @block.gpsimd
            def _(pool):
                for q in range(2):
                    pool.memset(xt[q][F:P, :], 0.0).then_inc(s_pad, 1)
                pool.wait_ge(s_pad, 2)
                pool.memset(nrm[:, :], 1.0).then_inc(s_pad, 1)
                pool.memset(unit_t[:, NPAD:NGPAD], 0.0).then_inc(s_pad, 1)
                take(pool, s_rows)
                load_wh(pool, POOL, 0)

            @block.sync
            def _(sp):
                sp.wait_ge(s_skip, 1)
                sp.dma_start(wh_rows.ap()[0:NPAD, :].rearrange("(i p) f -> p i f", p=P), skip[:, :, :]).then_inc(s_tab, 16)
                sp.dma_start(wh_rows.ap()[NPAD:NGPAD, :].rearrange("(i p) f -> p i f", p=P), skip[:, 0:1, :]).then_inc(s_tab, 16)
                sp.wait_ge(s_tab, 32)
                sp.sem_inc(s_rows, 1)
                load_wh(sp, SP, 1)

            @block.scalar
            def _(act):
                def turned(i, q):
                    take(act, s_turned)
                    for k, m in ((0, 4), (1, CH - 4)):
                        last = act.activation(xt[q][0:F, k * 4 * P:(k * 4 + m) * P], ps_t[0:F, k, 0:m * P], ACT.Copy)
                    last.then_inc(s_xt, 1)

                def unit(i, q):
                    take(act, s_ut)
                    for k, m in ((0, 4), (1, CH - 4)):
                        last = act.activation(unit_t[:, bass.ds(i * (CH * P) + k * 4 * P, m * P)], ps_u[q][:, k, 0:m * P], ACT.Copy)
                    last.then_inc(s_u_free, 1)

                act.wait_ge(s_var, 1)
                act.activation(mom[:, 2, :], mom[:, 1, :], ACT.Sqrt).then_inc(s_std, 1)
                chunks(act, turned, nothing)
                act.wait_ge(s_sq, 1)
                act.activation(norm, mom[:, 0, :], ACT.Sqrt).then_inc(s_nrm, 1)
                chunks(act, nothing, unit)

            @block.tensor
            def _(pe):
                def turn(i, q):
                    take(pe, s_stage)
                    for c in range(CH):
                        last = pe.matmul(ps_t[0:F, c // 4, c % 4 * P:(c % 4 + 1) * P], stage[q][:, c * F:(c + 1) * F], ident[:, :], start=True, stop=True)
                    last.then_inc(s_turned, 1)
                    take(pe, s_xt)

                def products(i, q):
                    for c in range(CH):
                        last = pe.matmul(ps_h[q][:, c * F:(c + 1) * F], xt[q][:, c * P:(c + 1) * P], w2[:, :], start=True, stop=True)
                    last.then_inc(s_wh, 1)

                def unit(i, q):
                    take(pe, s_u)
                    for c in range(CH):
                        last = pe.matmul(ps_u[q][:, c // 4, c % 4 * P:(c % 4 + 1) * P], stage_u[q][:, c, :, :].rearrange("p a f -> p (a f)"), ident[:, :], start=True, stop=True)
                    last.then_inc(s_ut, 1)

                pe.wait_ge(s_pad, 2)
                chunks(pe, turn, products)
                pe.wait_ge(s_min, 1)
                pe.matmul(ps_h[0][0:1, 0:1], low[:, 1:2], ones[:, :], start=True, stop=True).then_inc(s_minT, 1)
                chunks(pe, nothing, unit)

            @block.vector
            def _(dve):
                def link(ins):
                    ins.then_inc(v, 1)
                    take(dve, v)

                def copy(i, q):
                    dve.tensor_copy(stage[q][:, :].rearrange("p (c f) -> p c f", f=F), x_sb[:, bass.ds(i * CH, CH), :]).then_inc(s_stage, 1)

                def bias(i, q):
                    take(dve, s_wh)
                    dve.tensor_tensor(skip[:, bass.ds(i * CH, CH), :], ps_h[q][:, 0:CH * F].rearrange("p (c f) -> p c f", f=F),
                                      b2[:, :].rearrange("p (o f) -> p o f", o=1).to_broadcast([P, CH, F]), ALU.add).then_inc(v, 1)

                def unit(i, q):
                    take(dve, s_u_free)
                    dve.tensor_tensor(stage_u[q][:, :, :, :], skip[:, bass.ds(i * CH, CH), :].rearrange("p c (o f) -> p c o f", o=1).to_broadcast([P, CH, 2, F]),
                                      mom[:, 2, bass.ds(i * CH, CH)].rearrange("p (c a b) -> p c a b", a=1, b=1).to_broadcast([P, CH, 2, F]), ALU.mult).then_inc(s_u, 1)

                link(dve.tensor_tensor(acc[:, :, :], acc[:, :, :], skip[:, :, :], ALU.add))
                link(dve.tensor_tensor(acc[:, :, :], acc[:, :, :], x_sb[:, :, :], ALU.add))
                link(layer_norm(dve, link, s_var, s_std, x_sb[:, :, :], acc, tmp))
                chunks(dve, copy, bias)
                take(dve, v, NCH)
                dve.sem_inc(s_skip, 1)
                link(dve.tensor_tensor(tmp[:, :, :], skip[:, :, :], skip[:, :, :], ALU.mult))
                dve.tensor_reduce(mom[:, 0, :], tmp[:, :, :], AX.X, ALU.add).then_inc(s_sq, 1)
                dve.wait_ge(s_nrm, 1)
                link(dve.tensor_scalar(mom[:, 1, :], norm, TINY, None, ALU.max))
                link(dve.reciprocal(mom[:, 2, :], mom[:, 1, :]))
                dve.sem_inc(s_u_free, 2)
                dve.wait_ge(s_pad, 4)
                dve.tensor_copy(nrm[:, 0:NT - 1], norm[:, 0:NT - 1])
                link(dve.tensor_copy(nrm[0:LAST, NT - 1:NT], norm[0:LAST, NT - 1:NT]))
                link(dve.tensor_reduce(low[:, 0:1], nrm[:, :], AX.X, ALU.min))
                dve.tensor_scalar(low[:, 1:2], low[:, 0:1], 2.0 * EPS_SIM ** 0.5, None, ALU.is_lt).then_inc(s_min, 1)
                dve.wait_ge(s_minT, 1)
                link(dve.scalar_tensor_tensor(flags[0:1, 1:2], ps_h[0][0:1, 0:1], 1.0, flags[0:1, 0:1], ALU.mult, ALU.add))
                chunks(dve, nothing, unit)
                take(dve, s_u_free, 2)

          def finish(eng, s):
            eng.tensor_scalar(skip[:, :, :], skip[:, :, :], coeff[:, 7:8], None, ALU.mult).then_inc(s, 1)
            eng.wait_ge(s, 1)
            eng.tensor_tensor(x_sb[:, :, :], x_sb[:, :, :], skip[:, :, :], ALU.add).then_inc(s, 1)
            eng.wait_ge(s, 2)

          def dense_path():
            with ExitStack() as s12:
                out_t = sums_t
                unit_g = sb("unit_g", [P, PAIRS, STRIP], F32, s12)
                unit_s = sb("unit_s", [P, 2, SB], F32, s12)
                NBUF = 7
                adj_b = edge.ap().rearrange("p a e -> p (a e)")[:, 0:NBUF * 2 * SB].rearrange("p (k g n) -> p k g n", k=NBUF, g=2)
                LAG = 3
                CB = LAG + 1
                pos = sb("pos", [P, 2, 2, SB], F32, s12)
                con = sb("con", [P, CB, 2, SB], F32, s12)
                with scope() as s13, nc.Block() as block:
                    ps_c = [psum(f"ps_c{k}", [P, 2, 512], s13) for k in range(2)]
                    ps_o = psum("ps_o", [P, 512], s13)
                    s_ug, s_us, s_us_free, s_c, s_pos, s_blend, s_con, s_o, s_o_free = (
                        sem(f"d_{n}") for n in ("ug", "us", "us_free", "c", "pos", "blend", "con", "o", "o_free"))
                    s_us0, s_sum = sem("d_us0"), sem("d_sum")
                    s_adj = [sem(f"d_adj{k}") for k in range(NBUF)]
                    s_adj_free = [sem(f"d_adj_free{k}") for k in range(NBUF)]

                    @block.sync
                    def _(sp):
                        for k in range(NBUF):
                            sp.sem_inc(s_adj_free[k], 1)
                        half = GROUPS // 2
                        with sp.Fori(0, NSB) as b:
                            for p in range(PAIRS):
                                g = 2 * p
                                take(sp, s_adj_free[p % NBUF])
                                sp.dma_start(adj_b[:, p % NBUF, :, :], adj.ap()[g // half, g % half + 1:g % half + 3, :, bass.ds(b * SB, SB)].rearrange("g w n -> w g n")).then_inc(s_adj[p % NBUF], 16)

                    @block.gpsimd
                    def _(pool):
                        with pool.Fori(0, PAIRS) as p:
                            for h in range(2):
                                at = nc.values_load(firsts[0:1, bass.ds(8 * p + (4 * h + 1), 1)], engines=[POOL], min_val=0, max_val=NODES - 1, skip_runtime_bounds_check_because="dst is below the number of nodes")
                                pool.tensor_copy(unit_g[h * F:(h + 1) * F, bass.ds(p, 1), :].rearrange("p o w -> p (o w)"), unit_t[h * F:(h + 1) * F, bass.ds(at, STRIP)]).then_inc(s_ug, 1)
                        pool.wait_ge(s_ug, GROUPS)
                        finish(pool, s_sum)
                        with pool.Fori(1, NSB) as b:
                            take(pool, s_us_free)
                            for h in range(2):
                                pool.tensor_copy(unit_s[h * F:(h + 1) * F, h, :], unit_t[h * F:(h + 1) * F, bass.ds(b * SB, SB)]).then_inc(s_us, 1)

                    @block.tensor
                    def _(pe):
                        def cosines(b, p, first):
                            if p == 0:
                                take(pe, s_us, 2)
                            if first:
                                pe.wait_ge(s_ug, 2 * (p + 1))
                            if not first or p >= 2:
                                pe.wait_ge(s_blend, b * PAIRS + (p - 1))
                            for h in range(2):
                                last = pe.matmul(ps_c[p % 2][:, h, 0:SB], unit_g[:, p, :], unit_s[:, h, :], start=True, stop=True)
                            last.then_inc(s_c, 1)

                        def product(p):
                            if p == 0:
                                take(pe, s_o_free)
                            take(pe, s_con)
                            for h in range(2):
                                last = pe.matmul(ps_o[h * F:(h + 1) * F, 0:SB], wh_g[:, 2 * p + h, :], con[:, p % CB, h, :],
                                                 start=(p == 0), stop=(p == PAIRS - 1), skip_group_check=True)
                            last.then_inc(s_adj_free[p % NBUF] if p < PAIRS - 1 else s_o, 1)

                        def block_of_sources(b, first=False):
                            for p in range(PAIRS):
                                cosines(b, p, first)
                                if p >= LAG:
                                    if first and p == LAG:
                                        for k in range(2):
                                            pe.wait_ge(s_whg[k], 16 * (GROUPS // 2))
                                    product(p - LAG)
                                elif not first:
                                    product(PAIRS + p - LAG)

                        pe.sem_inc(s_o_free, 1)
                        block_of_sources(0, True)
                        with pe.Fori(1, NSB) as b:
                            block_of_sources(b)
                        for p in range(PAIRS - LAG, PAIRS):
                            product(p)

                    @block.scalar
                    def _(act):
                        def keep(b):
                            take(act, s_o)
                            act.sem_inc(s_adj_free[(PAIRS - 1) % NBUF], 1)
                            act.activation(out_t[:, bass.ds(b * SB, SB)], ps_o[:, 0:SB], ACT.Copy).then_inc(s_o_free, 1)

                        def positive(b, first=False):
                            for p in range(PAIRS):
                                take(act, s_c)
                                act.activation(pos[:, p % 2, :, :], ps_c[p % 2][:, :, 0:SB], ACT.Relu, scale=coeff[:, 4:5]).then_inc(s_pos, 1)
                                if p == LAG - 1 and not first:
                                    keep(b - 1)
                            act.sem_inc(s_us_free, 1)

                        for h in range(2):
                            act.wait_ge(s_us0, 1)
                            act.activation(unit_s[h * F:(h + 1) * F, h, :], unit_t[h * F:(h + 1) * F, 0:SB], ACT.Copy).then_inc(s_us, 1)
                        positive(0, True)
                        with act.Fori(1, NSB) as b:
                            positive(b)
                        keep(NSB - 1)
                        take(act, s_o_free)

                    @block.vector
                    def _(dve):
                        def blend(p):
                            take(dve, s_pos)
                            dve.scalar_tensor_tensor(con[:, p % CB, :, :], ps_c[p % 2][:, :, 0:SB], coeff[:, 5:6], pos[:, p % 2, :, :], ALU.mult, ALU.add).then_inc(s_blend, 1)

                        def weigh(p, b):
                            dve.wait_ge(s_blend, b * PAIRS + (p + 1))
                            dve.wait_ge(s_adj[p % NBUF], b * (16 * PAIRS // NBUF) + (p // NBUF + 1) * 16)
                            dve.tensor_tensor(con[:, p % CB, :, :], con[:, p % CB, :, :], adj_b[:, p % NBUF, :, :], ALU.mult).then_inc(s_con, 1)

                        dve.memset(unit_s[:, :, :], 0.0).then_inc(s_us0, 1)
                        with dve.Fori(0, NSB) as b:
                            blend(0)
                            for p in range(PAIRS):
                                if p < PAIRS - 1:
                                    blend(p + 1)
                                weigh(p, b)

                turn_back("dense", out_t, P, eye2[:, :])

          with nc.If(flag(1) == 0):
            dense_path()
          with nc.Else():
            with scope() as s16, nc.Block() as block:
                wide = sb("wide", [P, NT, F + 1], F32, s16)
                s_wide, s_w, s_o = sem("s_wide"), sem("s_w"), sem("s_o16")

                @block.vector
                def _(dve):
                    dve.tensor_copy(wide[:, :, 0:F], skip[:, :, :]).then_inc(s_wide, 1)
                    dve.tensor_copy(wide[:, :, F], mom[:, 3, :]).then_inc(s_wide, 1)

                @block.sync
                def _(sp):
                    for k in range(2):
                        sp.wait_ge(s_whg[k], 16 * (GROUPS // 2))
                    sp.wait_ge(s_wide, 2)
                    sp.dma_start(tab_g.ap().rearrange("(i p) f -> p i f", p=P), wide[:, :, :]).then_inc(s_w, 16)
                    sp.wait_ge(s_w, 16)

                for other in (block.scalar, block.tensor, block.gpsimd):
                    other(lambda eng: eng.sem_inc(s_o, 1))

            general_path(2)
            with scope() as _, nc.Block() as block:
                s_sg, s_o = sem("s_sg"), sem("s_other")

                @block.vector
                def _(dve):
                    dve.tensor_scalar(acc[:, :, :], acc[:, :, :], coeff[:, 6:7], None, ALU.mult)
                    finish(dve, s_sg)

                for other in (block.scalar, block.tensor, block.gpsimd, block.sync):
                    other(lambda eng: eng.sem_inc(s_o, 1))

        with scope() as s14, nc.Block() as block:
            nbuf = [sb(f"fin{k}", [P, NT, F], F32, s14) for k in range(2)]
            v, s_var, s_std = sem("v_n2"), sem("s_var2"), sem("s_std2")
            s_fin, s_out = sem("s_fin"), sem("s_out")

            @block.sync
            def _(sp):
                sp.wait_ge(s_fin, 1)
                sp.dma_start(out[0:(NT - 1) * P, :].rearrange("(i p) f -> p i f", p=P), nbuf[1][:, 0:NT - 1, :]).then_inc(s_out, 16)
                sp.dma_start(out[(NT - 1) * P:NODES, :], nbuf[1][0:LAST, NT - 1, :]).then_inc(s_out, 16)
                sp.wait_ge(s_out, 32)

            @block.scalar
            def _(act):
                act.wait_ge(s_var, 1)
                act.activation(mom[:, 2, :], mom[:, 1, :], ACT.Sqrt).then_inc(s_std, 1)

            @block.vector
            def _(dve):
                def link(ins):
                    ins.then_inc(v, 1)
                    take(dve, v)
                link(dve.tensor_tensor(coeff[:, 6:7], coeff[:, 6:7], coeff[:, 3:4], ALU.mult))
                link(dve.scalar_tensor_tensor(acc[:, :, :], acc[:, :, :], coeff[:, 6:7], x_sb[:, :, :], ALU.mult, ALU.add))
                layer_norm(dve, link, s_var, s_std, nbuf[1][:, :, :], acc, nbuf[0]).then_inc(s_fin, 1)


_INS = ["x", "src", "dst", "edge_type_5", "edge_weight", "edge_weight_n2", "L0_gnn_W0", "L0_gnn_Al0", "L0_gnn_Ar0",
        "L0_gnn_W1", "L0_gnn_Al1", "L0_gnn_Ar1", "L0_gnn_Wres", "L0_gnn_bres", "L1_gnn_W", "L1_gnn_b",
        "L1_gnn_deg_coeff", "L1_gnn_coeff_param", "L1_gnn_scale_param"]


def kernel(**inputs):
    import numpy as _np
    import concourse.bacc as _bacc
    from concourse import mybir as _mybir
    from concourse.bass_utils import run_bass_kernel_spmd as _run

    nc = _bacc.Bacc("TRN2", target_bir_lowering=False, num_devices=1)
    arrays, args = {}, {}
    for name in _INS:
        a = _np.ascontiguousarray(inputs[name])
        arrays[f"in_{name}"] = a
        args[name] = nc.dram_tensor(f"in_{name}", a.shape, _mybir.dt.from_np(a.dtype), kind="ExternalInput").ap()
    out = nc.dram_tensor("out", (NODES, F), F32, kind="ExternalOutput").ap()
    build(nc, args, out)
    r = _run(nc, [arrays], core_ids=[0])
    return r.results[0]["out"]
```
